# Optimizing a Trainium2 kernel written in Bass

```python
import numpy as np
import jax
import jax.numpy as jnp

def _softmax(x, axis=-1):
    return jax.nn.softmax(x, axis=axis)

def _gelu(x):
    return jax.nn.gelu(x, approximate=True)

def _silu(x):
    return jax.nn.silu(x)

def _sigmoid(x):
    return jax.nn.sigmoid(x)

def _layernorm(x, axis=-1, eps=1e-05):
    m = jnp.mean(x, axis=axis, keepdims=True)
    v = jnp.var(x, axis=axis, keepdims=True)
    return (x - m) / jnp.sqrt(v + eps)

def _scatter_add(tgt, idx, src, axis=0):
    return tgt.at[idx].add(src)

def _segment_sum(src, seg, n):
    return jax.ops.segment_sum(src, seg, n)
kernel_name = 'mk_vit_tower_d1_tok_img768_r4_008580'

def setup_inputs(seed: int=0):
    np.random.seed(seed)
    _w = jnp.asarray

    def _rec_inputs():
        import jax
        import jax.numpy as jnp
        _rk = jax.random.key(seed)
        x = 7.57192e-06 + 1.00007 * jax.random.normal(jax.random.fold_in(_rk, 1), (64, 224, 224, 3), jnp.float32)
        return x
    x = _rec_inputs()

    def _L0_tok_setup():
        import jax, jax.numpy as jnp
        import numpy as np
        IMG = 224
        P = 16
        HP = P // 2
        D = 192
        C_IN = 3
        B = 64

        def _crop_shift_pad(images, oh, ow):
            th = IMG - HP
            tw = IMG - HP
            out = jnp.zeros_like(images)
            return out.at[:, oh:oh + th, ow:ow + tw, :].set(images[:, oh:oh + th, ow:ow + tw, :])
        key = jax.random.key(seed)
        k1, k2 = jax.random.split(key, 2)
        images = jax.random.normal(k1, (B, IMG, IMG, C_IN), dtype=jnp.float32)
        pvs = P * P * C_IN * 5
        W = jax.random.normal(k2, (pvs, D), dtype=jnp.float32) * 0.02
        b = jnp.zeros((D,), dtype=jnp.float32)
        return {'images': images, 'W': W, 'b': b}
    _L0_tok_all = _L0_tok_setup()
    _L0_tok_in = {k: v for k, v in _L0_tok_all.items() if k in ('W', 'b')}
    del _L0_tok_all

    def _L0_attn_setup():
        import jax, jax.numpy as jnp
        import numpy as np
        B, N, DIM = (16, 577, 192)
        HEADS, HEAD_DIM = (12, 64)
        QKV_DIM = HEADS * HEAD_DIM
        MAX_REL = 14
        TABLE_ROWS = 2 * MAX_REL + 2

        def _rel_indices(n, max_rel):
            m = n - 1
            side = int(m ** 0.5)
            r = np.arange(m)
            dv = r[None, :] // side - r[:, None] // side
            dh = r[None, :] % side - r[:, None] % side
            iv = np.clip(dv, -max_rel, max_rel) + max_rel + 1
            ih = np.clip(dh, -max_rel, max_rel) + max_rel + 1
            iv = np.pad(iv, ((1, 0), (1, 0)))
            ih = np.pad(ih, ((1, 0), (1, 0)))
            return (jnp.asarray(iv), jnp.asarray(ih))
        key = jax.random.key(seed)
        ks = jax.random.split(key, 8)
        return {'x': jax.random.normal(ks[0], (B, N, DIM), jnp.float32), 'qkv_w': jax.random.normal(ks[1], (3 * QKV_DIM, DIM), jnp.float32) * 0.02, 'proj_w': jax.random.normal(ks[2], (DIM, QKV_DIM), jnp.float32) * 0.02, 'proj_b': jnp.zeros((DIM,), jnp.float32), 'tab_kv': jax.random.normal(ks[3], (TABLE_ROWS, HEAD_DIM), jnp.float32) * 0.02, 'tab_kh': jax.random.normal(ks[4], (TABLE_ROWS, HEAD_DIM), jnp.float32) * 0.02, 'tab_vv': jax.random.normal(ks[5], (TABLE_ROWS, HEAD_DIM), jnp.float32) * 0.02, 'tab_vh': jax.random.normal(ks[6], (TABLE_ROWS, HEAD_DIM), jnp.float32) * 0.02}
    _L0_attn_all = _L0_attn_setup()
    _L0_attn_in = {k: v for k, v in _L0_attn_all.items() if k in ('qkv_w', 'proj_w', 'proj_b', 'tab_kv', 'tab_kh', 'tab_vv', 'tab_vh')}
    del _L0_attn_all

    def _L0_ffn_setup():
        import jax, jax.numpy as jnp
        import numpy as np
        B, L, D, H, F = (4, 512, 192, 12, 768)
        ROUTE_FRAC = 0.15
        LN_EPS = 1e-05

        def _ln(x, g, b):
            m = jnp.mean(x, axis=-1, keepdims=True)
            v = jnp.mean((x - m) ** 2, axis=-1, keepdims=True)
            return (x - m) * jax.lax.rsqrt(v + LN_EPS) * g + b
        key = jax.random.key(seed)
        ks = jax.random.split(key, 20)
        s = 0.02
        return {'hidden_states': jax.random.normal(ks[0], (B, L, D), dtype=jnp.float32), 'g1': jnp.ones((D,), jnp.float32), 'b1': jnp.zeros((D,), jnp.float32), 'g2': jnp.ones((D,), jnp.float32), 'b2': jnp.zeros((D,), jnp.float32), 'Wr': jax.random.normal(ks[1], (D,), jnp.float32) * s, 'br': jnp.zeros((), jnp.float32), 'Wq': jax.random.normal(ks[2], (D, D), jnp.float32) * s, 'bq': jnp.zeros((D,), jnp.float32), 'Wk': jax.random.normal(ks[3], (D, D), jnp.float32) * s, 'bk': jnp.zeros((D,), jnp.float32), 'Wv': jax.random.normal(ks[4], (D, D), jnp.float32) * s, 'bv': jnp.zeros((D,), jnp.float32), 'Wo': jax.random.normal(ks[5], (D, D), jnp.float32) * s, 'bo': jnp.zeros((D,), jnp.float32), 'Wm': jax.random.normal(ks[6], (D, D), jnp.float32) * s, 'bm': jnp.zeros((D,), jnp.float32), 'W1': jax.random.normal(ks[7], (D, F), jnp.float32) * s, 'bf1': jnp.zeros((F,), jnp.float32), 'W2': jax.random.normal(ks[8], (F, D), jnp.float32) * s, 'bf2': jnp.zeros((D,), jnp.float32)}
    _L0_ffn_all = _L0_ffn_setup()
    _L0_ffn_in = {k: v for k, v in _L0_ffn_all.items() if k in ('g1', 'b1', 'g2', 'b2', 'Wr', 'br', 'Wq', 'bq', 'Wk', 'bk', 'Wv', 'bv', 'Wo', 'bo', 'Wm', 'bm', 'W1', 'bf1', 'W2', 'bf2')}
    del _L0_ffn_all
    return {'x': x, 'L0_tok_W': _L0_tok_in['W'], 'L0_tok_b': _L0_tok_in['b'], 'L0_attn_qkv_w': _L0_attn_in['qkv_w'], 'L0_attn_proj_w': _L0_attn_in['proj_w'], 'L0_attn_proj_b': _L0_attn_in['proj_b'], 'L0_attn_tab_kv': _L0_attn_in['tab_kv'], 'L0_attn_tab_kh': _L0_attn_in['tab_kh'], 'L0_attn_tab_vv': _L0_attn_in['tab_vv'], 'L0_attn_tab_vh': _L0_attn_in['tab_vh'], 'L0_ffn_g1': _L0_ffn_in['g1'], 'L0_ffn_b1': _L0_ffn_in['b1'], 'L0_ffn_g2': _L0_ffn_in['g2'], 'L0_ffn_b2': _L0_ffn_in['b2'], 'L0_ffn_Wr': _L0_ffn_in['Wr'], 'L0_ffn_br': _L0_ffn_in['br'], 'L0_ffn_Wq': _L0_ffn_in['Wq'], 'L0_ffn_bq': _L0_ffn_in['bq'], 'L0_ffn_Wk': _L0_ffn_in['Wk'], 'L0_ffn_bk': _L0_ffn_in['bk'], 'L0_ffn_Wv': _L0_ffn_in['Wv'], 'L0_ffn_bv': _L0_ffn_in['bv'], 'L0_ffn_Wo': _L0_ffn_in['Wo'], 'L0_ffn_bo': _L0_ffn_in['bo'], 'L0_ffn_Wm': _L0_ffn_in['Wm'], 'L0_ffn_bm': _L0_ffn_in['bm'], 'L0_ffn_W1': _L0_ffn_in['W1'], 'L0_ffn_bf1': _L0_ffn_in['bf1'], 'L0_ffn_W2': _L0_ffn_in['W2'], 'L0_ffn_bf2': _L0_ffn_in['bf2']}

def reference(x, L0_tok_W, L0_tok_b, L0_attn_qkv_w, L0_attn_proj_w, L0_attn_proj_b, L0_attn_tab_kv, L0_attn_tab_kh, L0_attn_tab_vv, L0_attn_tab_vh, L0_ffn_g1, L0_ffn_b1, L0_ffn_g2, L0_ffn_b2, L0_ffn_Wr, L0_ffn_br, L0_ffn_Wq, L0_ffn_bq, L0_ffn_Wk, L0_ffn_bk, L0_ffn_Wv, L0_ffn_bv, L0_ffn_Wo, L0_ffn_bo, L0_ffn_Wm, L0_ffn_bm, L0_ffn_W1, L0_ffn_bf1, L0_ffn_W2, L0_ffn_bf2):
    import jax
    import jax.numpy as jnp

    def _L0_tok_ref(images, W, b):
        import jax, jax.numpy as jnp
        import numpy as np
        IMG = 224
        P = 16
        HP = P // 2
        D = 192
        C_IN = 3
        B = 64

        def _crop_shift_pad(images, oh, ow):
            th = IMG - HP
            tw = IMG - HP
            out = jnp.zeros_like(images)
            return out.at[:, oh:oh + th, ow:ow + tw, :].set(images[:, oh:oh + th, ow:ow + tw, :])
        offsets = [(0, 0), (HP, 0), (0, HP), (HP, HP)]
        concat = jnp.concatenate([images] + [_crop_shift_pad(images, oh, ow) for oh, ow in offsets], axis=-1)
        Bn, _, _, C = concat.shape
        g = IMG // P
        x = concat.reshape(Bn, g, P, g, P, C)
        x = x.transpose(0, 1, 3, 2, 4, 5).reshape(Bn, g * g, P * P * C)
        return x @ W + b

    def _L0_attn_ref(x, qkv_w, proj_w, proj_b, tab_kv, tab_kh, tab_vv, tab_vh):
        import jax, jax.numpy as jnp
        import numpy as np
        B, N, DIM = (16, 577, 192)
        HEADS, HEAD_DIM = (12, 64)
        QKV_DIM = HEADS * HEAD_DIM
        MAX_REL = 14
        TABLE_ROWS = 2 * MAX_REL + 2

        def _rel_indices(n, max_rel):
            m = n - 1
            side = int(m ** 0.5)
            r = np.arange(m)
            dv = r[None, :] // side - r[:, None] // side
            dh = r[None, :] % side - r[:, None] % side
            iv = np.clip(dv, -max_rel, max_rel) + max_rel + 1
            ih = np.clip(dh, -max_rel, max_rel) + max_rel + 1
            iv = np.pad(iv, ((1, 0), (1, 0)))
            ih = np.pad(ih, ((1, 0), (1, 0)))
            return (jnp.asarray(iv), jnp.asarray(ih))
        b, n, _ = x.shape
        scale = HEAD_DIM ** (-0.5)
        qkv = (x @ qkv_w.T).reshape(b, n, 3, HEADS, HEAD_DIM).transpose(2, 0, 3, 1, 4)
        q, k, v = (qkv[0], qkv[1], qkv[2])
        attn = jnp.einsum('bhqd,bhkd->bhqk', q, k) * scale
        iv, ih = _rel_indices(n, MAX_REL)
        r_p_k = tab_kv[iv] + tab_kh[ih]
        attn = attn + jnp.einsum('bhqd,qkd->bhqk', q, r_p_k) * scale
        attn = jax.nn.softmax(attn, axis=-1)
        out = jnp.einsum('bhqk,bhkd->bhqd', attn, v)
        r_p_v = tab_vv[iv] + tab_vh[ih]
        out = out + jnp.einsum('bhqk,qkd->bhqd', attn, r_p_v)
        out = out.transpose(0, 2, 1, 3).reshape(b, n, QKV_DIM)
        return out @ proj_w.T + proj_b

    def _L0_ffn_ref(hidden_states, g1, b1, g2, b2, Wr, br, Wq, bq, Wk, bk, Wv, bv, Wo, bo, Wm, bm, W1, bf1, W2, bf2):
        import jax, jax.numpy as jnp
        import numpy as np
        B, L, D, H, F = (4, 512, 192, 12, 768)
        ROUTE_FRAC = 0.15
        LN_EPS = 1e-05

        def _ln(x, g, b):
            m = jnp.mean(x, axis=-1, keepdims=True)
            v = jnp.mean((x - m) ** 2, axis=-1, keepdims=True)
            return (x - m) * jax.lax.rsqrt(v + LN_EPS) * g + b
        b, l, d = hidden_states.shape
        dh = d // H
        normed = _ln(hidden_states, g1, b1)
        scores = jax.nn.sigmoid(jnp.einsum('bld,d->bl', normed, Wr) + br)
        k = max(1, int(round(ROUTE_FRAC * l)))
        _, idx = jax.lax.top_k(-scores, k)
        attn_mask = jnp.zeros((b, l), bool).at[jnp.arange(b)[:, None], idx].set(True)
        q = (normed @ Wq + bq).reshape(b, l, H, dh)
        kk = (normed @ Wk + bk).reshape(b, l, H, dh)
        v = (normed @ Wv + bv).reshape(b, l, H, dh)
        logits = jnp.einsum('blhd,bmhd->bhlm', q, kk) / jnp.sqrt(jnp.float32(dh))
        probs = jax.nn.softmax(logits, axis=-1)
        ctx = jnp.einsum('bhlm,bmhd->blhd', probs, v).reshape(b, l, d)
        attn_out = ctx @ Wo + bo
        w = scores / (jnp.sum(scores, axis=1, keepdims=True) + 1e-06)
        pooled = jnp.einsum('bl,bld->bd', w, normed)
        mix_out = (normed + scores[..., None] * pooled[:, None, :]) @ Wm + bm
        merged = jnp.where(attn_mask[..., None], attn_out, mix_out)
        h = hidden_states + merged
        n2 = _ln(h, g2, b2)
        ffn = jax.nn.gelu(n2 @ W1 + bf1, approximate=False) @ W2 + bf2
        return h + ffn
    h = _L0_tok_ref(x, L0_tok_W, L0_tok_b)
    h = h + _L0_attn_ref(_layernorm(h, axis=-1), L0_attn_qkv_w, L0_attn_proj_w, L0_attn_proj_b, L0_attn_tab_kv, L0_attn_tab_kh, L0_attn_tab_vv, L0_attn_tab_vh)
    h = h + _L0_ffn_ref(_layernorm(h, axis=-1), L0_ffn_g1, L0_ffn_b1, L0_ffn_g2, L0_ffn_b2, L0_ffn_Wr, L0_ffn_br, L0_ffn_Wq, L0_ffn_bq, L0_ffn_Wk, L0_ffn_bk, L0_ffn_Wv, L0_ffn_bv, L0_ffn_Wo, L0_ffn_bo, L0_ffn_Wm, L0_ffn_bm, L0_ffn_W1, L0_ffn_bf1, L0_ffn_W2, L0_ffn_bf2)
    return h

_drawn_inputs = setup_inputs


def setup_inputs(seed=0):
    import zlib

    import numpy as np

    out = dict(_drawn_inputs(seed))
    spreads = {'L0_tok_b': (0.0, 0.1),
     'L0_attn_proj_b': (0.0, 0.1),
     'L0_ffn_g1': (1.0, 0.2),
     'L0_ffn_b1': (0.0, 0.468),
     'L0_ffn_g2': (1.0, 0.6),
     'L0_ffn_b2': (0.0, 2.0),
     'L0_ffn_bq': (0.0, 0.8),
     'L0_ffn_bk': (0.0, 2.0),
     'L0_ffn_bv': (0.0, 0.8),
     'L0_ffn_bo': (0.0, 0.447),
     'L0_ffn_bm': (0.0, 0.273),
     'L0_ffn_bf1': (0.0, 0.566),
     'L0_ffn_bf2': (0.0, 0.1)}
    factors = {'L0_attn_qkv_w': 3.791,
     'L0_attn_proj_w': 3.727,
     'L0_attn_tab_kv': 8.0,
     'L0_attn_tab_kh': 8.0,
     'L0_attn_tab_vv': 8.0,
     'L0_attn_tab_vh': 8.0,
     'L0_ffn_Wq': 8.0,
     'L0_ffn_Wk': 8.0,
     'L0_ffn_Wv': 8.0,
     'L0_ffn_Wo': 8.0}
    for name, (base, spread) in spreads.items():
        noise = np.random.default_rng([zlib.crc32(name.encode()), seed]).standard_normal(out[name].shape)
        drawn = base * np.exp(spread * noise) if base else spread * noise
        out[name] = jnp.asarray(drawn.astype(out[name].dtype))
    for name, factor in factors.items():
        out[name] = (out[name] * factor).astype(out[name].dtype)
    return out
```

```python
from contextlib import ExitStack

import concourse.bass as bass
from concourse import mybir

F32 = mybir.dt.float32
ALU = mybir.AluOpType
ACT = mybir.ActivationFunctionType
AX = mybir.AxisListType
EPS = 1e-5

D = 192
LO, HI = 128, 64
IMG, P = 224, 16
GP = IMG // P
NT = GP * GP
TC = NT // 2
PIX = P * P * 3
KT = PIX // 128
H1, DH1 = 12, 64
SIDE = 13
ROWS = (NT - 1) // SIDE
IDX0 = 15
TAB = 31
SLOT = 16
KQ = DH1 + 2 * SLOT
GROUP = 4
GT = GROUP * NT


def counts(n):
    return not (isinstance(n, int) and n <= 0)


def tokenizer(nc, ctx, io, arena, psum, hA, nimg):
    OCT = nimg // 8
    NIN = 9
    off = [0]

    def take(cols):
        a = arena[:, off[0]:off[0] + cols]
        off[0] += cols
        return a

    wall = take(5 * KT * D).rearrange("p (v t n) -> p v t n", v=5, t=KT)
    CLS = ["mid", "top", "bot", "left", "right", "tl", "tr", "bl", "br"]
    wcls = {c: take(KT * D).rearrange("p (t n) -> p t n", t=KT) for c in CLS}
    xin = [take(KT * 128).rearrange("p (t m) -> p t m", t=KT) for _ in range(4)]
    hout = [take(D) for _ in range(4)]
    bias = take(D)
    sem = lambda n: ctx.enter_context(nc.semaphore(n))
    w_loaded, bias_loaded = sem("w_loaded"), sem("tokb_loaded")
    x_loaded = [sem(f"x_loaded{i}") for i in range(4)]
    tok_seen = sem("tok_seen")
    w_summed, tok_psum, tok_done = sem("w_summed"), sem("tok_psum"), sem("tok_done")
    h_stored = [sem(f"h_stored{i}") for i in range(4)]
    wpart = sem("w_partial")

    def octet():
        return [("mid", k, 128) for k in range(NIN)] + [(c, 0, 96) for c in CLS[1:5]]
    NCH = len(octet())
    corners = [(c, 0, nimg) for c in CLS[5:]]

    def x_src(cls, k, o):
        if cls == "mid":
            return io["xI"][o, k]
        if cls in CLS[1:5]:
            return io["xE"][CLS.index(cls) - 1, o]
        return io["xC"][CLS.index(cls) - 5]

    RE = nimg * 144
    RC = RE + 4 * nimg * 12

    def h_dst(cls, k, o, m):
        if cls == "mid":
            return hA[bass.ds(o * (NIN * 128) + k * 128, m), :]
        if cls in CLS[1:5]:
            return hA[bass.ds(o * 96 + RE + (CLS.index(cls) - 1) * nimg * 12, m), :]
        r = RC + (CLS.index(cls) - 5) * nimg
        return hA[r:r + m, :]

    USE = [len([j for j in range(NCH) if j % 4 == s]) for s in range(4)]

    def uses(j, o):
        return o * USE[j % 4] + j // 4

    with nc.Block() as block:
        @block.sync
        def _(sp):
            sp.dma_start(wall, io["tokW"]).then_inc(w_loaded, 16)
            sp.dma_start(bias, io["tokb"].partition_broadcast(128)).then_inc(bias_loaded, 16)

            def load(j, o, item):
                cls, k, m = item
                sp.dma_start(xin[j % 4][:, :, 0:m], x_src(cls, k, o)).then_inc(x_loaded[j % 4], 16)
            for j in range(4):
                load(j, 0, octet()[j])

            def body(o, following):
                for j in range(4, NCH):
                    sp.wait_ge(tok_psum, o * NCH + j - 3)
                    load(j, o, octet()[j])
                for j in (1, 2, 3, 0):
                    last = max(i for i in range(NCH) if i % 4 == j)
                    sp.wait_ge(tok_psum, o * NCH + last + 1)
                    sp.sem_inc(tok_seen, 1)
                    load(j, o + 1, following[j])
            body(0, octet())
            with sp.Fori(1, OCT - 1) as o:
                body(o, octet())
            body(OCT - 1, corners)

        @block.tensor
        def _(pe):
            pe.wait_ge(w_summed, 1)

            def product(j, o, item):
                cls, k, m = item
                if cls == "top" and isinstance(o, int):
                    pe.wait_ge(w_summed, 2)
                pe.wait_ge(x_loaded[j % 4], 16 * (uses(j, o) + 1))
                if counts(o * NCH + j - (3 if j >= 4 else j)):
                    pe.wait_ge(tok_done, o * NCH + j - (3 if j >= 4 else j))
                for t in range(KT):
                    mm = nc.tensor.matmul(psum[0:m, j % 4, 0:D], xin[j % 4][:, t, 0:m], wcls[cls][:, t, :],
                                          start=(t == 0), stop=(t == KT - 1))
                mm.then_inc(tok_psum, 1)
            for j, item in enumerate(octet()):
                product(j, 0, item)
            with pe.Fori(1, OCT) as o:
                for j, item in enumerate(octet()):
                    product(j, o, item)
            for j, item in enumerate(corners):
                product(j, OCT, item)

        @block.vector
        def _(dve):
            dve.wait_ge(w_loaded, 16)
            v = nc.vector
            mid = wcls["mid"]
            v.tensor_tensor(mid, wall[:, 0], wall[:, 1], ALU.add).then_inc(wpart, 1)
            for n in range(2, 5):
                dve.wait_ge(wpart, n - 1)
                ins = v.tensor_tensor(mid, mid, wall[:, n], ALU.add).then_inc(wpart, 1)
            dve.wait_ge(wpart, 4)
            dve.sem_inc(w_summed, 1)
            n = 4
            first = {}
            for step in range(3):
                for cls in CLS[1:]:
                    top, bot = cls in ("top", "tl", "tr"), cls in ("bot", "bl", "br")
                    left, right = cls in ("left", "tl", "bl"), cls in ("right", "tr", "br")
                    for jh in range(2):
                        for ih in range(2):
                            parts = {1, 2, 3, 4}
                            if top and ih == 0:
                                parts -= {2, 4}
                            if bot and ih == 1:
                                parts -= {1, 3}
                            if left and jh == 0:
                                parts -= {3, 4}
                            if right and jh == 1:
                                parts -= {1, 2}
                            whole = (slice(0, 128), 3 * jh + 2 * ih)
                            half = (slice(64 * ih, 64 * ih + 64), 3 * jh + 1)
                            for ps, t in (whole, half):
                                dst = wcls[cls][ps, t, :]
                                if step == 0:
                                    if len(parts) == 4:
                                        v.tensor_copy(dst, mid[ps, t, :]).then_inc(wpart, 1)
                                    else:
                                        v.tensor_tensor(dst, wall[ps, 0, t, :], wall[ps, min(parts), t, :],
                                                        ALU.add).then_inc(wpart, 1)
                                    n += 1
                                elif step == 1 and len(parts) == 2:
                                    v.tensor_tensor(dst, dst, wall[ps, max(parts), t, :], ALU.add).then_inc(wpart, 1)
                                    n += 1
                dve.wait_ge(wpart, n)
            dve.sem_inc(w_summed, 1)
            dve.wait_ge(bias_loaded, 16)

            def finish(j, o, item):
                m = item[2]
                dve.wait_ge(tok_psum, o * NCH + j + 1)
                if counts(16 * uses(j, o)):
                    dve.wait_ge(h_stored[j % 4], 16 * uses(j, o))
                v.tensor_tensor(hout[j % 4][0:m], psum[0:m, j % 4, 0:D], bias[0:m], ALU.add).then_inc(tok_done, 1)
            for j, item in enumerate(octet()):
                finish(j, 0, item)
            with dve.Fori(1, OCT) as o:
                for j, item in enumerate(octet()):
                    finish(j, o, item)
            for j, item in enumerate(corners):
                finish(j, OCT, item)

        @block.scalar
        def _(act):
            def store(j, o, item):
                act.wait_ge(tok_done, o * NCH + j + 1)
                act.dma_start(h_dst(*item[:2], o, item[2]), hout[j % 4][0:item[2]]).then_inc(h_stored[j % 4], 16)
            for j, item in enumerate(octet()):
                store(j, 0, item)
            with act.Fori(1, OCT) as o:
                for j, item in enumerate(octet()):
                    store(j, o, item)
            for j, item in enumerate(corners):
                store(j, OCT, item)
            for s in range(4):
                act.wait_ge(h_stored[s], 16 * (OCT * USE[s] + 1))


def attention_weights(nc, ctx, io, w, arena, psum, pv_rows):
    sem = lambda n: ctx.enter_context(nc.semaphore(n))
    loaded, built, tk_psum, tk_done = sem("aw_loaded"), sem("aw_built"), sem("tabk_psum"), sem("tabk_done")
    tv_psum, tv_done, pv_stored, pv_loaded = sem("tabv_psum"), sem("tabv_done"), sem("pv_stored"), sem("pv_loaded")
    pairs_up = sem("pairs_up")
    wq_d = arena[0:DH1, 0:H1 * D]
    proj_d = arena[0:DH1, H1 * D:2 * H1 * D]
    tabk = arena[0:DH1, 2 * H1 * D:2 * H1 * D + 2 * TAB]
    tabv = arena[0:DH1, 2 * H1 * D + 2 * TAB:2 * H1 * D + 4 * TAB]
    pv_sb = arena[0:2 * TAB, 3 * H1 * D:4 * H1 * D]
    t0 = arena[64:65, 4 * H1 * D:4 * H1 * D + 4 * DH1]
    n_loads = 13 + 3 * H1

    with nc.Block() as block:
        @block.sync
        def _(sp):
            n = 0
            for dst, src in ((wq_d, io["wq_d"]), (proj_d, io["proj_d"]), (tabk, io["tabk"]), (tabv, io["tabv"]),
                             (w["qkv_lo"][:, :], io["qkvT"][0:LO, :]), (w["qkv_hi"][0:HI, :], io["qkvT"][LO:D, :]),
                             (w["proj"], io["proj_p"]), (w["projb_lo"], io["projb"][0:LO, :]),
                             (w["projb_hi"], io["projb"][LO:D, :]), (w["ident"], io["ident"]),
                             (t0, io["t0"]), (w["xT_hi"][HI:HI + 1, :], io["first"]),
                             (w["mhalf"], io["mhalf"])):
                sp.dma_start(dst, src).then_inc(loaded, 16)
                n += 1
            for h in range(H1):
                sp.dma_start(w["kx"][DH1:KQ, h, :], io["onehot"]).then_inc(loaded, 16)
                for c in range(2):
                    sp.dma_start(w["vx"][:, c, h, DH1:KQ], io["onehotT"][c]).then_inc(loaded, 16)
                n += 3
            assert n == n_loads
            sp.wait_ge(tv_done, 6)
            sp.dma_start(pv_rows.rearrange("s i n -> (s i) n"), pv_sb).then_inc(pv_stored, 16)
            sp.wait_ge(pv_stored, 16)
            m = 0
            for side in range(2):
                n = ROWS if side == 0 else SIDE
                for h in range(H1):
                    if h < 8:
                        dst = w["pv_a"][h:h + 8 * (SLOT - 1) + 1:8, side * (ROWS + 1):side * (ROWS + 1) + n + 1, :]
                    else:
                        at = 64 * side + h - 8
                        dst = w["pv_b"][at:at + 4 * (SLOT - 1) + 1:4, 0:n + 1, :]
                    row = H1 * D
                    base = side * TAB * row + h * D
                    sp.dma_start(dst[:, 0:n, :], bass.AP(tensor=pv_rows.tensor, offset=base + (IDX0 - n + 1) * row,
                                                         ap=[[row, SLOT], [row, n], [1, D]])).then_inc(pv_loaded, 16)
                    sp.dma_start(dst[:, n, :], bass.AP(tensor=pv_rows.tensor, offset=base,
                                                       ap=[[0, SLOT], [1, D]])).then_inc(pv_loaded, 16)
                    m += 2
            sp.wait_ge(pv_loaded, 16 * m)

        @block.tensor
        def _(pe):
            pe.wait_ge(loaded, 16 * n_loads)
            for f, (a, m) in enumerate(((0, LO), (LO, HI))):
                for h in range(H1):
                    bank = f * 2 + h // 6
                    mm = nc.tensor.matmul(psum[0:m, bank, (h % 6) * 2 * TAB:(h % 6 + 1) * 2 * TAB],
                                          wq_d[:, h * D + a:h * D + a + m], tabk, start=True, stop=True)
            mm.then_inc(tk_psum, 1)
            for n in range(6):
                bank = 4 + n % 4
                if n >= 4:
                    pe.wait_ge(tv_done, n - 3)
                nc.tensor.matmul(psum[0:2 * TAB, bank, 0:2 * D], tabv, proj_d[:, n * 2 * D:(n + 1) * 2 * D],
                                 start=True, stop=True).then_inc(tv_psum, 1)

        @block.scalar
        def _(act):
            for n in range(6):
                act.wait_ge(tv_psum, n + 1)
                nc.scalar.copy(pv_sb[:, n * 2 * D:(n + 1) * 2 * D], psum[0:2 * TAB, 4 + n % 4, 0:2 * D]).then_inc(tv_done, 1)

        @block.vector
        def _(dve):
            v = nc.vector
            dve.wait_ge(loaded, 16 * n_loads)
            scale = DH1 ** -0.5
            qcols = slice(0, H1 * DH1)
            v.tensor_scalar(w["qkv_lo"][:, qcols], w["qkv_lo"][:, qcols], scale, None, ALU.mult).then_inc(built, 1)
            v.tensor_scalar(w["qkv_hi"][0:HI, qcols], w["qkv_hi"][0:HI, qcols], scale, None, ALU.mult).then_inc(built, 1)
            v.memset(w["qkv_hi"][HI:HI + 1, qcols], 0.0).then_inc(built, 1)
            for n in range(2):
                dst = w["qkv_hi"][HI:HI + 1, (n + 1) * H1 * DH1:(n + 2) * H1 * DH1].rearrange("p (h d) -> p h d", h=H1)
                a, b = (t0[:, (2 * n + k) * DH1:(2 * n + k + 1) * DH1].rearrange("p (o d) -> p o d", o=1)
                        .broadcast_to([1, H1, DH1]) for k in range(2))
                v.tensor_tensor(dst, a, b, ALU.add).then_inc(built, 1)
            dve.wait_ge(tk_psum, 1)
            for f, m in enumerate((LO, HI)):
                for bank, nh, hs in ((0, 6, "a"), (1, 2, "a"), (1, 4, "b")):
                    h0 = 0 if nh != 4 else 2
                    src = psum[0:m, f * 2 + bank, h0 * 2 * TAB:(h0 + nh) * 2 * TAB]
                    src = src.rearrange("p (h s i) -> p s i h", h=nh, s=2)
                    d0 = 6 if nh == 2 else 0
                    for side in range(2):
                        dst = w[f"tw_{hs}{f}"][:, side, :, d0:d0 + nh]
                        v.tensor_scalar(dst, src[:, side], scale, None, ALU.mult).then_inc(tk_done, 1)
            dve.wait_ge(tk_done, 12)
            for f, m in enumerate((LO, HI)):
                for hs, nh in (("a", 8), ("b", 4)):
                    for side in range(2):
                        v.tensor_copy(w[f"tz_{hs}{f}"][:, side], w[f"tw_{hs}{f}"][:, side, 0:1, :]
                                      .broadcast_to([m, SLOT, nh])).then_inc(tk_done, 1)
            dve.wait_ge(tk_done, 20)
            dve.wait_ge(built, 5)


def attention(nc, ctx, io, w, arena, psum, hA, h2, nimg):
    NG = nimg // GROUP
    NH = GROUP * H1
    sem = lambda n: ctx.enter_context(nc.semaphore(n))
    h_in, h_again, h_out = sem("h_in"), sem("h_again"), sem("h2_stored")
    stats_seen, kb_seen = sem("stats_seen"), sem("kb_seen")
    stats, moments, var_eps, rstd_ok, xhat_ok = (sem(n) for n in ("stats", "moments", "var_eps", "rstd", "xhat"))
    xT_psum, xT_ok = sem("xT_psum"), sem("xT_ok")
    kb_psum, kb_dve, kb_act = sem("kb_psum"), sem("kb_dve"), sem("kb_act")
    kb_moved_a, kb_moved_b = sem("kb_moved_a"), sem("kb_moved_b")
    qk_psum, v_psum, qk_ok, v_ok = (sem(n) for n in ("qk_psum", "v_psum", "qk_ok", "v_ok"))
    logits, max_ok, exp_ok, recip_ok, prob_ok = (sem(n) for n in ("logits", "max_ok", "exp_ok", "recip_ok", "prob_ok"))
    pT_psum, pT_ok, o_psum, o_ok, a_ok = (sem(n) for n in ("pT_psum", "pT_ok", "o_psum", "o_ok", "a_ok"))
    a_moved_a, a_moved_b = sem("a_moved_a"), sem("a_moved_b")
    y_psum, y_ok, vb_psum, vb_ok, hT_psum, h2_ok = (sem(n) for n in ("y_psum", "y_ok", "vb_psum", "vb_ok", "hT_psum", "h2_ok"))

    off = [0]

    def take(cols):
        a = arena[:, off[0]:off[0] + cols]
        off[0] += cols
        return a
    hin = take(8 * D).rearrange("p (c n) -> p c n", c=8)
    hres = take(8 * D).rearrange("p (c n) -> p c n", c=8)
    xhat = take(8 * D).rearrange("p (c n) -> p c n", c=8)
    st = take(8 * 6).rearrange("p (c n) -> p c n", c=8)
    mv = take(8 * 2).rearrange("p (c n) -> p c n", c=8)
    ve, rstd = take(8), take(8)
    kst = take(3 * GT).rearrange("p (t n) -> p t n", t=3)
    qx = take(H1 * NT).rearrange("p (h n) -> p h n", h=H1)
    prob = take(3 * 2 * NT).rearrange("p (b c n) -> p b c n", b=3, c=2)
    pT = take(2 * 2 * NT).rearrange("p (b c n) -> p b c n", b=2, c=2)
    nmax = take(3 * 2).rearrange("p (b c) -> p b c", b=3)
    psums = take(3 * 2).rearrange("p (b c) -> p b c", b=3)
    prec = take(3 * 2).rearrange("p (b c) -> p b c", b=3)
    oT = take(2 * 6 * NT).rearrange("p (b h n) -> p b h n", b=2, h=6)
    ast = take(H1 * NT).rearrange("p (h n) -> p h n", h=H1)
    ap = take(3 * GT).rearrange("p (t n) -> p t n", t=3)
    yT = take(2 * GT).rearrange("p (f n) -> p f n", f=2)
    assert off[0] <= arena.shape[1], off[0]
    xT_lo = w["xT_lo"].rearrange("p (i n) -> p i n", i=GROUP)
    xT_hi = w["xT_hi"].rearrange("p (i n) -> p i n", i=GROUP)
    kx, vx = w["kx"], w["vx"]
    QK, VB, L0, T0, OB, YB = 0, 1, 2, 4, 6, 7

    RE = nimg * 144
    RC = RE + 4 * nimg * 12

    def h_loads(dst, g):
        out = []
        d = dst.rearrange("p (i c) n -> p i c n", i=GROUP)
        b0 = g * GROUP
        for c in range(2):
            for a in range(6):
                to = d[14 * (a + 1 - c) + 1:14 * (a + 1 - c) + 13, :, c, :]
                rows = hA[bass.ds(b0 * 144, GROUP * 144), :].rearrange("(i a b) n -> a b i n", i=GROUP, a=12)[6 * c + a]
                out.append((to, rows))
            e = RE + c * nimg * 12
            out.append((d[14 * 6 * c + 1:14 * 6 * c + 13, :, c, :],
                        hA[bass.ds(b0 * 12 + e, GROUP * 12), :].rearrange("(i b) n -> b i n", b=12)))
            for s in range(2):
                e = RE + (2 + s) * nimg * 12
                at = 14 * (1 - c) + 13 * s
                out.append((d[at:at + 14 * 5 + 1:14, :, c, :],
                            hA[bass.ds(b0 * 12 + e, GROUP * 12), :].rearrange("(i a) n -> a i n", i=GROUP)[6 * c:6 * c + 6]))
                r = RC + (2 * c + s) * nimg
                at = 14 * 6 * c + 13 * s
                out.append((d[at:at + 1, :, c, :], hA[bass.ds(b0 + r, GROUP), :].rearrange("(o i) n -> o i n", o=1)))
        return out
    NL = 2 * (6 + 1 + 2 + 2)

    def kb_jobs():
        for side in range(2):
            n, step = (ROWS, SIDE) if side == 0 else (SIDE, ROWS)
            cut = (n + 1) // 2
            for hs, nh, p0 in (("a", 8, 0), ("b", 4, 64 * side)):
                for part, gs in enumerate((range(0, cut), range(cut, n))):
                    yield side, hs, nh, p0, part, gs

    def tokens(a, side, gs):
        if side == 0:
            lo = 1 + SIDE * gs[0]
            return a[:, :, lo:lo + SIDE * len(gs)].rearrange("p i (g j) -> p g i j", g=len(gs))
        return a[:, :, 1:].rearrange("p i (j g) -> p g i j", g=SIDE)[:, gs[0]:gs[-1] + 1]

    with nc.Block() as block:
        @block.sync
        def _(sp):
            for to, src in h_loads(hin, 0):
                sp.dma_start(to, src).then_inc(h_in, 16)

            def move(dst, src, s):
                sp.dma_start(dst, src).then_inc(s, 16)

            def bias_in(i, g):
                cols = slice(i * NT, (i + 1) * NT)
                if i == 0:
                    sp.wait_ge(kb_dve, 4 * (g + 1))
                    sp.sem_inc(kb_seen, 1)
                    sp.wait_ge(kb_act, 4 * (g + 1))
                    sp.sem_inc(kb_seen, 1)
                if counts(g * NH + (i * H1 - 4 if i else 0)):
                    sp.wait_ge(logits, g * NH + (i * H1 - 4 if i else 0))
                for side in range(2):
                    for h in range(8):
                        move(qx[DH1 + SLOT * side:DH1 + SLOT * (side + 1), h, :],
                             kst[h:h + 8 * (SLOT - 1) + 1:8, side, cols], kb_moved_a)
                if counts(g * NH + i * H1):
                    sp.wait_ge(logits, g * NH + i * H1)
                for side in range(2):
                    for h in range(4):
                        move(qx[DH1 + SLOT * side:DH1 + SLOT * (side + 1), 8 + h, :],
                             kst[64 * side + h:64 * side + h + 4 * (SLOT - 1) + 1:4, 2, cols], kb_moved_b)

            def sums_out(i, g):
                cols = slice(i * NT, (i + 1) * NT)
                sp.wait_ge(a_ok, g * NH // 2 + (i * H1 + 8) // 2)
                for side in range(2):
                    for h in range(8):
                        move(ap[h:h + 8 * (SLOT - 1) + 1:8, side, cols],
                             ast[DH1 + SLOT * side:DH1 + SLOT * (side + 1), h, :], a_moved_a)
                sp.wait_ge(a_ok, g * NH // 2 + (i + 1) * H1 // 2)
                for side in range(2):
                    for h in range(4):
                        move(ap[64 * side + h:64 * side + h + 4 * (SLOT - 1) + 1:4, 2, cols],
                             ast[DH1 + SLOT * side:DH1 + SLOT * (side + 1), 8 + h, :], a_moved_b)

            def group(g, last):
                bias_in(0, g)
                for i in range(GROUP):
                    if i + 1 < GROUP:
                        bias_in(i + 1, g)
                    sums_out(i, g)
                    if i == 0 and not last:
                        sp.wait_ge(xhat_ok, 8 * (g + 1))
                        for to, src in h_loads(hin, g + 1):
                            sp.dma_start(to, src).then_inc(h_in, 16)
                    if i == 1:
                        if counts(16 * GROUP * g):
                            sp.wait_ge(h_out, 16 * GROUP * g)
                        for to, src in h_loads(hres, g):
                            sp.dma_start(to, src).then_inc(h_again, 16)
                for i in range(GROUP):
                    sp.wait_ge(h2_ok, GROUP * g + i + 1)
                    sp.dma_start(h2[bass.ds(g * GT + i * NT, NT), :].rearrange("(c p) n -> p c n", p=TC),
                                 hres[0:TC, 2 * i:2 * i + 2, :]).then_inc(h_out, 16)
            group(0, False)
            with sp.Fori(1, NG - 1) as g:
                group(g, False)
            group(NG - 1, True)
            sp.wait_ge(h_out, 16 * GROUP * NG)

        @block.tensor
        def _(pe):
            mm = nc.tensor.matmul

            def transposes_in(g):
                for i in range(GROUP):
                    pe.wait_ge(xhat_ok, 8 * g + 2 * (i + 1))
                    if counts(GROUP * g):
                        pe.wait_ge(xT_ok, GROUP * g)
                    for c in range(2):
                        for f, (a, m) in enumerate(((0, LO), (LO, HI))):
                            t = nc.tensor.transpose(psum[0:m, i, (2 * f + c) * TC:(2 * f + c + 1) * TC],
                                                    xhat[0:TC, 2 * i + c, a:a + m], w["ident"][0:TC, 0:TC])
                    t.then_inc(xT_psum, 1)

            def bias_rows(g):
                pe.wait_ge(xT_ok, GROUP * (g + 1))
                for j, (side, hs, nh, p0, part, gs) in enumerate(kb_jobs()):
                    m = nh * SLOT
                    out = psum[p0:p0 + m, j, :]
                    n = GROUP * (SIDE if side == 0 else ROWS)
                    for k, q in enumerate(gs):
                        for a, x in enumerate((xT_lo, xT_hi[0:HI])):
                            t = mm(out[:, k * n:(k + 1) * n], w[f"tw_{hs}{a}"][:, side, IDX0 - q:IDX0 - q + SLOT, :],
                                   tokens(x, side, [q])[:, 0], start=(a == 0), stop=(a == 1), skip_group_check=True)
                    if part:
                        k = len(gs)
                        for a, x in enumerate((xT_lo, xT_hi[0:HI])):
                            t = mm(out[:, k * n:k * n + GROUP], w[f"tz_{hs}{a}"][:, side], x[:, :, 0],
                                   start=(a == 0), stop=(a == 1), skip_group_check=True)
                    t.then_inc(kb_psum, 1)

            def project(g, i, p):
                u = 24 * g + 6 * i + p
                if counts(u):
                    pe.wait_ge(qk_ok, u)
                for n in range(2):
                    cols = slice((n * H1 + 2 * p) * DH1, (n * H1 + 2 * p + 2) * DH1)
                    out = psum[:, QK, n * NT:(n + 1) * NT]
                    mm(out, w["qkv_lo"][:, cols], xT_lo[:, i, :], start=True, stop=False)
                    t = mm(out, w["qkv_hi"][:, cols], xT_hi[:, i, :], start=False, stop=True)
                t.then_inc(qk_psum, 1)
                if counts(u):
                    pe.wait_ge(v_ok, u)
                for c in range(2):
                    cols = slice((2 * H1 + 2 * p) * DH1, (2 * H1 + 2 * p + 2) * DH1)
                    out = psum[0:TC, VB, c * 2 * DH1:(c + 1) * 2 * DH1]
                    mm(out, xT_lo[:, i, c * TC:(c + 1) * TC], w["qkv_lo"][:, cols], start=True, stop=False)
                    t = mm(out, xT_hi[:, i, c * TC:(c + 1) * TC], w["qkv_hi"][:, cols], start=False, stop=True)
                t.then_inc(v_psum, 1)

            def make_logits(g, k):
                i, h = k // H1, k % H1
                pe.wait_ge(qk_ok, 24 * g + k // 2 + 1)
                if h < 8:
                    pe.wait_ge(kb_moved_a, 16 * 16 * (GROUP * g + i + 1))
                else:
                    pe.wait_ge(kb_moved_b, 16 * 8 * (GROUP * g + i + 1))
                if counts(g * NH + max(k - 1, 0)):
                    pe.wait_ge(exp_ok, g * NH + max(k - 1, 0))
                for c in range(2):
                    t = mm(psum[0:TC, L0 + k % 2, c * NT:(c + 1) * NT], qx[0:KQ, h, c * TC:(c + 1) * TC], kx[0:KQ, h, :],
                           start=True, stop=True)
                t.then_inc(logits, 1)

            def turn(g, k):
                pe.wait_ge(prob_ok, g * NH + k + 1)
                if counts(g * NH + max(k - 1, 0)):
                    pe.wait_ge(pT_ok, g * NH + max(k - 1, 0))
                for c in range(2):
                    for kc in range(2):
                        t = nc.tensor.transpose(psum[0:TC, T0 + k % 2, kc * NT + c * TC:kc * NT + (c + 1) * TC],
                                                prob[0:TC, k % 3, c, kc * TC:(kc + 1) * TC], w["ident"][0:TC, 0:TC])
                t.then_inc(pT_psum, 1)

            def weigh(g, k):
                pe.wait_ge(pT_ok, g * NH + k + 1)
                pe.wait_ge(v_ok, 24 * g + k // 2 + 1)
                if k % 2 == 0:
                    if counts(g * NH // 2 + k // 2):
                        pe.wait_ge(o_ok, g * NH // 2 + k // 2)
                    if counts(g * NH // 2 + k // 2):
                        pe.wait_ge(a_ok, g * NH // 2 + k // 2)
                for kc in range(2):
                    t = mm(psum[0:KQ, OB, (k % 2) * NT:(k % 2 + 1) * NT], vx[0:TC, kc, k % H1, :], pT[0:TC, k % 2, kc, :],
                           start=(kc == 0), stop=(kc == 1))
                t.then_inc(o_psum, 1)

            def output(g, i):
                pe.wait_ge(o_ok, g * NH // 2 + (i + 1) * 6)
                if counts(GROUP * g + i):
                    pe.wait_ge(y_ok, GROUP * g + i)
                for f, (a, m) in enumerate(((0, LO), (LO, HI))):
                    for p in range(6):
                        t = mm(psum[0:m, YB, f * NT:(f + 1) * NT], w["proj"][:, p, a:a + m], oT[:, i % 2, p, :],
                               start=(p == 0), stop=(p == 5))
                t.then_inc(y_psum, 1)

            def value_tables(g):
                pe.wait_ge(a_moved_a, 16 * 16 * GROUP * (g + 1))
                pe.wait_ge(a_moved_b, 16 * 8 * GROUP * (g + 1))
                pe.wait_ge(y_ok, GROUP * (g + 1))
                j = 0
                for side in range(2):
                    n, each = (ROWS, SIDE) if side == 0 else (SIDE, ROWS)
                    cut = (n + 1) // 2
                    at, bt = (ap[:, t, :].rearrange("p (i n) -> p i n", i=GROUP) for t in (side, 2))
                    bt = bt[64 * side:64 * side + 64]
                    for f, (a, m) in enumerate(((0, LO), (LO, HI))):
                        for part, gs in enumerate((range(0, cut), range(cut, n))):
                            out = psum[0:m, j, :]
                            for k, q in enumerate(gs):
                                o = out[:, k * GROUP * each:(k + 1) * GROUP * each]
                                mm(o, w["pv_a"][:, side * (ROWS + 1) + n - 1 - q, a:a + m], tokens(at, side, [q])[:, 0],
                                   start=True, stop=False, skip_group_check=True)
                                t = mm(o, w["pv_b"][64 * side:64 * side + 64, n - 1 - q, a:a + m], tokens(bt, side, [q])[:, 0],
                                       start=False, stop=True, skip_group_check=True)
                            if part:
                                k = len(gs) * GROUP * each
                                mm(out[:, k:k + GROUP], w["pv_a"][:, side * (ROWS + 1) + n, a:a + m], at[:, :, 0],
                                   start=True, stop=False, skip_group_check=True)
                                t = mm(out[:, k:k + GROUP], w["pv_b"][64 * side:64 * side + 64, n, a:a + m], bt[:, :, 0],
                                       start=False, stop=True, skip_group_check=True)
                            t.then_inc(vb_psum, 1)
                            j += 1

            def transposes_out(g):
                pe.wait_ge(vb_ok, 8 * (g + 1))
                for i in range(GROUP):
                    for c in range(2):
                        for f, (a, m) in enumerate(((0, LO), (LO, HI))):
                            t = nc.tensor.transpose(psum[0:TC, i, c * D + a:c * D + a + m],
                                                    yT[0:m, f, i * NT + c * TC:i * NT + (c + 1) * TC],
                                                    w["ident"][0:m, 0:m])
                    t.then_inc(hT_psum, 1)

            def group(g):
                if counts(4 * g):
                    pe.wait_ge(h2_ok, 4 * g)
                transposes_in(g)
                bias_rows(g)
                pe.wait_ge(kb_dve, 4 * (g + 1))
                pe.wait_ge(kb_act, 4 * (g + 1))
                for p in range(6):
                    project(g, 0, p)
                for s in range(NH + 6):
                    if s < NH:
                        make_logits(g, s)
                    if 0 <= s - 2 < NH:
                        turn(g, s - 2)
                    if 0 <= s - 3 < NH:
                        weigh(g, s - 3)
                    if s >= 5 and (s - 4) % 2 == 1:
                        i, p = (s - 4) // H1, (s - 4) % H1 // 2
                        if i + 1 < GROUP:
                            project(g, i + 1, p)
                    if s >= H1 + 5 and (s - 5) % H1 == 0:
                        output(g, (s - 5) // H1 - 1)
                value_tables(g)
                transposes_out(g)
            group(0)
            with pe.Fori(1, NG) as g:
                group(g)

        def kb_evacuate(eng, copy, g, parity, done):
            for j, (side, hs, nh, p0, part, gs) in enumerate(kb_jobs()):
                if j % 2 != parity:
                    continue
                eng.wait_ge(kb_psum, 8 * g + j + 1)
                m, each = nh * SLOT, (SIDE if side == 0 else ROWS)
                tile = side if hs == "a" else 2
                dst = kst[p0:p0 + m, tile, :].rearrange("p (i n) -> p i n", i=GROUP)
                n = len(gs) * GROUP * each
                src = psum[p0:p0 + m, j, 0:n].rearrange("p (g i j) -> p g i j", g=len(gs), i=GROUP)
                ins = copy(tokens(dst, side, gs), src)
                if part:
                    ins = copy(dst[:, :, 0], psum[p0:p0 + m, j, n:n + GROUP])
                ins.then_inc(done, 1)

        @block.scalar
        def _(act):
            def take_v(g, i, p):
                u = 24 * g + 6 * i + p
                act.wait_ge(v_psum, u + 1)
                nc.scalar.copy(vx[0:TC, :, 2 * p:2 * p + 2, 0:DH1],
                               psum[0:TC, VB, 0:4 * DH1].rearrange("p (c e d) -> p c e d", c=2, e=2)).then_inc(v_ok, 1)

            def exponent(g, k):
                act.wait_ge(max_ok, g * NH + k + 1)
                if counts(g * NH + max(k - 2, 0)):
                    act.wait_ge(pT_psum, g * NH + max(k - 2, 0))
                for c in range(2):
                    e = nc.scalar.activation(prob[0:TC, k % 3, c, :], psum[0:TC, L0 + k % 2, c * NT:(c + 1) * NT], ACT.Exp,
                                             bias=nmax[0:TC, k % 3, c:c + 1], accum_out=psums[0:TC, k % 3, c:c + 1])
                e.then_inc(exp_ok, 1)

            def take_out(g, u):
                i, p = u // 6, u % 6
                act.wait_ge(o_psum, g * NH + 2 * u + 2)
                if counts(GROUP * g + max(i - 1, 0)):
                    act.wait_ge(y_psum, GROUP * g + max(i - 1, 0))
                nc.scalar.copy(oT[0:DH1, i % 2, p, :], psum[0:DH1, OB, 0:NT])
                nc.scalar.copy(oT[DH1:2 * DH1, i % 2, p, :], psum[0:DH1, OB, NT:2 * NT]).then_inc(o_ok, 1)

            def group(g):
                if counts(16 * 16 * GROUP * g):
                    act.wait_ge(kb_moved_a, 16 * 16 * GROUP * g)
                if counts(16 * 8 * GROUP * g):
                    act.wait_ge(kb_moved_b, 16 * 8 * GROUP * g)
                kb_evacuate(act, nc.scalar.copy, g, 1, kb_act)
                for p in range(6):
                    take_v(g, 0, p)
                for s in range(NH + 6):
                    if s < NH:
                        exponent(g, s)
                    if s >= 4 and (s - 4) % 2 == 0 and (s - 4) // 2 < NH // 2:
                        take_out(g, (s - 4) // 2)
                    if s >= 5 and (s - 4) % 2 == 1:
                        i, p = (s - 4) // H1, (s - 4) % H1 // 2
                        if i + 1 < GROUP:
                            take_v(g, i + 1, p)
            group(0)
            with act.Fori(1, NG) as g:
                group(g)

        @block.gpsimd
        def _(pool):
            def norm(g):
                pool.wait_ge(var_eps, g + 1)
                nc.gpsimd.tensor_tensor(rstd[0:TC], ve[0:TC], w["mhalf"][0:TC], ALU.pow).then_inc(rstd_ok, 1)
            norm(0)

            def group(g, last):
                for k in range(NH):
                    pool.wait_ge(recip_ok, g * NH + k + 1)
                    b = k % 3
                    pr = prob[0:TC, b]
                    nc.gpsimd.tensor_tensor(pr, pr, prec[0:TC, b].rearrange("p (c o) -> p c o", o=1)
                                            .broadcast_to([TC, 2, NT]), ALU.mult).then_inc(prob_ok, 1)
                    if k == 30 and not last:
                        norm(g + 1)
            group(0, False)
            with pool.Fori(1, NG - 1) as g:
                group(g, False)
            group(NG - 1, True)

        @block.vector
        def _(dve):
            v = nc.vector

            def ln_stats(g):
                dve.wait_ge(h_in, 16 * NL * (g + 1))
                for c in range(8):
                    v.bn_stats(st[0:TC, c], hin[0:TC, c]).then_inc(stats, 1)
                dve.wait_ge(stats, 8 * (g + 1))
                dve.sem_inc(stats_seen, 1)
                for c in range(8):
                    v.bn_aggr(mv[0:TC, c], st[0:TC, c]).then_inc(moments, 1)
                dve.wait_ge(moments, 8 * (g + 1))
                v.tensor_scalar(ve[0:TC], mv[0:TC, :, 1], EPS, None, ALU.add).then_inc(var_eps, 1)

            def ln_apply(g):
                dve.wait_ge(rstd_ok, g + 1)
                if counts(GROUP * g):
                    dve.wait_ge(xT_psum, GROUP * g)
                for c in range(8):
                    v.tensor_scalar(xhat[0:TC, c], hin[0:TC, c], mv[0:TC, c, 0:1], rstd[0:TC, c:c + 1],
                                    ALU.subtract, ALU.mult).then_inc(xhat_ok, 1)

            def take_xT(g):
                for i in range(GROUP):
                    dve.wait_ge(xT_psum, GROUP * g + i + 1)
                    v.tensor_copy(xT_lo[:, i, :], psum[:, i, 0:NT])
                    v.tensor_copy(xT_hi[0:HI, i, :], psum[0:HI, i, NT:2 * NT]).then_inc(xT_ok, 1)

            def take_qk(g, i, p):
                dve.wait_ge(qk_psum, 24 * g + 6 * i + p + 1)
                v.tensor_copy(qx[0:DH1, 2 * p, :], psum[0:DH1, QK, 0:NT])
                v.tensor_copy(qx[0:DH1, 2 * p + 1, :], psum[DH1:2 * DH1, QK, 0:NT])
                v.tensor_copy(kx[0:DH1, 2 * p, :], psum[0:DH1, QK, NT:2 * NT])
                v.tensor_copy(kx[0:DH1, 2 * p + 1, :], psum[DH1:2 * DH1, QK, NT:2 * NT]).then_inc(qk_ok, 1)

            def maximum(g, k):
                dve.wait_ge(logits, g * NH + k + 1)
                v.tensor_reduce(nmax[0:TC, k % 3], psum[0:TC, L0 + k % 2, 0:2 * NT].rearrange("p (c n) -> p c n", c=2),
                                AX.X, ALU.max, negate=True).then_inc(max_ok, 1)

            def reciprocals(g, k):
                dve.wait_ge(exp_ok, g * NH + k + 1)
                v.reciprocal(prec[0:TC, k % 3], psums[0:TC, k % 3]).then_inc(recip_ok, 1)

            def take_pT(g, k):
                dve.wait_ge(pT_psum, g * NH + k + 1)
                if counts(g * NH + max(k - 1, 0)):
                    dve.wait_ge(o_psum, g * NH + max(k - 1, 0))
                v.tensor_copy(pT[0:TC, k % 2], psum[0:TC, T0 + k % 2, 0:2 * NT].rearrange("p (c n) -> p c n", c=2)).then_inc(pT_ok, 1)

            def take_sums(g, u):
                i, p = u // 6, u % 6
                dve.wait_ge(o_psum, g * NH + 2 * u + 2)
                if p < 4:
                    if counts(16 * 16 * (GROUP * g + i)):
                        dve.wait_ge(a_moved_a, 16 * 16 * (GROUP * g + i))
                else:
                    if counts(16 * 8 * (GROUP * g + i)):
                        dve.wait_ge(a_moved_b, 16 * 8 * (GROUP * g + i))
                v.tensor_copy(ast[DH1:KQ, 2 * p:2 * p + 2, :],
                              psum[DH1:KQ, OB, 0:2 * NT].rearrange("p (e n) -> p e n", e=2)).then_inc(a_ok, 1)

            def take_y(g, i):
                dve.wait_ge(y_psum, GROUP * g + i + 1)
                if counts(GROUP * g):
                    dve.wait_ge(hT_psum, GROUP * g)
                c = slice(i * NT, (i + 1) * NT)
                v.tensor_scalar(yT[:, 0, c], psum[:, YB, 0:NT], w["projb_lo"], None, ALU.add)
                v.tensor_scalar(yT[0:HI, 1, c], psum[0:HI, YB, NT:2 * NT], w["projb_hi"], None, ALU.add).then_inc(y_ok, 1)

            def add_tables(g):
                j = 0
                for side in range(2):
                    n, each = (ROWS, SIDE) if side == 0 else (SIDE, ROWS)
                    cut = (n + 1) // 2
                    for f, m in enumerate((LO, HI)):
                        for part, gs in enumerate((range(0, cut), range(cut, n))):
                            dve.wait_ge(vb_psum, 8 * g + j + 1)
                            dve.wait_ge(y_ok, GROUP * (g + 1))
                            if side:
                                dve.wait_ge(vb_ok, 8 * g + 4)
                            y = yT[0:m, f, :].rearrange("p (i n) -> p i n", i=GROUP)
                            k = len(gs) * GROUP * each
                            src = psum[0:m, j, 0:k].rearrange("p (g i j) -> p g i j", g=len(gs), i=GROUP)
                            ins = v.tensor_tensor(tokens(y, side, gs), src, tokens(y, side, gs), ALU.add)
                            if part:
                                ins = v.tensor_tensor(y[:, :, 0], psum[0:m, j, k:k + GROUP], y[:, :, 0], ALU.add)
                            ins.then_inc(vb_ok, 1)
                            j += 1

            def residual(g):
                dve.wait_ge(h_again, 16 * NL * (g + 1))
                for i in range(GROUP):
                    dve.wait_ge(hT_psum, GROUP * g + i + 1)
                    r = hres[0:TC, 2 * i:2 * i + 2, :]
                    v.tensor_tensor(r, psum[0:TC, i, 0:2 * D].rearrange("p (c n) -> p c n", c=2), r, ALU.add).then_inc(h2_ok, 1)

            ln_stats(0)
            ln_apply(0)

            def group(g, last):
                take_xT(g)
                if counts(16 * 16 * GROUP * g):
                    dve.wait_ge(kb_moved_a, 16 * 16 * GROUP * g)
                if counts(16 * 8 * GROUP * g):
                    dve.wait_ge(kb_moved_b, 16 * 8 * GROUP * g)
                kb_evacuate(dve, v.tensor_copy, g, 0, kb_dve)
                for p in range(6):
                    take_qk(g, 0, p)
                for s in range(NH + 6):
                    if 0 <= s - 1 < NH:
                        reciprocals(g, s - 1)
                    if s < NH:
                        maximum(g, s)
                    if 0 <= s - 2 < NH:
                        take_pT(g, s - 2)
                    if s >= 4 and (s - 4) % 2 == 0 and (s - 4) // 2 < NH // 2:
                        take_sums(g, (s - 4) // 2)
                    if s >= 5 and (s - 4) % 2 == 1:
                        i, p = (s - 4) // H1, (s - 4) % H1 // 2
                        if i + 1 < GROUP:
                            take_qk(g, i + 1, p)
                    if s >= H1 + 5 and (s - 5) % H1 == 0:
                        take_y(g, (s - 5) // H1 - 1)
                    if s == 30 and not last:
                        ln_stats(g + 1)
                    if s == 34 and not last:
                        ln_apply(g + 1)
                add_tables(g)
                residual(g)
            group(0, False)
            with dve.Fori(1, NG - 1) as g:
                group(g, False)
            group(NG - 1, True)



TOPK = max(1, int(round(0.15 * NT)))
DH3 = D // H1
F = 4 * D
FT = F // 128
HQ = 4
QT = HQ * TOPK


def feed_forward(nc, ctx, io, arena, psum, h2, out, nimg):
    def sems(*names):
        return [ctx.enter_context(nc.semaphore(n)) for n in names]
    off = [0]

    def take(cols):
        a = arena[:, off[0]:off[0] + cols]
        off[0] += cols
        return a

    def two(cols):
        return [take(cols) for _ in range(2)]

    def tok(cols=D):
        return [take(2 * cols)[0:TC].rearrange("p (c n) -> p c n", c=2) for _ in range(2)]
    W = {}
    for n in ("Wq", "Wk", "Wv", "Wo", "Wm", "W1"):
        c = F if n == "W1" else D
        W[n] = (take(c), take(c)[0:HI])
    W2 = take(FT * D).rearrange("p (t n) -> p t n", t=FT)
    row = {n: take(D) for n in ("g1", "b1", "g2", "b2", "Wr", "bv", "bo", "bm", "bf2")}
    col = {n: (take(1), take(1)[0:HI]) for n in ("bq", "bk")}
    bf1, br = take(FT), take(1)
    nbr = take(1)
    ident, ones = take(128), take(128)
    slots = take(TOPK)[0:TC]
    before = take(2 * NT)[0:TC].rearrange("p (c n) -> p c n", c=2)
    own = take(8)
    mhalf = take(2)[0:TC]
    hc, n0, xn, na, nn = tok(), tok(), tok(), tok(), tok()
    res, rb = tok(), tok()
    st = [take(12)[0:TC].rearrange("p (c n) -> p c n", c=2) for _ in range(2)]
    mv = [take(4)[0:TC].rearrange("p (c n) -> p c n", c=2) for _ in range(2)]
    ve, rs = [a[0:TC] for a in two(2)], [a[0:TC] for a in two(2)]
    st3 = take(12)[0:TC].rearrange("p (c n) -> p c n", c=2)
    mv3 = take(4)[0:TC].rearrange("p (c n) -> p c n", c=2)
    ve2, rs2 = take(2)[0:TC], take(2)[0:TC]
    cmp = [take(NT)[0:TC] for _ in range(4)]
    z = [a[0:TC] for a in two(2)]
    ez, ez1 = take(2)[0:TC], take(2)[0:TC]
    sel = [take(2 * (TOPK + 1))[0:TC].rearrange("p (c n) -> p c n", c=2) for _ in range(2)]
    zb = take(2 * TC)[0:TC].rearrange("p (c n) -> p c n", c=2)
    sb = take(2 * 128)[0:TC].rearrange("p (c n) -> p c n", c=2)
    junk = take(2 * D)[0:TC]
    lt, eq, rank = take(2)[0:TC], take(2)[0:TC], take(2)[0:TC]
    keep = [a[0:TC] for a in two(2)]
    nT = [(take(NT), take(NT)[0:HI]) for _ in range(2)]
    kT = [(take(NT), take(NT)[0:HI]) for _ in range(2)]
    vv = tok()
    nsel = (take(TOPK), take(TOPK)[0:HI])
    ssum, sinv = take(1), take(1)
    pooled = (take(1), take(1)[0:HI])
    selT = take(NT)[0:TOPK]
    qs = (take(TOPK), take(TOPK)[0:HI])
    qblk = (take(8 * TOPK).rearrange("p (h j) -> p h j", h=8), take(4 * TOPK)[0:HI].rearrange("p (h j) -> p h j", h=4))
    nmax, esum, einv = take(3)[0:QT], take(3)[0:QT], take(3)[0:QT]
    pr = take(3 * NT)[0:QT].rearrange("p (t n) -> p t n", t=3)
    pT = take(2 * 3 * QT)[0:TC].rearrange("p (c n) -> p c n", c=2)
    cm = (take(8 * TOPK).rearrange("p (h j) -> p h j", h=8), take(4 * TOPK)[0:HI].rearrange("p (h j) -> p h j", h=4))
    ctxT = (take(TOPK), take(TOPK)[0:HI])
    asel = take(D)[0:TOPK]
    mixT = (take(NT), take(NT)[0:HI])
    mixb, kept_mix = take(2 * D)[0:TC].rearrange("p (c n) -> p c n", c=2), take(2 * D)[0:TC].rearrange("p (c n) -> p c n", c=2)
    hh, hn, hg, n2 = tok(), tok(), tok(), tok()
    n2T = (take(NT), take(NT)[0:HI])
    gT = take(FT * NT).rearrange("p (t n) -> p t n", t=FT)
    oo = tok()
    assert off[0] <= arena.shape[1], off[0]
    NTB, RB, SB, KB, VB, L0, L1, UB = range(8)
    GA, GB, SS, ST, QA, QB = 0, 32, 64, 96, 300, 332
    feats = ((0, 0, LO), (1, LO, HI))

    stats3_seen, fw_loaded, f_const = sems("stats3_seen", "fw_loaded", "f_const")
    f_in, f_out = sems("f_in0", "f_in1"), sems("f_out0", "f_out1")
    a_stats, a_mom, a_var, a_rstd, a_n0 = sems("a_stats", "a_mom", "a_var", "a_rstd", "a_n0")
    a_stats2, a_mom2, a_var2, a_rstd2, a_xn = sems("a_stats2", "a_mom2", "a_var2", "a_rstd2", "a_xn")
    a_ng, a_n, a_res = sems("a_ng", "a_n", "a_res")
    a_z, a_ez, a_ez1, a_score = sems("a_z", "a_ez", "a_ez1", "a_score")
    a_zb, a_sb, a_zrow, a_srow = sems("a_zb", "a_sb", "a_zrow", "a_srow")
    a_cnt, a_rank, a_sel = sems("a_cnt", "a_rank", "a_sel")
    a_nT_ps, a_nT, a_k_ps, a_k, a_v_ps, a_v = sems("a_nT_ps", "a_nT", "a_k_ps", "a_k", "a_v_ps", "a_v")
    b_gat_ps, b_gat, b_sinv, b_pool = sems("b_gat_ps", "b_gat", "b_sinv", "b_pool")
    b_q_ps, b_q, b_qblk, b_log = sems("b_q_ps", "b_q", "b_qblk", "b_log")
    b_max, b_exp, b_inv, b_prob = sems("b_max", "b_exp", "b_inv", "b_prob")
    b_pT_ps, b_pT, b_av_ps, b_av, b_ctx = sems("b_pT_ps", "b_pT", "b_av_ps", "b_av", "b_ctx")
    b_wo_ps, b_asel, b_sca_ps, b_h, b_res = sems("b_wo_ps", "b_asel", "b_sca_ps", "b_h", "b_res")
    b_mixT, b_mix_ps, b_mixb, b_kept = sems("b_mixT", "b_mix_ps", "b_mixb", "b_kept")
    b_stats, b_mom, b_var, b_rstd = sems("b_stats", "b_mom", "b_var", "b_rstd")
    b_hn, b_hg, b_n2 = sems("b_hn", "b_hg", "b_n2")
    c_n2T_ps, c_n2T, c_down, c_out = sems("c_n2T_ps", "c_n2T", "c_down", "c_out")
    c_up, c_g = sems("c_up0", "c_up1", "c_up2"), sems("c_g0", "c_g1", "c_g2")
    mm, tr = nc.tensor.matmul, nc.tensor.transpose

    def pipeline(eng, step):
        for i in range(4):
            step(i, i % 2, [i - k >= 0 for k in range(3)])
        with eng.Fori(2, nimg // 2) as u:
            for r in range(2):
                step(u * 2 + r, r, [True] * 3)
        for i in range(nimg, nimg + 2):
            step(i, i % 2, [i - k < nimg for k in range(3)])

    with nc.Block() as block:
        LOADS = 12 + 1 + len(row) + 4 + 7

        @block.sync
        def _(sp):
            n = 0

            def load(dst, src):
                nonlocal n
                sp.dma_start(dst, src).then_inc(fw_loaded, 16)
                n += 1
            for name in ("Wq", "Wk", "Wv", "Wo", "Wm", "W1"):
                for f, a, m in feats:
                    load(W[name][f], io[name][a:a + m, :])
            load(W2, io["W2"].rearrange("(t p) n -> p t n", t=FT))
            for name in row:
                load(row[name], io[name].partition_broadcast(128))
            for name in col:
                for f, a, m in feats:
                    load(col[name][f], io[name].rearrange("(n o) -> n o", o=1)[a:a + m, :])
            load(bf1, io["bf1"])
            load(br, io["br"].partition_broadcast(128))
            load(ident, io["ident"])
            load(slots, io["slots"])
            load(before, io["before"])
            load(own, io["own"])
            load(mhalf, io["mhalf"][0:TC, 0:2])
            assert n == LOADS

            def step(i, r, on):
                if on[0]:
                    if counts(i - 1):
                        sp.wait_ge(a_res, i - 1)
                    if counts(i - 1):
                        sp.wait_ge(a_n0, i - 1)
                    src = h2[bass.ds(i * NT, NT), :].rearrange("(c p) n -> p c n", p=TC)
                    sp.dma_start(hc[r], src).then_inc(f_in[r], 16)
                if on[2]:
                    sp.wait_ge(c_out, i - 1)
                    dst = out[bass.ds((i - 2) * NT, NT), :].rearrange("(c p) n -> p c n", p=TC)
                    sp.dma_start(dst, oo[r]).then_inc(f_out[r], 16)
            pipeline(sp, step)
            for r in range(2):
                sp.wait_ge(f_out[r], 16 * (nimg // 2))

        @block.tensor
        def _(pe):
            def A_turn(i, r):
                pe.wait_ge(a_n, i + 1)
                if counts(i - 1):
                    pe.wait_ge(c_n2T, i - 1)
                for f, a, m in feats:
                    for c in range(2):
                        t = tr(psum[0:m, NTB, f * NT + c * TC:f * NT + (c + 1) * TC], nn[r][:, c, a:a + m], ident[0:TC, 0:TC])
                t.then_inc(a_nT_ps, 1)

            def A_zrow(i, r):
                pe.wait_ge(a_zb, i + 1)
                if counts(i):
                    pe.wait_ge(b_mixT, i)
                for c in range(2):
                    t = tr(psum[0:TC, RB, c * TC:(c + 1) * TC], zb[:, c, :], ident[0:TC, 0:TC])
                t.then_inc(a_zrow, 1)

            def A_srow(i, r):
                pe.wait_ge(a_sb, i + 1)
                pe.wait_ge(a_cnt, 4 * i + 4)
                for c in range(2):
                    t = tr(psum[:, RB, NT + c * TC:NT + (c + 1) * TC], sb[:, c, :], ident[0:TC, 0:TC])
                t.then_inc(a_srow, 1)

            def A_k(i, r):
                pe.wait_ge(a_nT, i + 1)
                if counts(i * 2 - 2):
                    pe.wait_ge(b_av, i * 2 - 2)
                if counts(i - 1):
                    pe.wait_ge(c_g[1], i - 1)
                for f, a, m in feats:
                    o = psum[0:m, KB, f * NT:(f + 1) * NT]
                    mm(o, W["Wk"][0][:, a:a + m], nT[r][0], start=True, stop=False)
                    t = mm(o, W["Wk"][1][:, a:a + m], nT[r][1], start=False, stop=True)
                t.then_inc(a_k_ps, 1)

            def A_v(i, r):
                if counts(i - 1):
                    pe.wait_ge(b_h, i - 1)
                for c in range(2):
                    o = psum[0:TC, VB, c * D:(c + 1) * D]
                    mm(o, nT[r][0][:, c * TC:(c + 1) * TC], W["Wv"][0], start=True, stop=False)
                    t = mm(o, nT[r][1][:, c * TC:(c + 1) * TC], W["Wv"][1], start=False, stop=True)
                t.then_inc(a_v_ps, 1)

            def B_gather(i, r):
                pe.wait_ge(a_sel, 4 * i + 4)
                pe.wait_ge(a_score, i + 1)
                if counts(i):
                    pe.wait_ge(b_asel, i)
                for (f, a, m), o in zip(feats, (GA, GB)):
                    for c in range(2):
                        mm(psum[0:m, SB, o:o + TOPK + 1], nn[r][:, c, a:a + m], sel[r][:, c, :],
                           start=(c == 0), stop=(c == 1))
                for c in range(2):
                    mm(psum[:, SB, SS:SS + 1], ones[0:TC, :], sel[r][:, c, TOPK:TOPK + 1], start=(c == 0), stop=(c == 1))
                for c in range(2):
                    t = tr(psum[0:TOPK, SB, ST + c * TC:ST + (c + 1) * TC], sel[r][:, c, 0:TOPK], ident[0:TC, 0:TC])
                t.then_inc(b_gat_ps, 1)

            def B_q(i, r):
                pe.wait_ge(b_gat, 4 * i + 4)
                pe.wait_ge(b_pool, 2 * i + 2)
                for (f, a, m), o in zip(feats, (QA, QB)):
                    for k in range(2):
                        t = mm(psum[0:m, SB, o:o + TOPK], W["Wq"][k][:, a:a + m], nsel[k], start=(k == 0), stop=(k == 1))
                t.then_inc(b_q_ps, 1)

            def B_logits(i, r):
                pe.wait_ge(b_qblk, 2 * i + 2)
                pe.wait_ge(a_k, i + 1)
                if counts(i):
                    pe.wait_ge(b_pT, i)
                for t3 in range(3):
                    k, h = (0, HQ * t3) if t3 < 2 else (1, 0)
                    o = psum[0:QT, L0 if t3 < 2 else L1, (t3 % 2) * NT:(t3 % 2 + 1) * NT]
                    t = mm(o, qblk[k][:, h:h + HQ, :], kT[r][k], start=True, stop=True)
                t.then_inc(b_log, 1)

            def B_turn(i, r):
                pe.wait_ge(b_prob, i + 1)
                for c in range(2):
                    for t3 in range(3):
                        t = tr(psum[0:TC, L0 + c, t3 * QT:(t3 + 1) * QT], pr[:, t3, c * TC:(c + 1) * TC], ident[0:QT, 0:QT])
                t.then_inc(b_pT_ps, 1)

            def B_av(i, r):
                pe.wait_ge(b_pT, i + 1)
                pe.wait_ge(a_v, i + 1)
                pe.wait_ge(a_k, min(i + 2, nimg) if isinstance(i, int) else i + 2)
                for k, (f, a, m) in enumerate(feats):
                    w_ = (8 if k == 0 else 4) * TOPK
                    for c in range(2):
                        t = mm(psum[0:m, KB, k * 8 * TOPK:k * 8 * TOPK + w_], vv[r][:, c, a:a + m],
                               pT[:, c, k * 8 * TOPK:k * 8 * TOPK + w_], start=(c == 0), stop=(c == 1))
                t.then_inc(b_av_ps, 1)

            def B_wo(i, r):
                pe.wait_ge(b_ctx, 2 * i + 2)
                for k in range(2):
                    t = mm(psum[0:TOPK, SB, 0:D], ctxT[k], W["Wo"][k], start=(k == 0), stop=(k == 1))
                t.then_inc(b_wo_ps, 1)

            def B_scatter(i, r):
                pe.wait_ge(b_asel, i + 1)
                pe.wait_ge(a_v, min(i + 2, nimg) if isinstance(i, int) else i + 2)
                for c in range(2):
                    t = mm(psum[0:TC, VB, c * D:(c + 1) * D], selT[:, c * TC:(c + 1) * TC], asel, start=True, stop=True)
                t.then_inc(b_sca_ps, 1)

            def B_mix(i, r):
                pe.wait_ge(b_mixT, i + 1)
                if counts(i):
                    pe.wait_ge(c_g[2], i)
                for c in range(2):
                    for k in range(2):
                        t = mm(psum[0:TC, UB, c * D:(c + 1) * D], mixT[k][:, c * TC:(c + 1) * TC], W["Wm"][k],
                               start=(k == 0), stop=(k == 1))
                t.then_inc(b_mix_ps, 1)

            def C_turn(i, r):
                pe.wait_ge(b_n2, i + 1)
                if counts(i):
                    pe.wait_ge(c_out, i)
                for f, a, m in feats:
                    for c in range(2):
                        t = tr(psum[0:m, NTB, f * NT + c * TC:f * NT + (c + 1) * TC], n2[r][:, c, a:a + m], ident[0:TC, 0:TC])
                t.then_inc(c_n2T_ps, 1)

            def C_up(i, r, n):
                pe.wait_ge(c_n2T, i + 1)
                if n == 0:
                    pe.wait_ge(b_mixb, i + 1)
                if n == 1:
                    pe.wait_ge(b_av, 2 * i + 2)
                if n == 2:
                    pe.wait_ge(c_g[0], i + 1)
                for e in range(2):
                    o = psum[:, (UB, KB, UB)[n], e * NT:(e + 1) * NT]
                    cols = slice((2 * n + e) * 128, (2 * n + e + 1) * 128)
                    mm(o, W["W1"][0][:, cols], n2T[0], start=True, stop=False)
                    t = mm(o, W["W1"][1][:, cols], n2T[1], start=False, stop=True)
                t.then_inc(c_up[n], 1)

            def C_down(i, r, c, ts):
                pe.wait_ge(c_g[2], i + 1)
                pe.wait_ge(c_g[1], i + 1)
                pe.wait_ge(a_nT, min(i + 3, nimg) if isinstance(i, int) else i + 3)
                for t3 in ts:
                    t = mm(psum[0:TC, NTB, c * D:(c + 1) * D], gT[:, t3, c * TC:(c + 1) * TC], W2[:, t3, :],
                           start=(t3 == 0), stop=(t3 == FT - 1))
                if c == 1 and ts[-1] == FT - 1:
                    t.then_inc(c_down, 1)

            def step(i, r, on):
                a, b, c = on
                q = 1 - r
                if c: C_turn(i - 2, r)
                if b: B_gather(i - 1, q)
                if c: C_up(i - 2, r, 0)
                if b: B_q(i - 1, q)
                if c: C_up(i - 2, r, 1)
                if b: B_logits(i - 1, q)
                if c: C_up(i - 2, r, 2)
                if a: A_turn(i, r)
                if a: A_k(i, r)
                if b: B_mix(i - 1, q)
                if b: B_turn(i - 1, q)
                if a: A_zrow(i, r)
                if a: A_v(i, r)
                if c: C_down(i - 2, r, 0, range(0, 3))
                if b: B_av(i - 1, q)
                if c: C_down(i - 2, r, 0, range(3, FT))
                if b: B_wo(i - 1, q)
                if c: C_down(i - 2, r, 1, range(0, FT))
                if b: B_scatter(i - 1, q)
                if a: A_srow(i, r)
            pe.wait_ge(fw_loaded, 16 * LOADS)
            pe.wait_ge(f_const, 2)
            pipeline(pe, step)

        @block.scalar
        def _(act):
            sa, cp = nc.scalar.activation, nc.scalar.copy

            def C_n2T(i):
                act.wait_ge(c_n2T_ps, i + 1)
                cp(n2T[0], psum[:, NTB, 0:NT])
                cp(n2T[1], psum[0:HI, NTB, NT:2 * NT]).then_inc(c_n2T, 1)

            def C_gelu(i, n):
                act.wait_ge(c_up[n], i + 1)
                if counts(i):
                    act.wait_ge(c_down, i)
                for e in range(2):
                    t = 2 * n + e
                    g = sa(gT[:, t, :], psum[:, (UB, KB, UB)[n], e * NT:(e + 1) * NT], ACT.Gelu, bias=bf1[:, t:t + 1])
                g.then_inc(c_g[n], 1)

            def A_nT(i, r):
                act.wait_ge(a_nT_ps, i + 1)
                if counts(i - 1):
                    act.wait_ge(b_mixT, i - 1)
                cp(nT[r][0], psum[:, NTB, 0:NT])
                cp(nT[r][1], psum[0:HI, NTB, NT:2 * NT]).then_inc(a_nT, 1)

            def A_k(i, r):
                act.wait_ge(a_k_ps, i + 1)
                for f, a, m in feats:
                    t = sa(kT[r][f], psum[0:m, KB, f * NT:(f + 1) * NT], ACT.Identity, bias=col["bk"][f])
                t.then_inc(a_k, 1)

            def A_ez(i, r):
                act.wait_ge(a_z, i + 1)
                if counts(i):
                    act.wait_ge(a_ez1, i)
                sa(ez, z[r], ACT.Exp, bias=nbr[0:TC], scale=-1.0).then_inc(a_ez, 1)

            def B_exp(i):
                act.wait_ge(b_max, 2 * i + 2)
                if counts(i):
                    act.wait_ge(b_pT_ps, i)
                for t in range(3):
                    o = psum[0:QT, L0 if t < 2 else L1, (t % 2) * NT:(t % 2 + 1) * NT]
                    e = sa(pr[:, t, :], o, ACT.Exp, bias=nmax[:, t:t + 1], accum_out=esum[:, t:t + 1])
                e.then_inc(b_exp, 1)

            def B_pT(i):
                act.wait_ge(b_pT_ps, i + 1)
                cp(pT[:, 0, :], psum[0:TC, L0, 0:3 * QT])
                cp(pT[:, 1, :], psum[0:TC, L1, 0:3 * QT]).then_inc(b_pT, 1)

            def step(i, r, on):
                a, b, c = on
                if c: C_n2T(i - 2)
                for n in range(3):
                    if c: C_gelu(i - 2, n)
                if b: B_exp(i - 1)
                if a: A_nT(i, r)
                if a: A_k(i, r)
                if a: A_ez(i, r)
                if b: B_pT(i - 1)
            act.wait_ge(fw_loaded, 16 * LOADS)
            act.wait_ge(f_const, 2)
            pipeline(act, step)

        def rowc(name):
            return row[name][0:TC].rearrange("p (o n) -> p o n", o=1).broadcast_to([TC, 2, D])

        @block.gpsimd
        def _(pool):
            g = nc.gpsimd

            def A_rstd(i):
                pool.wait_ge(a_var, i + 1)
                g.tensor_tensor(rs[0], ve[0], mhalf, ALU.pow).then_inc(a_rstd, 1)

            def A_res(i, r):
                pool.wait_ge(f_in[r], (i * 8 + (16 - 8 * r)))
                if counts(i - 1):
                    pool.wait_ge(b_res, i - 1)
                g.tensor_tensor(res[r], hc[r], rowc("bf2"), ALU.add).then_inc(a_res, 1)

            def A_rstd2(i):
                pool.wait_ge(a_var2, i + 1)
                g.tensor_tensor(rs[1], ve[1], mhalf, ALU.pow).then_inc(a_rstd2, 1)

            def A_affine(i, r):
                pool.wait_ge(a_xn, i + 1)
                g.tensor_tensor(na[r], xn[r], rowc("g1"), ALU.mult).then_inc(a_ng, 1)
                pool.wait_ge(a_ng, i + 1)
                if counts(i - 1):
                    pool.wait_ge(b_gat_ps, i - 1)
                g.tensor_tensor(nn[r], na[r], rowc("b1"), ALU.add).then_inc(a_n, 1)

            def A_zb(i, r):
                pool.wait_ge(f_const, 2)
                pool.wait_ge(a_z, i + 1)
                if counts(i):
                    pool.wait_ge(a_zrow, i)
                g.tensor_copy(zb, z[r].rearrange("p (c o) -> p c o", o=1).broadcast_to([TC, 2, TC])).then_inc(a_zb, 1)

            def A_sb(i, r):
                pool.wait_ge(f_const, 2)
                pool.wait_ge(a_score, i + 1)
                if counts(i):
                    pool.wait_ge(a_srow, i)
                g.tensor_copy(sb, sel[r][:, :, TOPK:TOPK + 1].broadcast_to([TC, 2, 128])).then_inc(a_sb, 1)

            def B_prob(i):
                pool.wait_ge(b_inv, i + 1)
                g.tensor_tensor(pr, pr, einv.rearrange("p (t o) -> p t o", o=1).broadcast_to([QT, 3, NT]),
                                ALU.mult).then_inc(b_prob, 1)

            def B_res(i, r):
                pool.wait_ge(b_h, i + 1)
                pool.wait_ge(a_res, i + 1)
                if counts(i - 1):
                    pool.wait_ge(c_out, i - 1)
                g.tensor_tensor(rb[r], res[r], hh[r], ALU.add).then_inc(b_res, 1)

            def B_rstd(i):
                pool.wait_ge(b_var, i + 1)
                g.tensor_tensor(rs2, ve2, mhalf, ALU.pow).then_inc(b_rstd, 1)

            def B_affine(i, r):
                pool.wait_ge(b_hn, i + 1)
                g.tensor_tensor(hg[r], hn[r], rowc("g2"), ALU.mult).then_inc(b_hg, 1)
                pool.wait_ge(b_hg, i + 1)
                if counts(i - 1):
                    pool.wait_ge(c_n2T_ps, i - 1)
                g.tensor_tensor(n2[r], hg[r], rowc("b2"), ALU.add).then_inc(b_n2, 1)

            def step(i, r, on):
                a, b, c = on
                q = 1 - r
                if a: A_rstd(i)
                if a: A_res(i, r)
                if a: A_rstd2(i)
                if a: A_affine(i, r)
                if b: B_prob(i - 1)
                if a: A_zb(i, r)
                if a: A_sb(i, r)
                if b: B_rstd(i - 1)
                if b: B_affine(i - 1, q)
                if b: B_res(i - 1, q)
            pool.wait_ge(fw_loaded, 16 * LOADS)
            pipeline(pool, step)

        @block.vector
        def _(dve):
            v = nc.vector

            def norm(src, to, st, mv, ve, rs, names, i):
                stats, mom, var, rstd, okay = names

                def first():
                    for c in range(2):
                        v.bn_stats(st[:, c], src[:, c]).then_inc(stats, 1)
                    dve.wait_ge(stats, 2 * i + 2)
                    dve.sem_inc(stats3_seen, 1)
                    for c in range(2):
                        v.bn_aggr(mv[:, c], st[:, c]).then_inc(mom, 1)
                    dve.wait_ge(mom, 2 * i + 2)
                    v.tensor_scalar(ve, mv[:, :, 1], EPS, None, ALU.add).then_inc(var, 1)

                def then():
                    dve.wait_ge(rstd, i + 1)
                    for c in range(2):
                        t = v.tensor_scalar(to[:, c], src[:, c], mv[:, c, 0:1], rs[:, c:c + 1], ALU.subtract, ALU.mult)
                    t.then_inc(okay, 1)
                return first, then

            def A_z(i, r):
                dve.wait_ge(a_n, i + 1)
                if counts(i - 1):
                    dve.wait_ge(a_ez, i - 1)
                if counts(i - 1):
                    dve.wait_ge(a_zb, i - 1)
                if counts(4 * i):
                    dve.wait_ge(a_cnt, 4 * i)
                for c in range(2):
                    t = v.tensor_tensor_reduce(out=junk[:, c * D:(c + 1) * D], in0=nn[r][:, c], in1=row["Wr"][0:TC], scale=1.0,
                                               scalar=0.0, op0=ALU.mult, op1=ALU.add, accum_out=z[r][:, c:c + 1])
                t.then_inc(a_z, 1)

            def A_rank(i, r):
                dve.wait_ge(a_zrow, i + 1)
                zr = psum[0:TC, RB, 0:NT]
                for c in range(2):
                    v.tensor_scalar(cmp[c], zr, z[r][:, c:c + 1], None, ALU.is_lt, ALU.add,
                                    accum_out=lt[:, c:c + 1]).then_inc(a_cnt, 1)
                    v.scalar_tensor_tensor(out=cmp[2 + c], in0=zr, scalar=z[r][:, c:c + 1], in1=before[:, c], op0=ALU.is_equal,
                                           op1=ALU.mult, accum_out=eq[:, c:c + 1]).then_inc(a_cnt, 1)
                dve.wait_ge(a_cnt, 4 * i + 4)
                v.tensor_tensor(rank, lt, eq, ALU.add).then_inc(a_rank, 1)
                dve.wait_ge(a_rank, i + 1)
                for c in range(2):
                    v.tensor_scalar(sel[r][:, c, 0:TOPK], slots, rank[:, c:c + 1], None, ALU.is_equal).then_inc(a_sel, 1)
                    v.tensor_scalar(keep[r][:, c:c + 1], rank[:, c:c + 1], float(TOPK), None, ALU.is_ge).then_inc(a_sel, 1)

            def A_score(i, r):
                dve.wait_ge(a_ez, i + 1)
                v.tensor_scalar(ez1, ez, 1.0, None, ALU.add).then_inc(a_ez1, 1)
                dve.wait_ge(a_ez1, i + 1)
                v.reciprocal(sel[r][:, :, TOPK], ez1).then_inc(a_score, 1)

            def A_v(i, r):
                dve.wait_ge(a_v_ps, i + 1)
                v.tensor_tensor(vv[r], psum[0:TC, VB, 0:2 * D].rearrange("p (c n) -> p c n", c=2), rowc("bv"),
                                ALU.add).then_inc(a_v, 1)

            def B_gat(i, r):
                dve.wait_ge(b_gat_ps, i + 1)
                v.tensor_scalar(ssum, psum[:, SB, SS:SS + 1], 1e-6, None, ALU.add).then_inc(b_gat, 1)
                v.tensor_copy(nsel[0], psum[:, SB, GA:GA + TOPK]).then_inc(b_gat, 1)
                v.tensor_copy(nsel[1], psum[0:HI, SB, GB:GB + TOPK]).then_inc(b_gat, 1)
                v.tensor_copy(selT, psum[0:TOPK, SB, ST:ST + NT]).then_inc(b_gat, 1)
                dve.wait_ge(b_gat, 4 * i + 4)
                v.reciprocal(sinv, ssum).then_inc(b_sinv, 1)
                dve.wait_ge(b_sinv, i + 1)
                for (f, a, m), o in zip(feats, (GA, GB)):
                    v.tensor_tensor(pooled[f], psum[0:m, SB, o + TOPK:o + TOPK + 1], sinv[0:m], ALU.mult).then_inc(b_pool, 1)

            def B_q(i):
                dve.wait_ge(b_q_ps, i + 1)
                for (f, a, m), o in zip(feats, (QA, QB)):
                    v.tensor_scalar(qs[f], psum[0:m, SB, o:o + TOPK], col["bq"][f], DH3 ** -0.5, ALU.add,
                                    ALU.mult).then_inc(b_q, 1)
                dve.wait_ge(b_q, 2 * i + 2)
                for k, nh in ((0, 8), (1, 4)):
                    m = qs[k].shape[0]
                    v.tensor_tensor(qblk[k], qs[k].rearrange("p (o j) -> p o j", o=1).broadcast_to([m, nh, TOPK]),
                                    own[0:m, 0:nh].rearrange("p (h o) -> p h o", o=1).broadcast_to([m, nh, TOPK]),
                                    ALU.mult).then_inc(b_qblk, 1)

            def B_max(i):
                dve.wait_ge(b_log, i + 1)
                v.tensor_reduce(nmax[:, 0:2], psum[0:QT, L0, 0:2 * NT].rearrange("p (t n) -> p t n", t=2), AX.X, ALU.max,
                                negate=True).then_inc(b_max, 1)
                v.tensor_reduce(nmax[:, 2:3], psum[0:QT, L1, 0:NT], AX.X, ALU.max, negate=True).then_inc(b_max, 1)

            def B_inv(i):
                dve.wait_ge(b_exp, i + 1)
                v.reciprocal(einv, esum).then_inc(b_inv, 1)

            def B_mixT(i, r):
                dve.wait_ge(a_srow, i + 1)
                dve.wait_ge(a_nT, i + 1)
                dve.wait_ge(b_pool, 2 * i + 2)
                if counts(i):
                    dve.wait_ge(b_mix_ps, i)
                for f, a, m in feats:
                    t = v.scalar_tensor_tensor(out=mixT[f], in0=psum[0:m, RB, NT:2 * NT], scalar=pooled[f], in1=nT[r][f],
                                               op0=ALU.mult, op1=ALU.add)
                t.then_inc(b_mixT, 1)

            def B_mixb(i):
                dve.wait_ge(b_mix_ps, i + 1)
                v.tensor_tensor(mixb, psum[0:TC, UB, 0:2 * D].rearrange("p (c n) -> p c n", c=2), rowc("bm"),
                                ALU.add).then_inc(b_mixb, 1)

            def B_kept(i, r):
                dve.wait_ge(b_mixb, i + 1)
                for c in range(2):
                    t = v.scalar_tensor_tensor(out=kept_mix[:, c], in0=mixb[:, c], scalar=keep[r][:, c:c + 1], in1=n0[r][:, c],
                                               op0=ALU.mult, op1=ALU.add)
                t.then_inc(b_kept, 1)

            def B_av(i):
                dve.wait_ge(b_av_ps, i + 1)
                for k, nh in ((0, 8), (1, 4)):
                    m = qs[k].shape[0]
                    o = psum[0:m, KB, k * 8 * TOPK:k * 8 * TOPK + nh * TOPK].rearrange("p (h j) -> p h j", h=nh)
                    v.tensor_tensor(cm[k], o, own[0:m, 0:nh].rearrange("p (h o) -> p h o", o=1).broadcast_to([m, nh, TOPK]),
                                    ALU.mult).then_inc(b_av, 1)
                dve.wait_ge(b_av, 2 * i + 2)
                for k in range(2):
                    v.tensor_reduce(ctxT[k], cm[k].rearrange("p h j -> p j h"), AX.X, ALU.add).then_inc(b_ctx, 1)

            def B_asel(i):
                dve.wait_ge(b_wo_ps, i + 1)
                v.tensor_tensor(asel, psum[0:TOPK, SB, 0:D], row["bo"][0:TOPK], ALU.add).then_inc(b_asel, 1)

            def B_h(i, r):
                dve.wait_ge(b_sca_ps, i + 1)
                dve.wait_ge(b_kept, i + 1)
                if counts(i - 1):
                    dve.wait_ge(b_res, i - 1)
                v.tensor_tensor(hh[r], psum[0:TC, VB, 0:2 * D].rearrange("p (c n) -> p c n", c=2), kept_mix,
                                ALU.add).then_inc(b_h, 1)

            def C_out(i, r):
                dve.wait_ge(c_down, i + 1)
                dve.wait_ge(b_res, i + 1)
                if counts(i * 8 - 8 * r):
                    dve.wait_ge(f_out[r], i * 8 - 8 * r)
                v.tensor_tensor(oo[r], psum[0:TC, NTB, 0:2 * D].rearrange("p (c n) -> p c n", c=2), rb[r],
                                ALU.add).then_inc(c_out, 1)

            def step(i, r, on):
                a, b, c = on
                q = 1 - r
                if a:
                    dve.wait_ge(f_in[r], i * 8 + (16 - 8 * r))
                    f1, t1 = norm(hc[r], n0[r], st[0], mv[0], ve[0], rs[0], (a_stats, a_mom, a_var, a_rstd, a_n0), i)
                    f2, t2 = norm(n0[r], xn[r], st[1], mv[1], ve[1], rs[1], (a_stats2, a_mom2, a_var2, a_rstd2, a_xn), i)
                    f1()
                if b: B_gat(i - 1, q)
                if a:
                    if counts(i - 1):
                        dve.wait_ge(b_kept, i - 1)
                    t1()
                if b: B_q(i - 1)
                if a:
                    dve.wait_ge(a_n0, i + 1)
                    f2()
                if b: B_max(i - 1)
                if a:
                    t2()
                if b: B_mixT(i - 1, q)
                if b: B_inv(i - 1)
                if a: A_z(i, r)
                if b: B_mixb(i - 1)
                if b: B_kept(i - 1, q)
                if a: A_rank(i, r)
                if a: A_v(i, r)
                if a: A_score(i, r)
                if b: B_av(i - 1)
                if b: B_asel(i - 1)
                if c: C_out(i - 2, r)
                if b:
                    B_h(i - 1, q)
                    f3, t3 = norm(hh[q], hn[q], st3, mv3, ve2, rs2, (b_stats, b_mom, b_var, b_rstd, b_hn), i - 1)
                    dve.wait_ge(b_h, i)
                    f3()
                    t3()
            dve.wait_ge(fw_loaded, 16 * LOADS)
            v.memset(ones, 1.0).then_inc(f_const, 1)
            v.tensor_scalar(nbr, br, -1.0, None, ALU.mult).then_inc(f_const, 1)
            pipeline(dve, step)


def kept(nc, ctx):
    sb = lambda n, cols: ctx.enter_context(nc.sbuf_tensor("sb_" + n, [128, cols], F32))
    w = {}
    w["qkv_lo"], w["qkv_hi"] = sb("qkv_lo", 3 * H1 * DH1)[:], sb("qkv_hi", 3 * H1 * DH1)[0:HI + 1]
    w["xT_lo"], w["xT_hi"] = sb("xT_lo", GT)[:], sb("xT_hi", GT)[0:HI + 1]
    w["proj"] = sb("proj", 6 * D)[:].rearrange("p (h n) -> p h n", h=6)
    w["projb_lo"], w["projb_hi"] = sb("projb_lo", 1)[:], sb("projb_hi", 1)[0:HI]
    w["ident"] = sb("ident", 128)[:]
    w["mhalf"] = sb("mhalf", 8)[:]
    w["kx"] = sb("kx", H1 * NT)[:].rearrange("p (h n) -> p h n", h=H1)
    w["vx"] = sb("vx", 2 * H1 * KQ)[0:TC].rearrange("p (c h d) -> p c h d", c=2, h=H1)
    for hs, nh in (("a", 8), ("b", 4)):
        for f, m in enumerate((LO, HI)):
            n = f"tw_{hs}{f}"
            w[n] = sb(n, 2 * nh * TAB)[0:m].rearrange("p (s i h) -> p s i h", s=2, h=nh)
            n = f"tz_{hs}{f}"
            w[n] = sb(n, 2 * nh * SLOT)[0:m].rearrange("p (s i h) -> p s i h", s=2, h=nh)
    w["pv_a"] = sb("pv_a", (ROWS + SIDE + 2) * D)[:].rearrange("p (g n) -> p g n", n=D)
    w["pv_b"] = sb("pv_b", (ROWS + 1) * D)[:].rearrange("p (g n) -> p g n", n=D)
    return w


def vit_block(nc, io, out, nimg):
    hA = nc.dram_tensor("h_by_class", [nimg * NT, D], F32).ap()
    h2 = nc.dram_tensor("h_attended", [nimg * NT, D], F32).ap()
    pv_rows = nc.dram_tensor("table_rows", [2, TAB, H1 * D], F32).ap()
    with ExitStack() as ctx:
        w = kept(nc, ctx)
        arena = ctx.enter_context(nc.sbuf_tensor("arena", [128, 29000], F32))[:]
        psum = ctx.enter_context(nc.psum_tensor("banks", [128, 8, 512], F32))
        tokenizer(nc, ctx, io, arena, psum, hA, nimg)
        attention_weights(nc, ctx, io, w, arena, psum, pv_rows)
        attention(nc, ctx, io, w, arena, psum, hA, h2, nimg)
        feed_forward(nc, ctx, io, arena, psum, h2, out, nimg)


def lay_out(x, tok_W, tok_b, qkv_w, proj_w, proj_b, tabs, ffn):
    import numpy as np
    n = x.shape[0]
    p = x.reshape(n, GP, P, GP, 2, P // 2, 3).transpose(0, 1, 3, 4, 2, 5, 6).reshape(n, GP, GP, PIX)

    def chunks(a, m):
        return a.reshape(-1, m, KT, 128).transpose(0, 3, 2, 1)
    e = GP - 1
    io = dict(
        xI=chunks(p[:, 1:e, 1:e].reshape(-1, PIX), 128).reshape(n // 8, 9, 128, KT, 128),
        xE=np.stack([chunks(a.reshape(-1, PIX), 96) for a in (p[:, 0, 1:e], p[:, e, 1:e], p[:, 1:e, 0], p[:, 1:e, e])]),
        xC=np.stack([chunks(a, n)[0] for a in (p[:, 0, 0], p[:, 0, e], p[:, e, 0], p[:, e, e])]),
        tokW=tok_W.reshape(P, 2, P // 2, 5, 3, D).transpose(3, 1, 0, 2, 4, 5).reshape(5, KT, 128, D).transpose(2, 0, 1, 3),
        tokb=tok_b)
    Q = H1 * DH1
    t = np.arange(NT)
    onehot = np.zeros((2 * SLOT, NT), np.float32)
    onehot[(t[1:] - 1) // SIDE, t[1:]] = 1
    onehot[SLOT + (t[1:] - 1) % SIDE, t[1:]] = 1
    first = np.zeros((1, GT), np.float32)
    first[0, ::NT] = 1
    side_by_side = lambda a, b: np.concatenate([np.pad(u.T, ((0, 0), (0, 1))) for u in (a, b)], 1)
    io.update(
        wq_d=qkv_w[:Q].reshape(H1, DH1, D).transpose(1, 0, 2).reshape(DH1, H1 * D),
        proj_d=proj_w.reshape(D, H1, DH1).transpose(2, 1, 0).reshape(DH1, H1 * D),
        tabk=side_by_side(*tabs[:2]), tabv=side_by_side(*tabs[2:]),
        t0=np.concatenate([u[0] for u in tabs]).reshape(1, 4 * DH1),
        qkvT=qkv_w.T, proj_p=proj_w.T.reshape(6, 128, D).transpose(1, 0, 2), projb=proj_b.reshape(D, 1),
        onehot=onehot, onehotT=onehot.T.reshape(2, TC, 2 * SLOT), first=first,
        ident=np.eye(128, dtype=np.float32), mhalf=np.full((128, 8), -0.5, np.float32),
        slots=np.tile(np.arange(TOPK, dtype=np.float32), (TC, 1)),
        before=(t[None] < t[:, None]).astype(np.float32).reshape(2, TC, NT).transpose(1, 0, 2),
        own=(np.arange(128)[:, None] // DH3 == np.arange(8)[None]).astype(np.float32))
    io.update(ffn)
    io["bf1"] = ffn["bf1"].reshape(FT, 128).T
    io["br"] = ffn["br"].reshape(1)
    return {k: np.ascontiguousarray(a) for k, a in io.items()}


def kernel(x, L0_tok_W, L0_tok_b, L0_attn_qkv_w, L0_attn_proj_w, L0_attn_proj_b, L0_attn_tab_kv, L0_attn_tab_kh,
           L0_attn_tab_vv, L0_attn_tab_vh, **ffn):
    import numpy as np
    import concourse.bacc as bacc
    from concourse.bass_utils import run_bass_kernel_spmd

    nimg = x.shape[0]
    ffn = {k.removeprefix("L0_ffn_"): np.asarray(a) for k, a in ffn.items()}
    arrays = lay_out(*(np.asarray(a) for a in (x, L0_tok_W, L0_tok_b, L0_attn_qkv_w, L0_attn_proj_w, L0_attn_proj_b)),
                     [np.asarray(a) for a in (L0_attn_tab_kv, L0_attn_tab_kh, L0_attn_tab_vv, L0_attn_tab_vh)], ffn)
    nc = bacc.Bacc("TRN2", target_bir_lowering=False, num_devices=1)
    io = {k: nc.dram_tensor("in_" + k, a.shape, F32, kind="ExternalInput").ap() for k, a in arrays.items()}
    out = nc.dram_tensor("out", [nimg * NT, D], F32, kind="ExternalOutput").ap()
    vit_block(nc, io, out, nimg)
    r = run_bass_kernel_spmd(nc, [{"in_" + k: a for k, a in arrays.items()}], core_ids=[0])
    return r.results[0]["out"].reshape(nimg, NT, D)
```

```python
from contextlib import ExitStack

import concourse.bass as bass
from concourse import mybir

F32 = mybir.dt.float32
ALU = mybir.AluOpType
ACT = mybir.ActivationFunctionType
AX = mybir.AxisListType
EPS = 1e-5

D = 192
LO, HI = 128, 64
IMG, P = 224, 16
GP = IMG // P
NT = GP * GP
TC = NT // 2
PIX = P * P * 3
KT = PIX // 128
H1, DH1 = 12, 64
SIDE = 13
ROWS = (NT - 1) // SIDE
IDX0 = 15
TAB = 31
SLOT = 16
KQ = DH1 + 2 * SLOT
GROUP = 8
GT = GROUP * NT
CHUNKS = 2 * GROUP


def counts(n):
    return not (isinstance(n, int) and n <= 0)


def tokenizer(nc, ctx, io, arena, psum, hA, nimg):
    OCT = nimg // 8
    NIN = 9
    off = [0]

    def take(cols):
        a = arena[:, off[0]:off[0] + cols]
        off[0] += cols
        return a

    wall = take(5 * KT * D).rearrange("p (v t n) -> p v t n", v=5, t=KT)
    CLS = ["mid", "top", "bot", "left", "right", "tl", "tr", "bl", "br"]
    wcls = {c: take(KT * D).rearrange("p (t n) -> p t n", t=KT) for c in CLS}
    xin = [take(KT * 128).rearrange("p (t m) -> p t m", t=KT) for _ in range(4)]
    hout = [take(D) for _ in range(4)]
    bias = take(D)
    sem = lambda n: ctx.enter_context(nc.semaphore(n))
    w_loaded, bias_loaded = sem("w_loaded"), sem("tokb_loaded")
    x_loaded = [sem(f"x_loaded{i}") for i in range(4)]
    tok_seen = sem("tok_seen")
    w_summed, tok_psum, tok_done = sem("w_summed"), sem("tok_psum"), sem("tok_done")
    h_stored = [sem(f"h_stored{i}") for i in range(4)]
    wpart = sem("w_partial")

    def octet():
        return [("mid", k, 128) for k in range(NIN)] + [(c, 0, 96) for c in CLS[1:5]]
    NCH = len(octet())
    corners = [(c, 0, nimg) for c in CLS[5:]]

    def x_src(cls, k, o):
        if cls == "mid":
            return io["xI"][o, k]
        if cls in CLS[1:5]:
            return io["xE"][CLS.index(cls) - 1, o]
        return io["xC"][CLS.index(cls) - 5]

    RE = nimg * 144
    RC = RE + 4 * nimg * 12

    def h_dst(cls, k, o, m):
        if cls == "mid":
            return hA[bass.ds(o * (NIN * 128) + k * 128, m), :]
        if cls in CLS[1:5]:
            return hA[bass.ds(o * 96 + RE + (CLS.index(cls) - 1) * nimg * 12, m), :]
        r = RC + (CLS.index(cls) - 5) * nimg
        return hA[r:r + m, :]

    USE = [len([j for j in range(NCH) if j % 4 == s]) for s in range(4)]

    def uses(j, o):
        return o * USE[j % 4] + j // 4

    with nc.Block() as block:
        @block.sync
        def _(sp):
            sp.dma_start(wall, io["tokW"]).then_inc(w_loaded, 16)
            sp.dma_start(bias, io["tokb"].partition_broadcast(128)).then_inc(bias_loaded, 16)

            def load(j, o, item):
                cls, k, m = item
                sp.dma_start(xin[j % 4][:, :, 0:m], x_src(cls, k, o)).then_inc(x_loaded[j % 4], 16)
            for j in range(4):
                load(j, 0, octet()[j])

            def body(o, following):
                for j in range(4, NCH):
                    sp.wait_ge(tok_psum, o * NCH + j - 3)
                    load(j, o, octet()[j])
                for j in (1, 2, 3, 0):
                    last = max(i for i in range(NCH) if i % 4 == j)
                    sp.wait_ge(tok_psum, o * NCH + last + 1)
                    sp.sem_inc(tok_seen, 1)
                    load(j, o + 1, following[j])
            body(0, octet())
            with sp.Fori(1, OCT - 1) as o:
                body(o, octet())
            body(OCT - 1, corners)

        @block.tensor
        def _(pe):
            pe.wait_ge(w_summed, 1)

            def product(j, o, item):
                cls, k, m = item
                if cls == "top" and isinstance(o, int):
                    pe.wait_ge(w_summed, 2)
                pe.wait_ge(x_loaded[j % 4], 16 * (uses(j, o) + 1))
                if counts(o * NCH + j - (3 if j >= 4 else j)):
                    pe.wait_ge(tok_done, o * NCH + j - (3 if j >= 4 else j))
                for t in range(KT):
                    mm = nc.tensor.matmul(psum[0:m, j % 4, 0:D], xin[j % 4][:, t, 0:m], wcls[cls][:, t, :],
                                          start=(t == 0), stop=(t == KT - 1))
                mm.then_inc(tok_psum, 1)
            for j, item in enumerate(octet()):
                product(j, 0, item)
            with pe.Fori(1, OCT) as o:
                for j, item in enumerate(octet()):
                    product(j, o, item)
            for j, item in enumerate(corners):
                product(j, OCT, item)

        @block.vector
        def _(dve):
            dve.wait_ge(w_loaded, 16)
            v = nc.vector
            mid = wcls["mid"]
            v.tensor_tensor(mid, wall[:, 0], wall[:, 1], ALU.add).then_inc(wpart, 1)
            for n in range(2, 5):
                dve.wait_ge(wpart, n - 1)
                ins = v.tensor_tensor(mid, mid, wall[:, n], ALU.add).then_inc(wpart, 1)
            dve.wait_ge(wpart, 4)
            dve.sem_inc(w_summed, 1)
            n = 4
            first = {}
            for step in range(3):
                for cls in CLS[1:]:
                    top, bot = cls in ("top", "tl", "tr"), cls in ("bot", "bl", "br")
                    left, right = cls in ("left", "tl", "bl"), cls in ("right", "tr", "br")
                    for jh in range(2):
                        for ih in range(2):
                            parts = {1, 2, 3, 4}
                            if top and ih == 0:
                                parts -= {2, 4}
                            if bot and ih == 1:
                                parts -= {1, 3}
                            if left and jh == 0:
                                parts -= {3, 4}
                            if right and jh == 1:
                                parts -= {1, 2}
                            whole = (slice(0, 128), 3 * jh + 2 * ih)
                            half = (slice(64 * ih, 64 * ih + 64), 3 * jh + 1)
                            for ps, t in (whole, half):
                                dst = wcls[cls][ps, t, :]
                                if step == 0:
                                    if len(parts) == 4:
                                        v.tensor_copy(dst, mid[ps, t, :]).then_inc(wpart, 1)
                                    else:
                                        v.tensor_tensor(dst, wall[ps, 0, t, :], wall[ps, min(parts), t, :],
                                                        ALU.add).then_inc(wpart, 1)
                                    n += 1
                                elif step == 1 and len(parts) == 2:
                                    v.tensor_tensor(dst, dst, wall[ps, max(parts), t, :], ALU.add).then_inc(wpart, 1)
                                    n += 1
                dve.wait_ge(wpart, n)
            dve.sem_inc(w_summed, 1)
            dve.wait_ge(bias_loaded, 16)

            def finish(j, o, item):
                m = item[2]
                dve.wait_ge(tok_psum, o * NCH + j + 1)
                if counts(16 * uses(j, o)):
                    dve.wait_ge(h_stored[j % 4], 16 * uses(j, o))
                v.tensor_tensor(hout[j % 4][0:m], psum[0:m, j % 4, 0:D], bias[0:m], ALU.add).then_inc(tok_done, 1)
            for j, item in enumerate(octet()):
                finish(j, 0, item)
            with dve.Fori(1, OCT) as o:
                for j, item in enumerate(octet()):
                    finish(j, o, item)
            for j, item in enumerate(corners):
                finish(j, OCT, item)

        @block.scalar
        def _(act):
            def store(j, o, item):
                act.wait_ge(tok_done, o * NCH + j + 1)
                act.dma_start(h_dst(*item[:2], o, item[2]), hout[j % 4][0:item[2]]).then_inc(h_stored[j % 4], 16)
            for j, item in enumerate(octet()):
                store(j, 0, item)
            with act.Fori(1, OCT) as o:
                for j, item in enumerate(octet()):
                    store(j, o, item)
            for j, item in enumerate(corners):
                store(j, OCT, item)
            for s in range(4):
                act.wait_ge(h_stored[s], 16 * (OCT * USE[s] + 1))


def x_transposed(take):
    return take(GT), take(GT)[0:HI + 1]


def attention_weights(nc, ctx, io, w, arena, psum, pv_rows):
    sem = lambda n: ctx.enter_context(nc.semaphore(n))
    loaded, built, tk_psum, tk_done = sem("aw_loaded"), sem("aw_built"), sem("tabk_psum"), sem("tabk_done")
    tv_psum, tv_done, pv_stored, pv_loaded = sem("tabv_psum"), sem("tabv_done"), sem("pv_stored"), sem("pv_loaded")
    pairs_up = sem("pairs_up")
    off = [0]

    def take(cols):
        a = arena[:, off[0]:off[0] + cols]
        off[0] += cols
        return a
    xT_lo, xT_hi = x_transposed(take)
    wq_d = take(H1 * D)[0:DH1]
    proj_d = take(H1 * D)[0:DH1]
    tabk, tabv = take(2 * TAB)[0:DH1], take(2 * TAB)[0:DH1]
    pv_sb = take(H1 * D)[0:2 * TAB]
    t0 = take(4 * DH1)[64:65]
    n_loads = 13 + 3 * H1

    with nc.Block() as block:
        @block.sync
        def _(sp):
            n = 0
            for dst, src in ((wq_d, io["wq_d"]), (proj_d, io["proj_d"]), (tabk, io["tabk"]), (tabv, io["tabv"]),
                             (w["qkv_lo"][:, :], io["qkvT"][0:LO, :]), (w["qkv_hi"][0:HI, :], io["qkvT"][LO:D, :]),
                             (w["proj"], io["proj_p"]), (w["projb_lo"], io["projb"][0:LO, :]),
                             (w["projb_hi"], io["projb"][LO:D, :]), (w["ident"], io["ident"]),
                             (t0, io["t0"]), (xT_hi[HI:HI + 1, :], io["first"]),
                             (w["mhalf"], io["mhalf"])):
                sp.dma_start(dst, src).then_inc(loaded, 16)
                n += 1
            for h in range(H1):
                sp.dma_start(w["kx"][DH1:KQ, h, :], io["onehot"]).then_inc(loaded, 16)
                for c in range(2):
                    sp.dma_start(w["vx"][:, c, h, DH1:KQ], io["onehotT"][c]).then_inc(loaded, 16)
                n += 3
            assert n == n_loads
            sp.wait_ge(tv_done, 6)
            sp.dma_start(pv_rows.rearrange("s i n -> (s i) n"), pv_sb).then_inc(pv_stored, 16)
            sp.wait_ge(pv_stored, 16)
            m = 0
            for side in range(2):
                n = ROWS if side == 0 else SIDE
                for h in range(H1):
                    if h < 8:
                        dst = w["pv_a"][h:h + 8 * (SLOT - 1) + 1:8, side * (ROWS + 1):side * (ROWS + 1) + n + 1, :]
                    else:
                        at = 64 * side + h - 8
                        dst = w["pv_b"][at:at + 4 * (SLOT - 1) + 1:4, 0:n + 1, :]
                    row = H1 * D
                    base = side * TAB * row + h * D
                    sp.dma_start(dst[:, 0:n, :], bass.AP(tensor=pv_rows.tensor, offset=base + (IDX0 - n + 1) * row,
                                                         ap=[[row, SLOT], [row, n], [1, D]])).then_inc(pv_loaded, 16)
                    sp.dma_start(dst[:, n, :], bass.AP(tensor=pv_rows.tensor, offset=base,
                                                       ap=[[0, SLOT], [1, D]])).then_inc(pv_loaded, 16)
                    m += 2
            sp.wait_ge(pv_loaded, 16 * m)

        @block.tensor
        def _(pe):
            pe.wait_ge(loaded, 16 * n_loads)
            for f, (a, m) in enumerate(((0, LO), (LO, HI))):
                for h in range(H1):
                    bank = f * 2 + h // 6
                    mm = nc.tensor.matmul(psum[0:m, bank, (h % 6) * 2 * TAB:(h % 6 + 1) * 2 * TAB],
                                          wq_d[:, h * D + a:h * D + a + m], tabk, start=True, stop=True)
            mm.then_inc(tk_psum, 1)
            for n in range(6):
                bank = 4 + n % 4
                if n >= 4:
                    pe.wait_ge(tv_done, n - 3)
                nc.tensor.matmul(psum[0:2 * TAB, bank, 0:2 * D], tabv, proj_d[:, n * 2 * D:(n + 1) * 2 * D],
                                 start=True, stop=True).then_inc(tv_psum, 1)

        @block.scalar
        def _(act):
            for n in range(6):
                act.wait_ge(tv_psum, n + 1)
                nc.scalar.copy(pv_sb[:, n * 2 * D:(n + 1) * 2 * D], psum[0:2 * TAB, 4 + n % 4, 0:2 * D]).then_inc(tv_done, 1)

        @block.vector
        def _(dve):
            v = nc.vector
            dve.wait_ge(loaded, 16 * n_loads)
            scale = DH1 ** -0.5
            qcols = slice(0, H1 * DH1)
            v.tensor_scalar(w["qkv_lo"][:, qcols], w["qkv_lo"][:, qcols], scale, None, ALU.mult).then_inc(built, 1)
            v.tensor_scalar(w["qkv_hi"][0:HI, qcols], w["qkv_hi"][0:HI, qcols], scale, None, ALU.mult).then_inc(built, 1)
            v.memset(w["qkv_hi"][HI:HI + 1, qcols], 0.0).then_inc(built, 1)
            for n in range(2):
                dst = w["qkv_hi"][HI:HI + 1, (n + 1) * H1 * DH1:(n + 2) * H1 * DH1].rearrange("p (h d) -> p h d", h=H1)
                a, b = (t0[:, (2 * n + k) * DH1:(2 * n + k + 1) * DH1].rearrange("p (o d) -> p o d", o=1)
                        .broadcast_to([1, H1, DH1]) for k in range(2))
                v.tensor_tensor(dst, a, b, ALU.add).then_inc(built, 1)
            dve.wait_ge(tk_psum, 1)
            for f, m in enumerate((LO, HI)):
                for bank, nh, hs in ((0, 6, "a"), (1, 2, "a"), (1, 4, "b")):
                    h0 = 0 if nh != 4 else 2
                    src = psum[0:m, f * 2 + bank, h0 * 2 * TAB:(h0 + nh) * 2 * TAB]
                    src = src.rearrange("p (h s i) -> p s i h", h=nh, s=2)
                    d0 = 6 if nh == 2 else 0
                    for side in range(2):
                        dst = w[f"tw_{hs}{f}"][:, side, :, d0:d0 + nh]
                        v.tensor_scalar(dst, src[:, side], scale, None, ALU.mult).then_inc(tk_done, 1)
            dve.wait_ge(tk_done, 12)
            for f, m in enumerate((LO, HI)):
                for hs, nh in (("a", 8), ("b", 4)):
                    for side in range(2):
                        v.tensor_copy(w[f"tz_{hs}{f}"][:, side], w[f"tw_{hs}{f}"][:, side, 0:1, :]
                                      .broadcast_to([m, SLOT, nh])).then_inc(tk_done, 1)
            dve.wait_ge(tk_done, 20)
            dve.wait_ge(built, 5)


def attention(nc, ctx, io, w, arena, psum, hA, h2, nimg):
    NG = nimg // GROUP
    NH = GROUP * H1
    PER_BANK = 512 // (GROUP * ROWS)
    LN_FROM = NH // 2
    JOBS = 16
    sem = lambda n: ctx.enter_context(nc.semaphore(n))
    h_in, h_again, h_out = sem("h_in"), sem("h_again"), sem("h2_stored")
    stats_seen, kb_seen = sem("stats_seen"), sem("kb_seen")
    stats, moments, var_eps, rstd_ok, xhat_ok = (sem(n) for n in ("stats", "moments", "var_eps", "rstd", "xhat"))
    xT_psum, xT_ok = sem("xT_psum"), sem("xT_ok")
    kb_psum, kb_dve, kb_act = sem("kb_psum"), sem("kb_dve"), sem("kb_act")
    kb_moved_a, kb_moved_b = sem("kb_moved_a"), sem("kb_moved_b")
    qk_psum, v_psum, qk_ok, v_ok = (sem(n) for n in ("qk_psum", "v_psum", "qk_ok", "v_ok"))
    logits, max_ok, exp_ok, recip_ok, prob_ok = (sem(n) for n in ("logits", "max_ok", "exp_ok", "recip_ok", "prob_ok"))
    pT_psum, pT_ok, o_psum, o_ok, a_ok = (sem(n) for n in ("pT_psum", "pT_ok", "o_psum", "o_ok", "a_ok"))
    a_moved_a, a_moved_b = sem("a_moved_a"), sem("a_moved_b")
    y_psum, y_ok, vb_psum, vb_ok, hT_psum, h2_ok = (sem(n) for n in ("y_psum", "y_ok", "vb_psum", "vb_ok", "hT_psum", "h2_ok"))

    off = [0]

    def take(cols):
        a = arena[:, off[0]:off[0] + cols]
        off[0] += cols
        return a
    xT_lo, xT_hi = (a.rearrange("p (i n) -> p i n", i=GROUP) for a in x_transposed(take))
    hin = take(CHUNKS * D).rearrange("p (c n) -> p c n", c=CHUNKS)
    hres = take(CHUNKS * D).rearrange("p (c n) -> p c n", c=CHUNKS)
    st = take(CHUNKS * 6).rearrange("p (c n) -> p c n", c=CHUNKS)
    mv = take(CHUNKS * 2).rearrange("p (c n) -> p c n", c=CHUNKS)
    ve, rstd = take(CHUNKS), take(CHUNKS)
    kst = take(3 * GT).rearrange("p (t n) -> p t n", t=3)
    qx = take(H1 * NT).rearrange("p (h n) -> p h n", h=H1)
    prob = take(3 * 2 * NT).rearrange("p (b c n) -> p b c n", b=3, c=2)
    pT = take(2 * 2 * NT).rearrange("p (b c n) -> p b c n", b=2, c=2)
    nmax = take(3 * 2).rearrange("p (b c) -> p b c", b=3)
    psums = take(3 * 2).rearrange("p (b c) -> p b c", b=3)
    prec = take(3 * 2).rearrange("p (b c) -> p b c", b=3)
    oT = take(2 * 6 * NT).rearrange("p (b h n) -> p b h n", b=2, h=6)
    ast = take(H1 * NT).rearrange("p (h n) -> p h n", h=H1)
    ap = take(3 * GT).rearrange("p (t n) -> p t n", t=3)
    yT = take(2 * GT).rearrange("p (f n) -> p f n", f=2)
    assert off[0] <= arena.shape[1], off[0]
    kx, vx = w["kx"], w["vx"]
    QK, VB, L0, T0, OB, YB = 0, 1, 2, 4, 6, 7

    RE = nimg * 144
    RC = RE + 4 * nimg * 12

    def h_loads(dst, g):
        out = []
        d = dst.rearrange("p (i c) n -> p i c n", i=GROUP)
        b0 = g * GROUP
        for c in range(2):
            for a in range(6):
                to = d[14 * (a + 1 - c) + 1:14 * (a + 1 - c) + 13, :, c, :]
                rows = hA[bass.ds(b0 * 144, GROUP * 144), :].rearrange("(i a b) n -> a b i n", i=GROUP, a=12)[6 * c + a]
                out.append((to, rows))
            e = RE + c * nimg * 12
            out.append((d[14 * 6 * c + 1:14 * 6 * c + 13, :, c, :],
                        hA[bass.ds(b0 * 12 + e, GROUP * 12), :].rearrange("(i b) n -> b i n", b=12)))
            for s in range(2):
                e = RE + (2 + s) * nimg * 12
                at = 14 * (1 - c) + 13 * s
                out.append((d[at:at + 14 * 5 + 1:14, :, c, :],
                            hA[bass.ds(b0 * 12 + e, GROUP * 12), :].rearrange("(i a) n -> a i n", i=GROUP)[6 * c:6 * c + 6]))
                r = RC + (2 * c + s) * nimg
                at = 14 * 6 * c + 13 * s
                out.append((d[at:at + 1, :, c, :], hA[bass.ds(b0 + r, GROUP), :].rearrange("(o i) n -> o i n", o=1)))
        return out
    NL = 2 * (6 + 1 + 2 + 2)

    def parts(side):
        n = ROWS if side == 0 else SIDE
        for q in range(0, n, PER_BANK):
            yield q + PER_BANK >= n, range(q, min(q + PER_BANK, n))

    def kb_jobs():
        for side in range(2):
            for hs, nh, p0 in (("a", 8, 0), ("b", 4, 64 * side)):
                for last, gs in parts(side):
                    yield side, hs, nh, p0, last, gs

    def tokens(a, side, gs):
        if side == 0:
            lo = 1 + SIDE * gs[0]
            return a[:, :, lo:lo + SIDE * len(gs)].rearrange("p i (g j) -> p g i j", g=len(gs))
        return a[:, :, 1:].rearrange("p i (j g) -> p g i j", g=SIDE)[:, gs[0]:gs[-1] + 1]

    with nc.Block() as block:
        @block.sync
        def _(sp):
            for to, src in h_loads(hin, 0):
                sp.dma_start(to, src).then_inc(h_in, 16)

            def move(dst, src, s):
                sp.dma_start(dst, src).then_inc(s, 16)

            def bias_in(i, g):
                cols = slice(i * NT, (i + 1) * NT)
                if i == 0:
                    sp.wait_ge(kb_dve, JOBS // 2 * (g + 1))
                    sp.sem_inc(kb_seen, 1)
                    sp.wait_ge(kb_act, JOBS // 2 * (g + 1))
                    sp.sem_inc(kb_seen, 1)
                if counts(g * NH + (i * H1 - 4 if i else 0)):
                    sp.wait_ge(logits, g * NH + (i * H1 - 4 if i else 0))
                for side in range(2):
                    for h in range(8):
                        move(qx[DH1 + SLOT * side:DH1 + SLOT * (side + 1), h, :],
                             kst[h:h + 8 * (SLOT - 1) + 1:8, side, cols], kb_moved_a)
                if counts(g * NH + i * H1):
                    sp.wait_ge(logits, g * NH + i * H1)
                for side in range(2):
                    for h in range(4):
                        move(qx[DH1 + SLOT * side:DH1 + SLOT * (side + 1), 8 + h, :],
                             kst[64 * side + h:64 * side + h + 4 * (SLOT - 1) + 1:4, 2, cols], kb_moved_b)

            def sums_out(i, g):
                cols = slice(i * NT, (i + 1) * NT)
                sp.wait_ge(a_ok, g * NH // 2 + (i * H1 + 8) // 2)
                for side in range(2):
                    for h in range(8):
                        move(ap[h:h + 8 * (SLOT - 1) + 1:8, side, cols],
                             ast[DH1 + SLOT * side:DH1 + SLOT * (side + 1), h, :], a_moved_a)
                sp.wait_ge(a_ok, g * NH // 2 + (i + 1) * H1 // 2)
                for side in range(2):
                    for h in range(4):
                        move(ap[64 * side + h:64 * side + h + 4 * (SLOT - 1) + 1:4, 2, cols],
                             ast[DH1 + SLOT * side:DH1 + SLOT * (side + 1), 8 + h, :], a_moved_b)

            def group(g, last):
                bias_in(0, g)
                for i in range(GROUP):
                    if i + 1 < GROUP:
                        bias_in(i + 1, g)
                    sums_out(i, g)
                    if i == 0 and not last:
                        sp.wait_ge(xT_psum, GROUP * (g + 1))
                        for to, src in h_loads(hin, g + 1):
                            sp.dma_start(to, src).then_inc(h_in, 16)
                    if i == 1:
                        if counts(16 * GROUP * g):
                            sp.wait_ge(h_out, 16 * GROUP * g)
                        for to, src in h_loads(hres, g):
                            sp.dma_start(to, src).then_inc(h_again, 16)
                for i in range(GROUP):
                    sp.wait_ge(h2_ok, GROUP * g + i + 1)
                    sp.dma_start(h2[bass.ds(g * GT + i * NT, NT), :].rearrange("(c p) n -> p c n", p=TC),
                                 hres[0:TC, 2 * i:2 * i + 2, :]).then_inc(h_out, 16)
            group(0, False)
            with sp.Fori(1, NG - 1) as g:
                group(g, False)
            group(NG - 1, True)
            sp.wait_ge(h_out, 16 * GROUP * NG)

        @block.tensor
        def _(pe):
            mm = nc.tensor.matmul

            def transposes_in(g):
                for i in range(GROUP):
                    pe.wait_ge(xhat_ok, CHUNKS * g + 2 * (i + 1))
                    if counts(GROUP * g):
                        pe.wait_ge(xT_ok, GROUP * g)
                    for c in range(2):
                        for f, (a, m) in enumerate(((0, LO), (LO, HI))):
                            t = nc.tensor.transpose(psum[0:m, i, (2 * f + c) * TC:(2 * f + c + 1) * TC],
                                                    hin[0:TC, 2 * i + c, a:a + m], w["ident"][0:TC, 0:TC])
                    t.then_inc(xT_psum, 1)

            def bias_rows(g):
                pe.wait_ge(xT_ok, GROUP * (g + 1))
                for j, (side, hs, nh, p0, last, gs) in enumerate(kb_jobs()):
                    m = nh * SLOT
                    if j >= 8:
                        pe.wait_ge(kb_act if j % 2 else kb_dve, JOBS // 2 * g + (j - 8) // 2 + 1)
                    out = psum[p0:p0 + m, j % 8, :]
                    n = GROUP * (SIDE if side == 0 else ROWS)
                    for k, q in enumerate(gs):
                        for a, x in enumerate((xT_lo, xT_hi[0:HI])):
                            t = mm(out[:, k * n:(k + 1) * n], w[f"tw_{hs}{a}"][:, side, IDX0 - q:IDX0 - q + SLOT, :],
                                   tokens(x, side, [q])[:, 0], start=(a == 0), stop=(a == 1), skip_group_check=True)
                    if last:
                        k = len(gs)
                        for a, x in enumerate((xT_lo, xT_hi[0:HI])):
                            t = mm(out[:, k * n:k * n + GROUP], w[f"tz_{hs}{a}"][:, side], x[:, :, 0],
                                   start=(a == 0), stop=(a == 1), skip_group_check=True)
                    t.then_inc(kb_psum, 1)

            def project(g, i, p):
                u = 6 * (GROUP * g + i) + p
                if counts(u):
                    pe.wait_ge(qk_ok, u)
                for n in range(2):
                    cols = slice((n * H1 + 2 * p) * DH1, (n * H1 + 2 * p + 2) * DH1)
                    out = psum[:, QK, n * NT:(n + 1) * NT]
                    mm(out, w["qkv_lo"][:, cols], xT_lo[:, i, :], start=True, stop=False)
                    t = mm(out, w["qkv_hi"][:, cols], xT_hi[:, i, :], start=False, stop=True)
                t.then_inc(qk_psum, 1)
                if counts(u):
                    pe.wait_ge(v_ok, u)
                for c in range(2):
                    cols = slice((2 * H1 + 2 * p) * DH1, (2 * H1 + 2 * p + 2) * DH1)
                    out = psum[0:TC, VB, c * 2 * DH1:(c + 1) * 2 * DH1]
                    mm(out, xT_lo[:, i, c * TC:(c + 1) * TC], w["qkv_lo"][:, cols], start=True, stop=False)
                    t = mm(out, xT_hi[:, i, c * TC:(c + 1) * TC], w["qkv_hi"][:, cols], start=False, stop=True)
                t.then_inc(v_psum, 1)

            def make_logits(g, k):
                i, h = k // H1, k % H1
                pe.wait_ge(qk_ok, 6 * GROUP * g + k // 2 + 1)
                if h < 8:
                    pe.wait_ge(kb_moved_a, 16 * 16 * (GROUP * g + i + 1))
                else:
                    pe.wait_ge(kb_moved_b, 16 * 8 * (GROUP * g + i + 1))
                if counts(g * NH + max(k - 1, 0)):
                    pe.wait_ge(exp_ok, g * NH + max(k - 1, 0))
                for c in range(2):
                    t = mm(psum[0:TC, L0 + k % 2, c * NT:(c + 1) * NT], qx[0:KQ, h, c * TC:(c + 1) * TC], kx[0:KQ, h, :],
                           start=True, stop=True)
                t.then_inc(logits, 1)

            def turn(g, k):
                pe.wait_ge(prob_ok, g * NH + k + 1)
                if counts(g * NH + max(k - 1, 0)):
                    pe.wait_ge(pT_ok, g * NH + max(k - 1, 0))
                for c in range(2):
                    for kc in range(2):
                        t = nc.tensor.transpose(psum[0:TC, T0 + k % 2, kc * NT + c * TC:kc * NT + (c + 1) * TC],
                                                prob[0:TC, k % 3, c, kc * TC:(kc + 1) * TC], w["ident"][0:TC, 0:TC])
                t.then_inc(pT_psum, 1)

            def weigh(g, k):
                pe.wait_ge(pT_ok, g * NH + k + 1)
                pe.wait_ge(v_ok, 6 * GROUP * g + k // 2 + 1)
                if k % 2 == 0:
                    if counts(g * NH // 2 + k // 2):
                        pe.wait_ge(o_ok, g * NH // 2 + k // 2)
                    if counts(g * NH // 2 + k // 2):
                        pe.wait_ge(a_ok, g * NH // 2 + k // 2)
                for kc in range(2):
                    t = mm(psum[0:KQ, OB, (k % 2) * NT:(k % 2 + 1) * NT], vx[0:TC, kc, k % H1, :], pT[0:TC, k % 2, kc, :],
                           start=(kc == 0), stop=(kc == 1))
                t.then_inc(o_psum, 1)

            def output(g, i):
                pe.wait_ge(o_ok, g * NH // 2 + (i + 1) * 6)
                if counts(GROUP * g + i):
                    pe.wait_ge(y_ok, GROUP * g + i)
                for f, (a, m) in enumerate(((0, LO), (LO, HI))):
                    for p in range(6):
                        t = mm(psum[0:m, YB, f * NT:(f + 1) * NT], w["proj"][:, p, a:a + m], oT[:, i % 2, p, :],
                               start=(p == 0), stop=(p == 5))
                t.then_inc(y_psum, 1)

            def value_tables(g):
                pe.wait_ge(a_moved_a, 16 * 16 * GROUP * (g + 1))
                pe.wait_ge(a_moved_b, 16 * 8 * GROUP * (g + 1))
                pe.wait_ge(y_ok, GROUP * (g + 1))
                j = 0
                for side in range(2):
                    n, each = (ROWS, SIDE) if side == 0 else (SIDE, ROWS)
                    at, bt = (ap[:, t, :].rearrange("p (i n) -> p i n", i=GROUP) for t in (side, 2))
                    bt = bt[64 * side:64 * side + 64]
                    for f, (a, m) in enumerate(((0, LO), (LO, HI))):
                        for last, gs in parts(side):
                            if j >= 8:
                                pe.wait_ge(vb_ok, JOBS * g + j - 7)
                            out = psum[0:m, j % 8, :]
                            for k, q in enumerate(gs):
                                o = out[:, k * GROUP * each:(k + 1) * GROUP * each]
                                mm(o, w["pv_a"][:, side * (ROWS + 1) + n - 1 - q, a:a + m], tokens(at, side, [q])[:, 0],
                                   start=True, stop=False, skip_group_check=True)
                                t = mm(o, w["pv_b"][64 * side:64 * side + 64, n - 1 - q, a:a + m], tokens(bt, side, [q])[:, 0],
                                       start=False, stop=True, skip_group_check=True)
                            if last:
                                k = len(gs) * GROUP * each
                                mm(out[:, k:k + GROUP], w["pv_a"][:, side * (ROWS + 1) + n, a:a + m], at[:, :, 0],
                                   start=True, stop=False, skip_group_check=True)
                                t = mm(out[:, k:k + GROUP], w["pv_b"][64 * side:64 * side + 64, n, a:a + m], bt[:, :, 0],
                                       start=False, stop=True, skip_group_check=True)
                            t.then_inc(vb_psum, 1)
                            j += 1

            def transposes_out(g):
                pe.wait_ge(vb_ok, JOBS * (g + 1))
                for i in range(GROUP):
                    for c in range(2):
                        for f, (a, m) in enumerate(((0, LO), (LO, HI))):
                            t = nc.tensor.transpose(psum[0:TC, i, c * D + a:c * D + a + m],
                                                    yT[0:m, f, i * NT + c * TC:i * NT + (c + 1) * TC],
                                                    w["ident"][0:m, 0:m])
                    t.then_inc(hT_psum, 1)

            def group(g):
                if counts(g):
                    pe.wait_ge(h2_ok, GROUP * g)
                transposes_in(g)
                bias_rows(g)
                pe.wait_ge(kb_dve, JOBS // 2 * (g + 1))
                pe.wait_ge(kb_act, JOBS // 2 * (g + 1))
                for p in range(6):
                    project(g, 0, p)
                for s in range(NH + 6):
                    if s < NH:
                        make_logits(g, s)
                    if 0 <= s - 2 < NH:
                        turn(g, s - 2)
                    if 0 <= s - 3 < NH:
                        weigh(g, s - 3)
                    if s >= 5 and (s - 4) % 2 == 1:
                        i, p = (s - 4) // H1, (s - 4) % H1 // 2
                        if i + 1 < GROUP:
                            project(g, i + 1, p)
                    if s >= H1 + 5 and (s - 5) % H1 == 0:
                        output(g, (s - 5) // H1 - 1)
                value_tables(g)
                transposes_out(g)
            group(0)
            with pe.Fori(1, NG) as g:
                group(g)

        def kb_evacuate(eng, copy, g, parity, done):
            for j, (side, hs, nh, p0, last, gs) in enumerate(kb_jobs()):
                if j % 2 != parity:
                    continue
                eng.wait_ge(kb_psum, JOBS * g + j + 1)
                m, each = nh * SLOT, (SIDE if side == 0 else ROWS)
                tile = side if hs == "a" else 2
                dst = kst[p0:p0 + m, tile, :].rearrange("p (i n) -> p i n", i=GROUP)
                n = len(gs) * GROUP * each
                src = psum[p0:p0 + m, j % 8, 0:n].rearrange("p (g i j) -> p g i j", g=len(gs), i=GROUP)
                ins = copy(tokens(dst, side, gs), src)
                if last:
                    ins = copy(dst[:, :, 0], psum[p0:p0 + m, j % 8, n:n + GROUP])
                ins.then_inc(done, 1)

        @block.scalar
        def _(act):
            def take_v(g, i, p):
                u = 6 * (GROUP * g + i) + p
                act.wait_ge(v_psum, u + 1)
                nc.scalar.copy(vx[0:TC, :, 2 * p:2 * p + 2, 0:DH1],
                               psum[0:TC, VB, 0:4 * DH1].rearrange("p (c e d) -> p c e d", c=2, e=2)).then_inc(v_ok, 1)

            def exponent(g, k):
                act.wait_ge(max_ok, g * NH + k + 1)
                if counts(g * NH + max(k - 2, 0)):
                    act.wait_ge(pT_psum, g * NH + max(k - 2, 0))
                for c in range(2):
                    e = nc.scalar.activation(prob[0:TC, k % 3, c, :], psum[0:TC, L0 + k % 2, c * NT:(c + 1) * NT], ACT.Exp,
                                             bias=nmax[0:TC, k % 3, c:c + 1], accum_out=psums[0:TC, k % 3, c:c + 1])
                e.then_inc(exp_ok, 1)

            def take_out(g, u):
                i, p = u // 6, u % 6
                act.wait_ge(o_psum, g * NH + 2 * u + 2)
                if counts(GROUP * g + max(i - 1, 0)):
                    act.wait_ge(y_psum, GROUP * g + max(i - 1, 0))
                nc.scalar.copy(oT[0:DH1, i % 2, p, :], psum[0:DH1, OB, 0:NT])
                nc.scalar.copy(oT[DH1:2 * DH1, i % 2, p, :], psum[0:DH1, OB, NT:2 * NT]).then_inc(o_ok, 1)

            def group(g):
                if counts(16 * 16 * GROUP * g):
                    act.wait_ge(kb_moved_a, 16 * 16 * GROUP * g)
                if counts(16 * 8 * GROUP * g):
                    act.wait_ge(kb_moved_b, 16 * 8 * GROUP * g)
                kb_evacuate(act, nc.scalar.copy, g, 1, kb_act)
                for p in range(6):
                    take_v(g, 0, p)
                for s in range(NH + 6):
                    if s < NH:
                        exponent(g, s)
                    if s >= 4 and (s - 4) % 2 == 0 and (s - 4) // 2 < NH // 2:
                        take_out(g, (s - 4) // 2)
                    if s >= 5 and (s - 4) % 2 == 1:
                        i, p = (s - 4) // H1, (s - 4) % H1 // 2
                        if i + 1 < GROUP:
                            take_v(g, i + 1, p)
            group(0)
            with act.Fori(1, NG) as g:
                group(g)

        @block.gpsimd
        def _(pool):
            def norm(g):
                pool.wait_ge(var_eps, g + 1)
                nc.gpsimd.tensor_tensor(rstd[0:TC], ve[0:TC], w["mhalf"][0:TC], ALU.pow).then_inc(rstd_ok, 1)
            norm(0)

            def group(g, last):
                for k in range(NH):
                    pool.wait_ge(recip_ok, g * NH + k + 1)
                    b = k % 3
                    pr = prob[0:TC, b]
                    nc.gpsimd.tensor_tensor(pr, pr, prec[0:TC, b].rearrange("p (c o) -> p c o", o=1)
                                            .broadcast_to([TC, 2, NT]), ALU.mult).then_inc(prob_ok, 1)
                    if k == LN_FROM + GROUP and not last:
                        norm(g + 1)
            group(0, False)
            with pool.Fori(1, NG - 1) as g:
                group(g, False)
            group(NG - 1, True)

        @block.vector
        def _(dve):
            v = nc.vector

            def ln_stats(g, i):
                if i == 0:
                    dve.wait_ge(h_in, 16 * NL * (g + 1))
                for c in (2 * i, 2 * i + 1):
                    v.bn_stats(st[0:TC, c], hin[0:TC, c]).then_inc(stats, 1)

            def ln_moments(g):
                dve.wait_ge(stats, CHUNKS * (g + 1))
                dve.sem_inc(stats_seen, 1)
                for c in range(CHUNKS):
                    v.bn_aggr(mv[0:TC, c], st[0:TC, c]).then_inc(moments, 1)
                dve.wait_ge(moments, CHUNKS * (g + 1))
                v.tensor_scalar(ve[0:TC], mv[0:TC, :, 1], EPS, None, ALU.add).then_inc(var_eps, 1)

            def ln_apply(g, i):
                if i == 0:
                    dve.wait_ge(rstd_ok, g + 1)
                for c in (2 * i, 2 * i + 1):
                    v.tensor_scalar(hin[0:TC, c], hin[0:TC, c], mv[0:TC, c, 0:1], rstd[0:TC, c:c + 1],
                                    ALU.subtract, ALU.mult).then_inc(xhat_ok, 1)

            def take_xT(g):
                for i in range(GROUP):
                    dve.wait_ge(xT_psum, GROUP * g + i + 1)
                    v.tensor_copy(xT_lo[:, i, :], psum[:, i, 0:NT])
                    v.tensor_copy(xT_hi[0:HI, i, :], psum[0:HI, i, NT:2 * NT]).then_inc(xT_ok, 1)

            def take_qk(g, i, p):
                dve.wait_ge(qk_psum, 6 * (GROUP * g + i) + p + 1)
                v.tensor_copy(qx[0:DH1, 2 * p, :], psum[0:DH1, QK, 0:NT])
                v.tensor_copy(qx[0:DH1, 2 * p + 1, :], psum[DH1:2 * DH1, QK, 0:NT])
                v.tensor_copy(kx[0:DH1, 2 * p, :], psum[0:DH1, QK, NT:2 * NT])
                v.tensor_copy(kx[0:DH1, 2 * p + 1, :], psum[DH1:2 * DH1, QK, NT:2 * NT]).then_inc(qk_ok, 1)

            def maximum(g, k):
                dve.wait_ge(logits, g * NH + k + 1)
                v.tensor_reduce(nmax[0:TC, k % 3], psum[0:TC, L0 + k % 2, 0:2 * NT].rearrange("p (c n) -> p c n", c=2),
                                AX.X, ALU.max, negate=True).then_inc(max_ok, 1)

            def reciprocals(g, k):
                dve.wait_ge(exp_ok, g * NH + k + 1)
                v.reciprocal(prec[0:TC, k % 3], psums[0:TC, k % 3]).then_inc(recip_ok, 1)

            def take_pT(g, k):
                dve.wait_ge(pT_psum, g * NH + k + 1)
                if counts(g * NH + max(k - 1, 0)):
                    dve.wait_ge(o_psum, g * NH + max(k - 1, 0))
                v.tensor_copy(pT[0:TC, k % 2], psum[0:TC, T0 + k % 2, 0:2 * NT].rearrange("p (c n) -> p c n", c=2)).then_inc(pT_ok, 1)

            def take_sums(g, u):
                i, p = u // 6, u % 6
                dve.wait_ge(o_psum, g * NH + 2 * u + 2)
                if p < 4:
                    if counts(16 * 16 * (GROUP * g + i)):
                        dve.wait_ge(a_moved_a, 16 * 16 * (GROUP * g + i))
                else:
                    if counts(16 * 8 * (GROUP * g + i)):
                        dve.wait_ge(a_moved_b, 16 * 8 * (GROUP * g + i))
                v.tensor_copy(ast[DH1:KQ, 2 * p:2 * p + 2, :],
                              psum[DH1:KQ, OB, 0:2 * NT].rearrange("p (e n) -> p e n", e=2)).then_inc(a_ok, 1)

            def take_y(g, i):
                dve.wait_ge(y_psum, GROUP * g + i + 1)
                if counts(GROUP * g):
                    dve.wait_ge(hT_psum, GROUP * g)
                c = slice(i * NT, (i + 1) * NT)
                v.tensor_scalar(yT[:, 0, c], psum[:, YB, 0:NT], w["projb_lo"], None, ALU.add)
                v.tensor_scalar(yT[0:HI, 1, c], psum[0:HI, YB, NT:2 * NT], w["projb_hi"], None, ALU.add).then_inc(y_ok, 1)

            def add_tables(g):
                j = 0
                for side in range(2):
                    n, each = (ROWS, SIDE) if side == 0 else (SIDE, ROWS)
                    for f, m in enumerate((LO, HI)):
                        for last, gs in parts(side):
                            dve.wait_ge(vb_psum, JOBS * g + j + 1)
                            dve.wait_ge(y_ok, GROUP * (g + 1))
                            if side:
                                dve.wait_ge(vb_ok, JOBS * g + JOBS // 2)
                            y = yT[0:m, f, :].rearrange("p (i n) -> p i n", i=GROUP)
                            k = len(gs) * GROUP * each
                            src = psum[0:m, j % 8, 0:k].rearrange("p (g i j) -> p g i j", g=len(gs), i=GROUP)
                            ins = v.tensor_tensor(tokens(y, side, gs), src, tokens(y, side, gs), ALU.add)
                            if last:
                                ins = v.tensor_tensor(y[:, :, 0], psum[0:m, j % 8, k:k + GROUP], y[:, :, 0], ALU.add)
                            ins.then_inc(vb_ok, 1)
                            j += 1

            def residual(g):
                dve.wait_ge(h_again, 16 * NL * (g + 1))
                for i in range(GROUP):
                    dve.wait_ge(hT_psum, GROUP * g + i + 1)
                    r = hres[0:TC, 2 * i:2 * i + 2, :]
                    v.tensor_tensor(r, psum[0:TC, i, 0:2 * D].rearrange("p (c n) -> p c n", c=2), r, ALU.add).then_inc(h2_ok, 1)

            for i in range(GROUP):
                ln_stats(0, i)
            ln_moments(0)
            for i in range(GROUP):
                ln_apply(0, i)

            def group(g, last):
                take_xT(g)
                if counts(16 * 16 * GROUP * g):
                    dve.wait_ge(kb_moved_a, 16 * 16 * GROUP * g)
                if counts(16 * 8 * GROUP * g):
                    dve.wait_ge(kb_moved_b, 16 * 8 * GROUP * g)
                kb_evacuate(dve, v.tensor_copy, g, 0, kb_dve)
                for p in range(6):
                    take_qk(g, 0, p)
                for s in range(NH + 6):
                    if 0 <= s - 1 < NH:
                        reciprocals(g, s - 1)
                    if s < NH:
                        maximum(g, s)
                    if 0 <= s - 2 < NH:
                        take_pT(g, s - 2)
                    if s >= 4 and (s - 4) % 2 == 0 and (s - 4) // 2 < NH // 2:
                        take_sums(g, (s - 4) // 2)
                    if s >= 5 and (s - 4) % 2 == 1:
                        i, p = (s - 4) // H1, (s - 4) % H1 // 2
                        if i + 1 < GROUP:
                            take_qk(g, i + 1, p)
                    if s >= H1 + 5 and (s - 5) % H1 == 0:
                        take_y(g, (s - 5) // H1 - 1)
                    if not last and 0 <= s - LN_FROM < GROUP:
                        ln_stats(g + 1, s - LN_FROM)
                    if not last and s == LN_FROM + GROUP:
                        ln_moments(g + 1)
                    if not last and 0 <= s - LN_FROM - GROUP - 4 < GROUP:
                        ln_apply(g + 1, s - LN_FROM - GROUP - 4)
                add_tables(g)
                residual(g)
            group(0, False)
            with dve.Fori(1, NG - 1) as g:
                group(g, False)
            group(NG - 1, True)



TOPK = max(1, int(round(0.15 * NT)))
DH3 = D // H1
F = 4 * D
FT = F // 128
HQ = 4
QT = HQ * TOPK


def feed_forward(nc, ctx, io, arena, psum, h2, out, nimg):
    def sems(*names):
        return [ctx.enter_context(nc.semaphore(n)) for n in names]
    off = [0]

    def take(cols):
        a = arena[:, off[0]:off[0] + cols]
        off[0] += cols
        return a

    def two(cols):
        return [take(cols) for _ in range(2)]

    def tok(cols=D):
        return [take(2 * cols)[0:TC].rearrange("p (c n) -> p c n", c=2) for _ in range(2)]
    W = {}
    for n in ("Wq", "Wk", "Wv", "Wo", "Wm", "W1"):
        c = F if n == "W1" else D
        W[n] = (take(c), take(c)[0:HI])
    W2 = take(FT * D).rearrange("p (t n) -> p t n", t=FT)
    row = {n: take(D) for n in ("g1", "b1", "g2", "b2", "Wr", "bv", "bo", "bm", "bf2")}
    col = {n: (take(1), take(1)[0:HI]) for n in ("bq", "bk")}
    bf1, br = take(FT), take(1)
    nbr = take(1)
    ident, ones = take(128), take(128)
    slots = take(TOPK)[0:TC]
    before = take(2 * NT)[0:TC].rearrange("p (c n) -> p c n", c=2)
    own = take(8)
    mhalf = take(2)[0:TC]
    hc, n0, nn = tok(), tok(), tok()
    res, rb = tok(), tok()
    st = [take(12)[0:TC].rearrange("p (c n) -> p c n", c=2) for _ in range(2)]
    mv = [take(4)[0:TC].rearrange("p (c n) -> p c n", c=2) for _ in range(2)]
    ve, rs = [a[0:TC] for a in two(2)], [a[0:TC] for a in two(2)]
    st3 = take(12)[0:TC].rearrange("p (c n) -> p c n", c=2)
    mv3 = take(4)[0:TC].rearrange("p (c n) -> p c n", c=2)
    ve2, rs2 = take(2)[0:TC], take(2)[0:TC]
    cmp = [take(NT)[0:TC] for _ in range(4)]
    z = [a[0:TC] for a in two(2)]
    ez, ez1 = take(2)[0:TC], take(2)[0:TC]
    sel = [take(2 * (TOPK + 1))[0:TC].rearrange("p (c n) -> p c n", c=2) for _ in range(2)]
    zb = take(2 * TC)[0:TC].rearrange("p (c n) -> p c n", c=2)
    sb = take(2 * 128)[0:TC].rearrange("p (c n) -> p c n", c=2)
    junk = take(2 * D)[0:TC]
    lt, eq, rank = take(2)[0:TC], take(2)[0:TC], take(2)[0:TC]
    keep = [a[0:TC] for a in two(2)]
    nT = [(take(NT), take(NT)[0:HI]) for _ in range(2)]
    kT = [(take(NT), take(NT)[0:HI]) for _ in range(2)]
    vv = tok()
    nsel = (take(TOPK), take(TOPK)[0:HI])
    ssum, sinv = take(1), take(1)
    pooled = (take(1), take(1)[0:HI])
    selT = take(NT)[0:TOPK]
    qs = (take(TOPK), take(TOPK)[0:HI])
    qblk = (take(8 * TOPK).rearrange("p (h j) -> p h j", h=8), take(4 * TOPK)[0:HI].rearrange("p (h j) -> p h j", h=4))
    nmax, esum, einv = take(3)[0:QT], take(3)[0:QT], take(3)[0:QT]
    pr = take(3 * NT)[0:QT].rearrange("p (t n) -> p t n", t=3)
    pT = take(2 * 3 * QT)[0:TC].rearrange("p (c n) -> p c n", c=2)
    cm = (take(8 * TOPK).rearrange("p (h j) -> p h j", h=8), take(4 * TOPK)[0:HI].rearrange("p (h j) -> p h j", h=4))
    ctxT = (take(TOPK), take(TOPK)[0:HI])
    asel = take(D)[0:TOPK]
    mixT = (take(NT), take(NT)[0:HI])
    mixb, kept_mix = take(2 * D)[0:TC].rearrange("p (c n) -> p c n", c=2), take(2 * D)[0:TC].rearrange("p (c n) -> p c n", c=2)
    hh, n2 = tok(), tok()
    na, hg = tok()
    n2T = (take(NT), take(NT)[0:HI])
    gT = take(FT * NT).rearrange("p (t n) -> p t n", t=FT)
    oo = tok()
    assert off[0] <= arena.shape[1], off[0]
    NTB, RB, SB, KB, VB, L0, L1, UB = range(8)
    GA, GB, SS, ST, QA, QB = 0, 32, 64, 96, 300, 332
    feats = ((0, 0, LO), (1, LO, HI))

    stats3_seen, fw_loaded, f_const = sems("stats3_seen", "fw_loaded", "f_const")
    f_in, f_out = sems("f_in0", "f_in1"), sems("f_out0", "f_out1")
    a_stats, a_mom, a_var, a_rstd, a_n0 = sems("a_stats", "a_mom", "a_var", "a_rstd", "a_n0")
    a_stats2, a_mom2, a_var2, a_rstd2 = sems("a_stats2", "a_mom2", "a_var2", "a_rstd2")
    a_ng, a_n, a_res = sems("a_ng", "a_n", "a_res")
    a_z, a_ez, a_ez1, a_score = sems("a_z", "a_ez", "a_ez1", "a_score")
    a_zb, a_sb, a_zrow, a_srow = sems("a_zb", "a_sb", "a_zrow", "a_srow")
    a_cnt, a_rank, a_sel = sems("a_cnt", "a_rank", "a_sel")
    a_nT_ps, a_nT, a_k_ps, a_k, a_v_ps, a_v = sems("a_nT_ps", "a_nT", "a_k_ps", "a_k", "a_v_ps", "a_v")
    b_gat_ps, b_gat, b_sinv, b_pool = sems("b_gat_ps", "b_gat", "b_sinv", "b_pool")
    b_q_ps, b_q, b_qblk, b_log = sems("b_q_ps", "b_q", "b_qblk", "b_log")
    b_max, b_exp, b_inv, b_prob = sems("b_max", "b_exp", "b_inv", "b_prob")
    b_pT_ps, b_pT, b_av_ps, b_av, b_ctx = sems("b_pT_ps", "b_pT", "b_av_ps", "b_av", "b_ctx")
    b_wo_ps, b_asel, b_sca_ps, b_h, b_res = sems("b_wo_ps", "b_asel", "b_sca_ps", "b_h", "b_res")
    b_mixT, b_mix_ps, b_mixb, b_kept = sems("b_mixT", "b_mix_ps", "b_mixb", "b_kept")
    b_stats, b_mom, b_var, b_rstd = sems("b_stats", "b_mom", "b_var", "b_rstd")
    b_hg, b_n2 = sems("b_hg", "b_n2")
    c_n2T_ps, c_n2T, c_down, c_out = sems("c_n2T_ps", "c_n2T", "c_down", "c_out")
    c_up, c_g = sems("c_up0", "c_up1", "c_up2"), sems("c_g0", "c_g1", "c_g2")
    mm, tr = nc.tensor.matmul, nc.tensor.transpose

    def images(n):
        return min(n, nimg) if isinstance(n, int) else n

    def pipeline(eng, step):
        def peeled(i):
            step(i, i % 2, [0 <= i - k < nimg for k in range(-1, 4)])
        for i in range(-1, 6):
            peeled(i)
        with eng.Fori(3, nimg // 2 - 1) as u:
            for r in range(2):
                step(u * 2 + r, r, [True] * 5)
        for i in range(nimg - 2, nimg + 3):
            peeled(i)

    with nc.Block() as block:
        LOADS = 12 + 1 + len(row) + 4 + 7

        @block.sync
        def _(sp):
            n = 0

            def load(dst, src):
                nonlocal n
                sp.dma_start(dst, src).then_inc(fw_loaded, 16)
                n += 1
            for name in ("Wq", "Wk", "Wv", "Wo", "Wm", "W1"):
                for f, a, m in feats:
                    load(W[name][f], io[name][a:a + m, :])
            load(W2, io["W2"].rearrange("(t p) n -> p t n", t=FT))
            for name in row:
                load(row[name], io[name].partition_broadcast(128))
            for name in col:
                for f, a, m in feats:
                    load(col[name][f], io[name].rearrange("(n o) -> n o", o=1)[a:a + m, :])
            load(bf1, io["bf1"])
            load(br, io["br"].partition_broadcast(128))
            load(ident, io["ident"])
            load(slots, io["slots"])
            load(before, io["before"])
            load(own, io["own"])
            load(mhalf, io["mhalf"][0:TC, 0:2])
            assert n == LOADS

            def step(i, r, on):
                if on[0]:
                    if counts(i):
                        sp.wait_ge(a_res, i)
                        sp.wait_ge(a_n0, i)
                    src = h2[bass.ds((i + 1) * NT, NT), :].rearrange("(c p) n -> p c n", p=TC)
                    sp.dma_start(hc[1 - r], src).then_inc(f_in[1 - r], 16)
                if on[4]:
                    sp.wait_ge(c_out, i - 2)
                    dst = out[bass.ds((i - 3) * NT, NT), :].rearrange("(c p) n -> p c n", p=TC)
                    sp.dma_start(dst, oo[1 - r]).then_inc(f_out[1 - r], 16)
            pipeline(sp, step)
            for r in range(2):
                sp.wait_ge(f_out[r], 16 * (nimg // 2))

        @block.tensor
        def _(pe):
            def A_turn(i, r):
                pe.wait_ge(a_n, i + 1)
                if counts(i - 2):
                    pe.wait_ge(c_n2T, i - 2)
                for f, a, m in feats:
                    for c in range(2):
                        t = tr(psum[0:m, NTB, f * NT + c * TC:f * NT + (c + 1) * TC], nn[r][:, c, a:a + m], ident[0:TC, 0:TC])
                t.then_inc(a_nT_ps, 1)

            def A_zrow(i, r):
                pe.wait_ge(a_zb, i + 1)
                if counts(i):
                    pe.wait_ge(b_mixT, i)
                for c in range(2):
                    t = tr(psum[0:TC, RB, c * TC:(c + 1) * TC], zb[:, c, :], ident[0:TC, 0:TC])
                t.then_inc(a_zrow, 1)

            def A_srow(i, r):
                pe.wait_ge(a_sb, i + 1)
                pe.wait_ge(a_cnt, 4 * i + 4)
                for c in range(2):
                    t = tr(psum[:, RB, NT + c * TC:NT + (c + 1) * TC], sb[:, c, :], ident[0:TC, 0:TC])
                t.then_inc(a_srow, 1)

            def A_k(i, r):
                pe.wait_ge(a_nT, i + 1)
                if counts(i * 2 - 2):
                    pe.wait_ge(b_av, i * 2 - 2)
                if counts(i - 2):
                    pe.wait_ge(c_g[1], i - 2)
                for f, a, m in feats:
                    o = psum[0:m, KB, f * NT:(f + 1) * NT]
                    mm(o, W["Wk"][0][:, a:a + m], nT[r][0], start=True, stop=False)
                    t = mm(o, W["Wk"][1][:, a:a + m], nT[r][1], start=False, stop=True)
                t.then_inc(a_k_ps, 1)

            def A_v(i, r):
                if counts(i - 1):
                    pe.wait_ge(b_h, i - 1)
                for c in range(2):
                    o = psum[0:TC, VB, c * D:(c + 1) * D]
                    mm(o, nT[r][0][:, c * TC:(c + 1) * TC], W["Wv"][0], start=True, stop=False)
                    t = mm(o, nT[r][1][:, c * TC:(c + 1) * TC], W["Wv"][1], start=False, stop=True)
                t.then_inc(a_v_ps, 1)

            def B_gather(i, r):
                pe.wait_ge(a_sel, 4 * i + 4)
                pe.wait_ge(a_score, i + 1)
                if counts(i):
                    pe.wait_ge(b_asel, i)
                for (f, a, m), o in zip(feats, (GA, GB)):
                    for c in range(2):
                        mm(psum[0:m, SB, o:o + TOPK + 1], nn[r][:, c, a:a + m], sel[r][:, c, :],
                           start=(c == 0), stop=(c == 1))
                for c in range(2):
                    mm(psum[:, SB, SS:SS + 1], ones[0:TC, :], sel[r][:, c, TOPK:TOPK + 1], start=(c == 0), stop=(c == 1))
                for c in range(2):
                    t = tr(psum[0:TOPK, SB, ST + c * TC:ST + (c + 1) * TC], sel[r][:, c, 0:TOPK], ident[0:TC, 0:TC])
                t.then_inc(b_gat_ps, 1)

            def B_q(i, r):
                pe.wait_ge(b_gat, 4 * i + 4)
                pe.wait_ge(b_pool, 2 * i + 2)
                for (f, a, m), o in zip(feats, (QA, QB)):
                    for k in range(2):
                        t = mm(psum[0:m, SB, o:o + TOPK], W["Wq"][k][:, a:a + m], nsel[k], start=(k == 0), stop=(k == 1))
                t.then_inc(b_q_ps, 1)

            def B_logits(i, r):
                pe.wait_ge(b_qblk, 2 * i + 2)
                pe.wait_ge(a_k, i + 1)
                if counts(i):
                    pe.wait_ge(b_pT, i)
                for t3 in range(3):
                    k, h = (0, HQ * t3) if t3 < 2 else (1, 0)
                    o = psum[0:QT, L0 if t3 < 2 else L1, (t3 % 2) * NT:(t3 % 2 + 1) * NT]
                    t = mm(o, qblk[k][:, h:h + HQ, :], kT[r][k], start=True, stop=True)
                t.then_inc(b_log, 1)

            def B_turn(i, r):
                pe.wait_ge(b_prob, i + 1)
                for c in range(2):
                    for t3 in range(3):
                        t = tr(psum[0:TC, L0 + c, t3 * QT:(t3 + 1) * QT], pr[:, t3, c * TC:(c + 1) * TC], ident[0:QT, 0:QT])
                t.then_inc(b_pT_ps, 1)

            def B_av(i, r):
                pe.wait_ge(b_pT, i + 1)
                pe.wait_ge(a_v, i + 1)
                pe.wait_ge(a_k, images(i + 2))
                for k, (f, a, m) in enumerate(feats):
                    w_ = (8 if k == 0 else 4) * TOPK
                    for c in range(2):
                        t = mm(psum[0:m, KB, k * 8 * TOPK:k * 8 * TOPK + w_], vv[r][:, c, a:a + m],
                               pT[:, c, k * 8 * TOPK:k * 8 * TOPK + w_], start=(c == 0), stop=(c == 1))
                t.then_inc(b_av_ps, 1)

            def B_wo(i, r):
                pe.wait_ge(b_ctx, 2 * i + 2)
                for k in range(2):
                    t = mm(psum[0:TOPK, SB, 0:D], ctxT[k], W["Wo"][k], start=(k == 0), stop=(k == 1))
                t.then_inc(b_wo_ps, 1)

            def B_scatter(i, r):
                pe.wait_ge(b_asel, i + 1)
                pe.wait_ge(a_v, images(i + 2))
                for c in range(2):
                    t = mm(psum[0:TC, VB, c * D:(c + 1) * D], selT[:, c * TC:(c + 1) * TC], asel, start=True, stop=True)
                t.then_inc(b_sca_ps, 1)

            def B_mix(i, r):
                pe.wait_ge(b_mixT, i + 1)
                if counts(i - 1):
                    pe.wait_ge(c_g[2], i - 1)
                for c in range(2):
                    for k in range(2):
                        t = mm(psum[0:TC, UB, c * D:(c + 1) * D], mixT[k][:, c * TC:(c + 1) * TC], W["Wm"][k],
                               start=(k == 0), stop=(k == 1))
                t.then_inc(b_mix_ps, 1)

            def C_turn(i, r):
                pe.wait_ge(b_n2, i + 1)
                if counts(i):
                    pe.wait_ge(c_out, i)
                for f, a, m in feats:
                    for c in range(2):
                        t = tr(psum[0:m, NTB, f * NT + c * TC:f * NT + (c + 1) * TC], n2[r][:, c, a:a + m], ident[0:TC, 0:TC])
                t.then_inc(c_n2T_ps, 1)

            def C_up(i, r, n):
                pe.wait_ge(c_n2T, i + 1)
                if n == 0:
                    pe.wait_ge(b_mixb, images(i + 2))
                if n == 1:
                    pe.wait_ge(b_av, 2 * images(i + 2))
                if n == 2:
                    pe.wait_ge(c_g[0], i + 1)
                for e in range(2):
                    o = psum[:, (UB, KB, UB)[n], e * NT:(e + 1) * NT]
                    cols = slice((2 * n + e) * 128, (2 * n + e + 1) * 128)
                    mm(o, W["W1"][0][:, cols], n2T[0], start=True, stop=False)
                    t = mm(o, W["W1"][1][:, cols], n2T[1], start=False, stop=True)
                t.then_inc(c_up[n], 1)

            def C_down(i, r, c, ts):
                pe.wait_ge(c_g[2], i + 1)
                pe.wait_ge(c_g[1], i + 1)
                pe.wait_ge(a_nT, images(i + 4))
                for t3 in ts:
                    t = mm(psum[0:TC, NTB, c * D:(c + 1) * D], gT[:, t3, c * TC:(c + 1) * TC], W2[:, t3, :],
                           start=(t3 == 0), stop=(t3 == FT - 1))
                if c == 1 and ts[-1] == FT - 1:
                    t.then_inc(c_down, 1)

            def step(i, r, on):
                nxt, a, b, b2, c = on
                q = 1 - r
                if c: C_turn(i - 3, q)
                if b: B_gather(i - 1, q)
                if c: C_up(i - 3, q, 0)
                if b: B_q(i - 1, q)
                if c: C_up(i - 3, q, 1)
                if b: B_logits(i - 1, q)
                if c: C_up(i - 3, q, 2)
                if a: A_turn(i, r)
                if b: B_mix(i - 1, q)
                if a: A_k(i, r)
                if a: A_zrow(i, r)
                if a: A_v(i, r)
                if b: B_turn(i - 1, q)
                if c: C_down(i - 3, q, 0, range(0, 3))
                if b: B_av(i - 1, q)
                if c: C_down(i - 3, q, 0, range(3, 6))
                if c: C_down(i - 3, q, 1, range(0, 3))
                if b: B_wo(i - 1, q)
                if c: C_down(i - 3, q, 1, range(3, 6))
                if b: B_scatter(i - 1, q)
                if a: A_srow(i, r)
            pe.wait_ge(fw_loaded, 16 * LOADS)
            pe.wait_ge(f_const, 2)
            pipeline(pe, step)

        @block.scalar
        def _(act):
            sa, cp = nc.scalar.activation, nc.scalar.copy

            def C_n2T(i):
                act.wait_ge(c_n2T_ps, i + 1)
                cp(n2T[0], psum[:, NTB, 0:NT])
                cp(n2T[1], psum[0:HI, NTB, NT:2 * NT]).then_inc(c_n2T, 1)

            def C_gelu(i, n):
                act.wait_ge(c_up[n], i + 1)
                if counts(i):
                    act.wait_ge(c_down, i)
                for e in range(2):
                    t = 2 * n + e
                    g = sa(gT[:, t, :], psum[:, (UB, KB, UB)[n], e * NT:(e + 1) * NT], ACT.Gelu, bias=bf1[:, t:t + 1])
                g.then_inc(c_g[n], 1)

            def A_nT(i, r):
                act.wait_ge(a_nT_ps, i + 1)
                if counts(i - 1):
                    act.wait_ge(b_mixT, i - 1)
                cp(nT[r][0], psum[:, NTB, 0:NT])
                cp(nT[r][1], psum[0:HI, NTB, NT:2 * NT]).then_inc(a_nT, 1)

            def A_k(i, r):
                act.wait_ge(a_k_ps, i + 1)
                for f, a, m in feats:
                    t = sa(kT[r][f], psum[0:m, KB, f * NT:(f + 1) * NT], ACT.Identity, bias=col["bk"][f])
                t.then_inc(a_k, 1)

            def A_ez(i, r):
                act.wait_ge(a_z, i + 1)
                if counts(i):
                    act.wait_ge(a_ez1, i)
                sa(ez, z[r], ACT.Exp, bias=nbr[0:TC], scale=-1.0).then_inc(a_ez, 1)

            def B_exp(i):
                act.wait_ge(b_max, 2 * i + 2)
                if counts(i):
                    act.wait_ge(b_pT_ps, i)
                for t in range(3):
                    o = psum[0:QT, L0 if t < 2 else L1, (t % 2) * NT:(t % 2 + 1) * NT]
                    e = sa(pr[:, t, :], o, ACT.Exp, bias=nmax[:, t:t + 1], accum_out=esum[:, t:t + 1])
                e.then_inc(b_exp, 1)

            def B_pT(i):
                act.wait_ge(b_pT_ps, i + 1)
                cp(pT[:, 0, :], psum[0:TC, L0, 0:3 * QT])
                cp(pT[:, 1, :], psum[0:TC, L1, 0:3 * QT]).then_inc(b_pT, 1)

            def step(i, r, on):
                nxt, a, b, b2, c = on
                if c: C_n2T(i - 3)
                for n in range(3):
                    if c: C_gelu(i - 3, n)
                if a: A_nT(i, r)
                if b: B_exp(i - 1)
                if a: A_k(i, r)
                if a: A_ez(i, r)
                if b: B_pT(i - 1)
            act.wait_ge(fw_loaded, 16 * LOADS)
            act.wait_ge(f_const, 2)
            pipeline(act, step)

        def rowc(name):
            return row[name][0:TC].rearrange("p (o n) -> p o n", o=1).broadcast_to([TC, 2, D])

        @block.gpsimd
        def _(pool):
            g = nc.gpsimd

            def A_rstd(i):
                pool.wait_ge(a_var, i + 1)
                g.tensor_tensor(rs[0], ve[0], mhalf, ALU.pow).then_inc(a_rstd, 1)

            def A_res(i, r):
                pool.wait_ge(f_in[r], (i * 8 + (16 - 8 * r)))
                if counts(i - 1):
                    pool.wait_ge(b_res, i - 1)
                g.tensor_tensor(res[r], hc[r], rowc("bf2"), ALU.add).then_inc(a_res, 1)

            def A_rstd2(i):
                pool.wait_ge(a_var2, i + 1)
                g.tensor_tensor(rs[1], ve[1], mhalf, ALU.pow).then_inc(a_rstd2, 1)

            def A_zb(i, r):
                pool.wait_ge(f_const, 2)
                pool.wait_ge(a_z, i + 1)
                if counts(i):
                    pool.wait_ge(a_zrow, i)
                g.tensor_copy(zb, z[r].rearrange("p (c o) -> p c o", o=1).broadcast_to([TC, 2, TC])).then_inc(a_zb, 1)

            def A_sb(i, r):
                pool.wait_ge(f_const, 2)
                pool.wait_ge(a_score, i + 1)
                if counts(i):
                    pool.wait_ge(a_srow, i)
                g.tensor_copy(sb, sel[r][:, :, TOPK:TOPK + 1].broadcast_to([TC, 2, 128])).then_inc(a_sb, 1)

            def B_prob(i):
                pool.wait_ge(b_inv, i + 1)
                g.tensor_tensor(pr, pr, einv.rearrange("p (t o) -> p t o", o=1).broadcast_to([QT, 3, NT]),
                                ALU.mult).then_inc(b_prob, 1)

            def B_res(i, r):
                pool.wait_ge(b_h, i + 1)
                pool.wait_ge(a_res, i + 1)
                if counts(i - 1):
                    pool.wait_ge(c_out, i - 1)
                g.tensor_tensor(rb[r], res[r], hh[r], ALU.add).then_inc(b_res, 1)

            def B_rstd(i):
                pool.wait_ge(b_var, i + 1)
                g.tensor_tensor(rs2, ve2, mhalf, ALU.pow).then_inc(b_rstd, 1)

            def step(i, r, on):
                nxt, a, b, b2, c = on
                q = 1 - r
                if a: A_rstd2(i)
                if b2: B_rstd(i - 2)
                if a: A_zb(i, r)
                if b: B_prob(i - 1)
                if b2: B_res(i - 2, r)
                if a: A_res(i, r)
                if nxt: A_rstd(i + 1)
                if a: A_sb(i, r)
            pool.wait_ge(fw_loaded, 16 * LOADS)
            pipeline(pool, step)

        @block.vector
        def _(dve):
            v = nc.vector

            def statistics(src, st, mv, ve, stats, mom, var, i):
                for c in range(2):
                    v.bn_stats(st[:, c], src[:, c]).then_inc(stats, 1)
                dve.wait_ge(stats, 2 * i + 2)
                dve.sem_inc(stats3_seen, 1)
                for c in range(2):
                    v.bn_aggr(mv[:, c], st[:, c]).then_inc(mom, 1)
                dve.wait_ge(mom, 2 * i + 2)
                v.tensor_scalar(ve, mv[:, :, 1], EPS, None, ALU.add).then_inc(var, 1)

            def less_mean(src, to, mv, gain, done):
                for c in range(2):
                    v.scalar_tensor_tensor(out=to[:, c], in0=src[:, c], scalar=mv[:, c, 0:1], in1=row[gain][0:TC],
                                           op0=ALU.subtract, op1=ALU.mult).then_inc(done, 1)

            def scaled(src, to, rs, shift, done):
                for c in range(2):
                    t = v.scalar_tensor_tensor(out=to[:, c], in0=src[:, c], scalar=rs[:, c:c + 1], in1=row[shift][0:TC],
                                               op0=ALU.mult, op1=ALU.add)
                t.then_inc(done, 1)

            def A_stats(i, r):
                dve.wait_ge(f_in[r], i * 8 + (16 - 8 * r))
                statistics(hc[r], st[0], mv[0], ve[0], a_stats, a_mom, a_var, i)

            def A_n0(i, r):
                if counts(i - 1):
                    dve.wait_ge(b_kept, i - 1)
                dve.wait_ge(a_rstd, i + 1)
                for c in range(2):
                    t = v.tensor_scalar(n0[r][:, c], hc[r][:, c], mv[0][:, c, 0:1], rs[0][:, c:c + 1],
                                        ALU.subtract, ALU.mult)
                t.then_inc(a_n0, 1)

            def A_stats2(i, r):
                dve.wait_ge(a_n0, i + 1)
                statistics(n0[r], st[1], mv[1], ve[1], a_stats2, a_mom2, a_var2, i)
                less_mean(n0[r], na, mv[1], "g1", a_ng)

            def A_n(i, r):
                dve.wait_ge(a_ng, 2 * i + 2)
                dve.wait_ge(a_rstd2, i + 1)
                if counts(i - 1):
                    dve.wait_ge(b_gat_ps, i - 1)
                scaled(na, nn[r], rs[1], "b1", a_n)

            def B_stats(i, r):
                dve.wait_ge(b_h, i + 1)
                statistics(hh[r], st3, mv3, ve2, b_stats, b_mom, b_var, i)
                less_mean(hh[r], hg, mv3, "g2", b_hg)

            def B_n2(i, r):
                dve.wait_ge(b_hg, 2 * i + 2)
                dve.wait_ge(b_rstd, i + 1)
                if counts(i - 1):
                    dve.wait_ge(c_n2T_ps, i - 1)
                scaled(hg, n2[r], rs2, "b2", b_n2)

            def A_z(i, r):
                dve.wait_ge(a_n, i + 1)
                if counts(i - 1):
                    dve.wait_ge(a_ez, i - 1)
                if counts(i - 1):
                    dve.wait_ge(a_zb, i - 1)
                if counts(4 * i):
                    dve.wait_ge(a_cnt, 4 * i)
                for c in range(2):
                    t = v.tensor_tensor_reduce(out=junk[:, c * D:(c + 1) * D], in0=nn[r][:, c], in1=row["Wr"][0:TC], scale=1.0,
                                               scalar=0.0, op0=ALU.mult, op1=ALU.add, accum_out=z[r][:, c:c + 1])
                t.then_inc(a_z, 1)

            def A_rank(i, r):
                dve.wait_ge(a_zrow, i + 1)
                zr = psum[0:TC, RB, 0:NT]
                for c in range(2):
                    v.tensor_scalar(cmp[c], zr, z[r][:, c:c + 1], None, ALU.is_lt, ALU.add,
                                    accum_out=lt[:, c:c + 1]).then_inc(a_cnt, 1)
                    v.scalar_tensor_tensor(out=cmp[2 + c], in0=zr, scalar=z[r][:, c:c + 1], in1=before[:, c], op0=ALU.is_equal,
                                           op1=ALU.mult, accum_out=eq[:, c:c + 1]).then_inc(a_cnt, 1)
                dve.wait_ge(a_cnt, 4 * i + 4)
                v.tensor_tensor(rank, lt, eq, ALU.add).then_inc(a_rank, 1)
                dve.wait_ge(a_rank, i + 1)
                for c in range(2):
                    v.tensor_scalar(sel[r][:, c, 0:TOPK], slots, rank[:, c:c + 1], None, ALU.is_equal).then_inc(a_sel, 1)
                    v.tensor_scalar(keep[r][:, c:c + 1], rank[:, c:c + 1], float(TOPK), None, ALU.is_ge).then_inc(a_sel, 1)

            def A_score(i, r):
                dve.wait_ge(a_ez, i + 1)
                v.tensor_scalar(ez1, ez, 1.0, None, ALU.add).then_inc(a_ez1, 1)
                dve.wait_ge(a_ez1, i + 1)
                v.reciprocal(sel[r][:, :, TOPK], ez1).then_inc(a_score, 1)

            def A_v(i, r):
                dve.wait_ge(a_v_ps, i + 1)
                v.tensor_tensor(vv[r], psum[0:TC, VB, 0:2 * D].rearrange("p (c n) -> p c n", c=2), rowc("bv"),
                                ALU.add).then_inc(a_v, 1)

            def B_gat(i, r):
                dve.wait_ge(b_gat_ps, i + 1)
                v.tensor_scalar(ssum, psum[:, SB, SS:SS + 1], 1e-6, None, ALU.add).then_inc(b_gat, 1)
                v.tensor_copy(nsel[0], psum[:, SB, GA:GA + TOPK]).then_inc(b_gat, 1)
                v.tensor_copy(nsel[1], psum[0:HI, SB, GB:GB + TOPK]).then_inc(b_gat, 1)
                v.tensor_copy(selT, psum[0:TOPK, SB, ST:ST + NT]).then_inc(b_gat, 1)
                dve.wait_ge(b_gat, 4 * i + 4)
                v.reciprocal(sinv, ssum).then_inc(b_sinv, 1)
                dve.wait_ge(b_sinv, i + 1)
                for (f, a, m), o in zip(feats, (GA, GB)):
                    v.tensor_tensor(pooled[f], psum[0:m, SB, o + TOPK:o + TOPK + 1], sinv[0:m], ALU.mult).then_inc(b_pool, 1)

            def B_q(i):
                dve.wait_ge(b_q_ps, i + 1)
                for (f, a, m), o in zip(feats, (QA, QB)):
                    v.tensor_scalar(qs[f], psum[0:m, SB, o:o + TOPK], col["bq"][f], DH3 ** -0.5, ALU.add,
                                    ALU.mult).then_inc(b_q, 1)
                dve.wait_ge(b_q, 2 * i + 2)
                for k, nh in ((0, 8), (1, 4)):
                    m = qs[k].shape[0]
                    v.tensor_tensor(qblk[k], qs[k].rearrange("p (o j) -> p o j", o=1).broadcast_to([m, nh, TOPK]),
                                    own[0:m, 0:nh].rearrange("p (h o) -> p h o", o=1).broadcast_to([m, nh, TOPK]),
                                    ALU.mult).then_inc(b_qblk, 1)

            def B_max(i):
                dve.wait_ge(b_log, i + 1)
                v.tensor_reduce(nmax[:, 0:2], psum[0:QT, L0, 0:2 * NT].rearrange("p (t n) -> p t n", t=2), AX.X, ALU.max,
                                negate=True).then_inc(b_max, 1)
                v.tensor_reduce(nmax[:, 2:3], psum[0:QT, L1, 0:NT], AX.X, ALU.max, negate=True).then_inc(b_max, 1)

            def B_inv(i):
                dve.wait_ge(b_exp, i + 1)
                v.reciprocal(einv, esum).then_inc(b_inv, 1)

            def B_mixT(i, r):
                dve.wait_ge(a_srow, i + 1)
                dve.wait_ge(a_nT, i + 1)
                dve.wait_ge(b_pool, 2 * i + 2)
                if counts(i):
                    dve.wait_ge(b_mix_ps, i)
                for f, a, m in feats:
                    t = v.scalar_tensor_tensor(out=mixT[f], in0=psum[0:m, RB, NT:2 * NT], scalar=pooled[f], in1=nT[r][f],
                                               op0=ALU.mult, op1=ALU.add)
                t.then_inc(b_mixT, 1)

            def B_mixb(i):
                dve.wait_ge(b_mix_ps, i + 1)
                v.tensor_tensor(mixb, psum[0:TC, UB, 0:2 * D].rearrange("p (c n) -> p c n", c=2), rowc("bm"),
                                ALU.add).then_inc(b_mixb, 1)

            def B_kept(i, r):
                dve.wait_ge(b_mixb, i + 1)
                for c in range(2):
                    t = v.scalar_tensor_tensor(out=kept_mix[:, c], in0=mixb[:, c], scalar=keep[r][:, c:c + 1], in1=n0[r][:, c],
                                               op0=ALU.mult, op1=ALU.add)
                t.then_inc(b_kept, 1)

            def B_av(i):
                dve.wait_ge(b_av_ps, i + 1)
                for k, nh in ((0, 8), (1, 4)):
                    m = qs[k].shape[0]
                    o = psum[0:m, KB, k * 8 * TOPK:k * 8 * TOPK + nh * TOPK].rearrange("p (h j) -> p h j", h=nh)
                    v.tensor_tensor(cm[k], o, own[0:m, 0:nh].rearrange("p (h o) -> p h o", o=1).broadcast_to([m, nh, TOPK]),
                                    ALU.mult).then_inc(b_av, 1)
                dve.wait_ge(b_av, 2 * i + 2)
                for k in range(2):
                    v.tensor_reduce(ctxT[k], cm[k].rearrange("p h j -> p j h"), AX.X, ALU.add).then_inc(b_ctx, 1)

            def B_asel(i):
                dve.wait_ge(b_wo_ps, i + 1)
                v.tensor_tensor(asel, psum[0:TOPK, SB, 0:D], row["bo"][0:TOPK], ALU.add).then_inc(b_asel, 1)

            def B_h(i, r):
                dve.wait_ge(b_sca_ps, i + 1)
                dve.wait_ge(b_kept, i + 1)
                if counts(i - 1):
                    dve.wait_ge(b_res, i - 1)
                v.tensor_tensor(hh[r], psum[0:TC, VB, 0:2 * D].rearrange("p (c n) -> p c n", c=2), kept_mix,
                                ALU.add).then_inc(b_h, 1)

            def C_out(i, r):
                dve.wait_ge(c_down, i + 1)
                dve.wait_ge(b_res, i + 1)
                if counts(i * 8 - 8 * r):
                    dve.wait_ge(f_out[r], i * 8 - 8 * r)
                v.tensor_tensor(oo[r], psum[0:TC, NTB, 0:2 * D].rearrange("p (c n) -> p c n", c=2), rb[r],
                                ALU.add).then_inc(c_out, 1)

            def step(i, r, on):
                nxt, a, b, b2, c = on
                q = 1 - r
                if b2: B_h(i - 2, r)
                if b: B_gat(i - 1, q)
                if a: A_stats2(i, r)
                if b: B_q(i - 1)
                if b: B_mixT(i - 1, q)
                if a: A_n(i, r)
                if b: B_max(i - 1)
                if a: A_z(i, r)
                if b2: B_stats(i - 2, r)
                if b: B_mixb(i - 1)
                if b: B_kept(i - 1, q)
                if b: B_inv(i - 1)
                if b2: B_n2(i - 2, r)
                if nxt: A_stats(i + 1, q)
                if a: A_rank(i, r)
                if nxt: A_n0(i + 1, q)
                if a: A_v(i, r)
                if a: A_score(i, r)
                if b: B_av(i - 1)
                if b: B_asel(i - 1)
                if c: C_out(i - 3, q)
            dve.wait_ge(fw_loaded, 16 * LOADS)
            v.memset(ones, 1.0).then_inc(f_const, 1)
            v.tensor_scalar(nbr, br, -1.0, None, ALU.mult).then_inc(f_const, 1)
            pipeline(dve, step)


def kept(nc, ctx):
    sb = lambda n, cols: ctx.enter_context(nc.sbuf_tensor("sb_" + n, [128, cols], F32))
    w = {}
    w["qkv_lo"], w["qkv_hi"] = sb("qkv_lo", 3 * H1 * DH1)[:], sb("qkv_hi", 3 * H1 * DH1)[0:HI + 1]
    w["proj"] = sb("proj", 6 * D)[:].rearrange("p (h n) -> p h n", h=6)
    w["projb_lo"], w["projb_hi"] = sb("projb_lo", 1)[:], sb("projb_hi", 1)[0:HI]
    w["ident"] = sb("ident", 128)[:]
    w["mhalf"] = sb("mhalf", CHUNKS)[:]
    w["kx"] = sb("kx", H1 * NT)[:].rearrange("p (h n) -> p h n", h=H1)
    w["vx"] = sb("vx", 2 * H1 * KQ)[0:TC].rearrange("p (c h d) -> p c h d", c=2, h=H1)
    for hs, nh in (("a", 8), ("b", 4)):
        for f, m in enumerate((LO, HI)):
            n = f"tw_{hs}{f}"
            w[n] = sb(n, 2 * nh * TAB)[0:m].rearrange("p (s i h) -> p s i h", s=2, h=nh)
            n = f"tz_{hs}{f}"
            w[n] = sb(n, 2 * nh * SLOT)[0:m].rearrange("p (s i h) -> p s i h", s=2, h=nh)
    w["pv_a"] = sb("pv_a", (ROWS + SIDE + 2) * D)[:].rearrange("p (g n) -> p g n", n=D)
    w["pv_b"] = sb("pv_b", (ROWS + 1) * D)[:].rearrange("p (g n) -> p g n", n=D)
    return w


def vit_block(nc, io, out, nimg):
    hA = nc.dram_tensor("h_by_class", [nimg * NT, D], F32).ap()
    h2 = nc.dram_tensor("h_attended", [nimg * NT, D], F32).ap()
    pv_rows = nc.dram_tensor("table_rows", [2, TAB, H1 * D], F32).ap()
    with ExitStack() as ctx:
        w = kept(nc, ctx)
        arena = ctx.enter_context(nc.sbuf_tensor("arena", [128, 31040], F32))[:]
        psum = ctx.enter_context(nc.psum_tensor("banks", [128, 8, 512], F32))
        tokenizer(nc, ctx, io, arena, psum, hA, nimg)
        attention_weights(nc, ctx, io, w, arena, psum, pv_rows)
        attention(nc, ctx, io, w, arena, psum, hA, h2, nimg)
        feed_forward(nc, ctx, io, arena, psum, h2, out, nimg)


def lay_out(x, tok_W, tok_b, qkv_w, proj_w, proj_b, tabs, ffn):
    import numpy as np
    n = x.shape[0]
    p = x.reshape(n, GP, P, GP, 2, P // 2, 3).transpose(0, 1, 3, 4, 2, 5, 6).reshape(n, GP, GP, PIX)

    def chunks(a, m):
        return a.reshape(-1, m, KT, 128).transpose(0, 3, 2, 1)
    e = GP - 1
    io = dict(
        xI=chunks(p[:, 1:e, 1:e].reshape(-1, PIX), 128).reshape(n // 8, 9, 128, KT, 128),
        xE=np.stack([chunks(a.reshape(-1, PIX), 96) for a in (p[:, 0, 1:e], p[:, e, 1:e], p[:, 1:e, 0], p[:, 1:e, e])]),
        xC=np.stack([chunks(a, n)[0] for a in (p[:, 0, 0], p[:, 0, e], p[:, e, 0], p[:, e, e])]),
        tokW=tok_W.reshape(P, 2, P // 2, 5, 3, D).transpose(3, 1, 0, 2, 4, 5).reshape(5, KT, 128, D).transpose(2, 0, 1, 3),
        tokb=tok_b)
    Q = H1 * DH1
    t = np.arange(NT)
    onehot = np.zeros((2 * SLOT, NT), np.float32)
    onehot[(t[1:] - 1) // SIDE, t[1:]] = 1
    onehot[SLOT + (t[1:] - 1) % SIDE, t[1:]] = 1
    first = np.zeros((1, GT), np.float32)
    first[0, ::NT] = 1
    side_by_side = lambda a, b: np.concatenate([np.pad(u.T, ((0, 0), (0, 1))) for u in (a, b)], 1)
    io.update(
        wq_d=qkv_w[:Q].reshape(H1, DH1, D).transpose(1, 0, 2).reshape(DH1, H1 * D),
        proj_d=proj_w.reshape(D, H1, DH1).transpose(2, 1, 0).reshape(DH1, H1 * D),
        tabk=side_by_side(*tabs[:2]), tabv=side_by_side(*tabs[2:]),
        t0=np.concatenate([u[0] for u in tabs]).reshape(1, 4 * DH1),
        qkvT=qkv_w.T, proj_p=proj_w.T.reshape(6, 128, D).transpose(1, 0, 2), projb=proj_b.reshape(D, 1),
        onehot=onehot, onehotT=onehot.T.reshape(2, TC, 2 * SLOT), first=first,
        ident=np.eye(128, dtype=np.float32), mhalf=np.full((128, CHUNKS), -0.5, np.float32),
        slots=np.tile(np.arange(TOPK, dtype=np.float32), (TC, 1)),
        before=(t[None] < t[:, None]).astype(np.float32).reshape(2, TC, NT).transpose(1, 0, 2),
        own=(np.arange(128)[:, None] // DH3 == np.arange(8)[None]).astype(np.float32))
    io.update(ffn)
    io["bf1"] = ffn["bf1"].reshape(FT, 128).T
    io["br"] = ffn["br"].reshape(1)
    return {k: np.ascontiguousarray(a) for k, a in io.items()}


def kernel(x, L0_tok_W, L0_tok_b, L0_attn_qkv_w, L0_attn_proj_w, L0_attn_proj_b, L0_attn_tab_kv, L0_attn_tab_kh,
           L0_attn_tab_vv, L0_attn_tab_vh, **ffn):
    import numpy as np
    import concourse.bacc as bacc
    from concourse.bass_utils import run_bass_kernel_spmd

    nimg = x.shape[0]
    ffn = {k.removeprefix("L0_ffn_"): np.asarray(a) for k, a in ffn.items()}
    arrays = lay_out(*(np.asarray(a) for a in (x, L0_tok_W, L0_tok_b, L0_attn_qkv_w, L0_attn_proj_w, L0_attn_proj_b)),
                     [np.asarray(a) for a in (L0_attn_tab_kv, L0_attn_tab_kh, L0_attn_tab_vv, L0_attn_tab_vh)], ffn)
    nc = bacc.Bacc("TRN2", target_bir_lowering=False, num_devices=1)
    io = {k: nc.dram_tensor("in_" + k, a.shape, F32, kind="ExternalInput").ap() for k, a in arrays.items()}
    out = nc.dram_tensor("out", [nimg * NT, D], F32, kind="ExternalOutput").ap()
    vit_block(nc, io, out, nimg)
    r = run_bass_kernel_spmd(nc, [{"in_" + k: a for k, a in arrays.items()}], core_ids=[0])
    return r.results[0]["out"].reshape(nimg, NT, D)
```

```python
from contextlib import ExitStack

import concourse.bass as bass
from concourse import mybir

F32 = mybir.dt.float32
ALU = mybir.AluOpType
ACT = mybir.ActivationFunctionType
AX = mybir.AxisListType
EPS = 1e-5

D = 192
LO, HI = 128, 64
IMG, P = 224, 16
GP = IMG // P
NT = GP * GP
TC = NT // 2
PIX = P * P * 3
KT = PIX // 128
H1, DH1 = 12, 64
SIDE = 13
ROWS = (NT - 1) // SIDE
IDX0 = 15
TAB = 31
SLOT = 16
KQ = DH1 + 2 * SLOT
GROUP = 8
GT = GROUP * NT
CHUNKS = 2 * GROUP


def counts(n):
    return not (isinstance(n, int) and n <= 0)


def tokenizer(nc, ctx, io, w, arena, psum, hA, nimg, aw_loaded):
    OCT = nimg // 8
    RING = 5
    NIN = 9
    off = [0]

    def take(cols):
        a = arena[:, off[0]:off[0] + cols]
        off[0] += cols
        return a

    wall = take(5 * KT * D).rearrange("p (v t n) -> p v t n", v=5, t=KT)
    CLS = ["mid", "top", "bot", "left", "right", "tl", "tr", "bl", "br"]
    wcls = {c: take(KT * D).rearrange("p (t n) -> p t n", t=KT) for c in CLS}
    xin = [take(KT * 128).rearrange("p (t m) -> p t m", t=KT) for _ in range(RING)]
    hout = [take(D) for _ in range(RING)]
    bias = take(D)
    sem = lambda n: ctx.enter_context(nc.semaphore(n))
    w_loaded, bias_loaded = [sem(f"w_loaded{n}") for n in range(5)], sem("tokb_loaded")
    x_loaded = [sem(f"x_loaded{i}") for i in range(RING)]
    tok_seen = sem("tok_seen")
    tok_psum, tok_done = sem("tok_psum"), sem("tok_done")
    h_stored = [sem(f"h_stored{i}") for i in range(RING)]
    w_mid, w_edges, w_corners = sem("w_mid"), sem("w_edges"), sem("w_corners")
    mid_part, edge_part, corner_part = sem("mid_part"), sem("edge_part"), sem("corner_part")
    edges_seen, corners_seen = sem("edges_seen"), sem("corners_seen")

    def octet():
        return [("mid", k, 128) for k in range(NIN)] + [(c, 0, 96) for c in CLS[1:5]]
    NCH = len(octet())
    corners = [(c, 0, nimg) for c in CLS[5:]]

    def x_src(cls, k, o):
        if cls == "mid":
            return io["xI"][o, k]
        if cls in CLS[1:5]:
            return io["xE"][CLS.index(cls) - 1, o]
        return io["xC"][CLS.index(cls) - 5]

    RE = nimg * 144
    RC = RE + 4 * nimg * 12

    def h_dst(cls, k, o, m):
        if cls == "mid":
            return hA[bass.ds(o * (NIN * 128) + k * 128, m), :]
        if cls in CLS[1:5]:
            return hA[bass.ds(o * 96 + RE + (CLS.index(cls) - 1) * nimg * 12, m), :]
        r = RC + (CLS.index(cls) - 5) * nimg
        return hA[r:r + m, :]

    USE = [len(range(s, NCH, RING)) for s in range(RING)]

    def uses(j, o):
        return o * USE[j % RING] + j // RING

    def freed(j, o):
        return o * NCH + (j - RING + 1 if j >= RING else 1 + max(range(j, NCH, RING)) - NCH)

    with nc.Block() as block:
        @block.sync
        def _(sp):
            for n in range(5):
                sp.dma_start(wall[:, n], io["tokW"][:, n]).then_inc(w_loaded[n], 16)
            sp.dma_start(bias, io["tokb"].partition_broadcast(128)).then_inc(bias_loaded, 16)

            def load(j, o, item):
                cls, k, m = item
                sp.dma_start(xin[j % RING][:, :, 0:m], x_src(cls, k, o)).then_inc(x_loaded[j % RING], 16)
            for j in range(RING):
                load(j, 0, octet()[j])

            def body(o, following):
                for j in range(RING, NCH):
                    sp.wait_ge(tok_psum, freed(j, o))
                    sp.sem_inc(tok_seen, 1)
                    load(j, o, octet()[j])
                for j in range(min(RING, len(following))):
                    sp.wait_ge(tok_psum, freed(j, o + 1))
                    sp.sem_inc(tok_seen, 1)
                    load(j, o + 1, following[j])
            body(0, octet())
            with sp.Fori(1, OCT - 1) as o:
                body(o, octet())
            body(OCT - 1, corners)

        @block.gpsimd
        def _(pool):
            load_attention_weights(pool, io, w, arena, aw_loaded)

        @block.tensor
        def _(pe):
            pe.wait_ge(w_mid, 1)

            def product(j, o, item):
                cls, k, m = item
                if cls == "top" and isinstance(o, int):
                    pe.wait_ge(w_edges, 1)
                if cls == "tl":
                    pe.wait_ge(w_corners, 1)
                pe.wait_ge(x_loaded[j % RING], 16 * (uses(j, o) + 1))
                if counts(freed(j, o)):
                    pe.wait_ge(tok_done, freed(j, o))
                for t in range(KT):
                    mm = nc.tensor.matmul(psum[0:m, j % RING, 0:D], xin[j % RING][:, t, 0:m], wcls[cls][:, t, :],
                                          start=(t == 0), stop=(t == KT - 1))
                mm.then_inc(tok_psum, 1)
            for j, item in enumerate(octet()):
                product(j, 0, item)
            with pe.Fori(1, OCT) as o:
                for j, item in enumerate(octet()):
                    product(j, o, item)
            for j, item in enumerate(corners):
                product(j, OCT, item)

        @block.vector
        def _(dve):
            v = nc.vector

            def class_sums(classes, partial, seen):
                n = 0
                for step in range(3):
                    for cls in classes:
                        top, bot = cls in ("top", "tl", "tr"), cls in ("bot", "bl", "br")
                        left, right = cls in ("left", "tl", "bl"), cls in ("right", "tr", "br")
                        for jh in range(2):
                            for ih in range(2):
                                crops = {1, 2, 3, 4}
                                if top and ih == 0:
                                    crops -= {2, 4}
                                if bot and ih == 1:
                                    crops -= {1, 3}
                                if left and jh == 0:
                                    crops -= {3, 4}
                                if right and jh == 1:
                                    crops -= {1, 2}
                                whole = (slice(0, 128), 3 * jh + 2 * ih)
                                half = (slice(64 * ih, 64 * ih + 64), 3 * jh + 1)
                                for ps, t in (whole, half):
                                    dst = wcls[cls][ps, t, :]
                                    if step == 0:
                                        if len(crops) == 4:
                                            v.tensor_copy(dst, wcls["mid"][ps, t, :]).then_inc(partial, 1)
                                        else:
                                            v.tensor_tensor(dst, wall[ps, 0, t, :], wall[ps, min(crops), t, :],
                                                            ALU.add).then_inc(partial, 1)
                                        n += 1
                                    elif step == 1 and len(crops) == 2:
                                        v.tensor_tensor(dst, dst, wall[ps, max(crops), t, :], ALU.add).then_inc(partial, 1)
                                        n += 1
                    dve.wait_ge(partial, n)
                    dve.sem_inc(seen, 1)

            mid = wcls["mid"]
            dve.wait_ge(w_loaded[0], 16)
            dve.wait_ge(w_loaded[1], 16)
            v.tensor_tensor(mid, wall[:, 0], wall[:, 1], ALU.add).then_inc(mid_part, 1)
            for n in range(2, 5):
                dve.wait_ge(w_loaded[n], 16)
                dve.wait_ge(mid_part, n - 1)
                v.tensor_tensor(mid, mid, wall[:, n], ALU.add).then_inc(mid_part, 1)
            dve.wait_ge(mid_part, 4)
            dve.sem_inc(w_mid, 1)
            class_sums(CLS[1:5], edge_part, edges_seen)
            dve.sem_inc(w_edges, 1)
            dve.wait_ge(bias_loaded, 16)

            def finish(j, o, item):
                m = item[2]
                dve.wait_ge(tok_psum, o * NCH + j + 1)
                if counts(uses(j, o)):
                    dve.wait_ge(h_stored[j % RING], 16 * uses(j, o))
                v.tensor_tensor(hout[j % RING][0:m], psum[0:m, j % RING, 0:D], bias[0:m], ALU.add).then_inc(tok_done, 1)
            for j, item in enumerate(octet()):
                finish(j, 0, item)
            class_sums(CLS[5:], corner_part, corners_seen)
            dve.sem_inc(w_corners, 1)
            with dve.Fori(1, OCT) as o:
                for j, item in enumerate(octet()):
                    finish(j, o, item)
            for j, item in enumerate(corners):
                finish(j, OCT, item)

        @block.scalar
        def _(act):
            def store(j, o, item):
                act.wait_ge(tok_done, o * NCH + j + 1)
                act.dma_start(h_dst(*item[:2], o, item[2]), hout[j % RING][0:item[2]]).then_inc(h_stored[j % RING], 16)
            for j, item in enumerate(octet()):
                store(j, 0, item)
            with act.Fori(1, OCT) as o:
                for j, item in enumerate(octet()):
                    store(j, o, item)
            for j, item in enumerate(corners):
                store(j, OCT, item)
            for s in range(RING):
                act.wait_ge(h_stored[s], 16 * (OCT * USE[s] + len(range(s, len(corners), RING))))


def h_loads(hA, nimg, dst, g):
    RE = nimg * 144
    RC = RE + 4 * nimg * 12
    out = []
    d = dst.rearrange("p (i c) n -> p i c n", i=GROUP)
    b0 = g * GROUP
    for c in range(2):
        for a in range(6):
            to = d[14 * (a + 1 - c) + 1:14 * (a + 1 - c) + 13, :, c, :]
            rows = hA[bass.ds(b0 * 144, GROUP * 144), :].rearrange("(i a b) n -> a b i n", i=GROUP, a=12)[6 * c + a]
            out.append((to, rows))
        e = RE + c * nimg * 12
        out.append((d[14 * 6 * c + 1:14 * 6 * c + 13, :, c, :],
                    hA[bass.ds(b0 * 12 + e, GROUP * 12), :].rearrange("(i b) n -> b i n", b=12)))
        for s in range(2):
            e = RE + (2 + s) * nimg * 12
            at = 14 * (1 - c) + 13 * s
            out.append((d[at:at + 14 * 5 + 1:14, :, c, :],
                        hA[bass.ds(b0 * 12 + e, GROUP * 12), :].rearrange("(i a) n -> a i n", i=GROUP)[6 * c:6 * c + 6]))
            r = RC + (2 * c + s) * nimg
            at = 14 * 6 * c + 13 * s
            out.append((d[at:at + 1, :, c, :], hA[bass.ds(b0 + r, GROUP), :].rearrange("(o i) n -> o i n", o=1)))
    return out


NL = 2 * (6 + 1 + 2 + 2)


def group_rows(arena):
    xT_lo, xT_hi = arena[:, 0:GT], arena[0:HI + 1, GT:2 * GT]
    hin = arena[:, 2 * GT:2 * GT + CHUNKS * D].rearrange("p (c n) -> p c n", c=CHUNKS)
    return xT_lo, xT_hi, hin


def weight_sources(arena):
    off = [arena.shape[1]]

    def take(cols):
        off[0] -= cols
        return arena[:, off[0]:off[0] + cols]
    wq_d = take(H1 * D)[0:DH1]
    proj_d = take(H1 * D)[0:DH1]
    tabk, tabv = take(2 * TAB)[0:DH1], take(2 * TAB)[0:DH1]
    t0 = take(4 * DH1)[64:65]
    pv_sb = take(H1 * D)[0:2 * TAB]
    return wq_d, proj_d, tabk, tabv, t0, pv_sb


N_EARLY = 15


def load_attention_weights(pool, io, w, arena, aw_loaded):
    wq_d, proj_d, tabk, tabv, t0, _ = weight_sources(arena)
    n = 0
    for dst, src in ((wq_d, io["wq_d"]), (proj_d, io["proj_d"]), (tabk, io["tabk"]), (tabv, io["tabv"]),
                     (w["qkv_lo"][:, :], io["qkvT"][0:LO, :]), (w["qkv_hi"][0:HI, :], io["qkvT"][LO:D, :]),
                     (w["proj"], io["proj_p"]), (w["projb_lo"], io["projb"][0:LO, :]),
                     (w["projb_hi"], io["projb"][LO:D, :]), (w["ident"], io["ident"]),
                     (t0, io["t0"]), (w["mhalf"], io["mhalf"])):
        pool.dma_start(dst, src).then_inc(aw_loaded, 16)
        n += 1
    pool.dma_start(w["kx"][DH1:KQ, :, :], bass.AP(tensor=io["onehot"].tensor, offset=0,
                                                  ap=[[NT, 2 * SLOT], [0, H1], [1, NT]])).then_inc(aw_loaded, 16)
    for c in range(2):
        pool.dma_start(w["vx"][:, c, :, DH1:KQ],
                       bass.AP(tensor=io["onehotT"].tensor, offset=c * TC * 2 * SLOT,
                               ap=[[2 * SLOT, TC], [0, H1], [1, 2 * SLOT]])).then_inc(aw_loaded, 16)
    n += 3
    assert n == N_EARLY


def attention_weights(nc, ctx, io, w, arena, psum, pv_rows, aw_loaded, hA, h_in, nimg):
    sem = lambda n: ctx.enter_context(nc.semaphore(n))
    built, tk_psum, tk_done = sem("aw_built"), sem("tabk_psum"), sem("tabk_done")
    tv_psum, tv_done, pv_stored, first_loaded = sem("tabv_psum"), sem("tabv_done"), sem("pv_stored"), sem("first_loaded")
    wq_d, proj_d, tabk, tabv, t0, pv_sb = weight_sources(arena)
    _, xT_hi, hin = group_rows(arena)

    with nc.Block() as block:
        @block.sync
        def _(sp):
            sp.dma_start(xT_hi[HI:HI + 1, :], io["first"]).then_inc(first_loaded, 16)
            for to, src in h_loads(hA, nimg, hin, 0):
                sp.dma_start(to, src).then_inc(h_in, 16)
            sp.wait_ge(tv_done, 6)
            sp.dma_start(pv_rows.rearrange("s i n -> (s i) n"), pv_sb).then_inc(pv_stored, 16)
            sp.wait_ge(pv_stored, 16)
            sp.wait_ge(first_loaded, 16)

        @block.tensor
        def _(pe):
            pe.wait_ge(aw_loaded, 16 * N_EARLY)
            for f, (a, m) in enumerate(((0, LO), (LO, HI))):
                for h in range(H1):
                    bank = f * 2 + h // 6
                    mm = nc.tensor.matmul(psum[0:m, bank, (h % 6) * 2 * TAB:(h % 6 + 1) * 2 * TAB],
                                          wq_d[:, h * D + a:h * D + a + m], tabk, start=True, stop=True)
            mm.then_inc(tk_psum, 1)
            for n in range(6):
                bank = 4 + n % 4
                if n >= 4:
                    pe.wait_ge(tv_done, n - 3)
                nc.tensor.matmul(psum[0:2 * TAB, bank, 0:2 * D], tabv, proj_d[:, n * 2 * D:(n + 1) * 2 * D],
                                 start=True, stop=True).then_inc(tv_psum, 1)

        @block.scalar
        def _(act):
            for n in range(6):
                act.wait_ge(tv_psum, n + 1)
                nc.scalar.copy(pv_sb[:, n * 2 * D:(n + 1) * 2 * D], psum[0:2 * TAB, 4 + n % 4, 0:2 * D]).then_inc(tv_done, 1)

        @block.vector
        def _(dve):
            v = nc.vector
            dve.wait_ge(aw_loaded, 16 * N_EARLY)
            scale = DH1 ** -0.5
            qcols = slice(0, H1 * DH1)
            v.tensor_scalar(w["qkv_lo"][:, qcols], w["qkv_lo"][:, qcols], scale, None, ALU.mult).then_inc(built, 1)
            v.tensor_scalar(w["qkv_hi"][0:HI, qcols], w["qkv_hi"][0:HI, qcols], scale, None, ALU.mult).then_inc(built, 1)
            v.memset(w["qkv_hi"][HI:HI + 1, qcols], 0.0).then_inc(built, 1)
            for n in range(2):
                dst = w["qkv_hi"][HI:HI + 1, (n + 1) * H1 * DH1:(n + 2) * H1 * DH1].rearrange("p (h d) -> p h d", h=H1)
                a, b = (t0[:, (2 * n + k) * DH1:(2 * n + k + 1) * DH1].rearrange("p (o d) -> p o d", o=1)
                        .broadcast_to([1, H1, DH1]) for k in range(2))
                v.tensor_tensor(dst, a, b, ALU.add).then_inc(built, 1)
            dve.wait_ge(tk_psum, 1)
            for f, m in enumerate((LO, HI)):
                for bank, nh, hs in ((0, 6, "a"), (1, 2, "a"), (1, 4, "b")):
                    h0 = 0 if nh != 4 else 2
                    src = psum[0:m, f * 2 + bank, h0 * 2 * TAB:(h0 + nh) * 2 * TAB]
                    src = src.rearrange("p (h s i) -> p s i h", h=nh, s=2)
                    d0 = 6 if nh == 2 else 0
                    for side in range(2):
                        dst = w[f"tw_{hs}{f}"][:, side, :, d0:d0 + nh]
                        v.tensor_scalar(dst, src[:, side], scale, None, ALU.mult).then_inc(tk_done, 1)
            dve.wait_ge(tk_done, 12)
            for f, m in enumerate((LO, HI)):
                for hs, nh in (("a", 8), ("b", 4)):
                    for side in range(2):
                        v.tensor_copy(w[f"tz_{hs}{f}"][:, side], w[f"tw_{hs}{f}"][:, side, 0:1, :]
                                      .broadcast_to([m, SLOT, nh])).then_inc(tk_done, 1)
            dve.wait_ge(tk_done, 20)
            dve.wait_ge(built, 5)


def attention(nc, ctx, io, w, arena, psum, pv_rows, hA, h_in, h2, nimg):
    NG = nimg // GROUP
    NH = GROUP * H1
    PER_BANK = 512 // (GROUP * ROWS)
    LN_FROM = NH // 2
    JOBS = 16
    sem = lambda n: ctx.enter_context(nc.semaphore(n))
    pv_loaded = sem("pv_loaded")
    h_again, h_out = sem("h_again"), sem("h2_stored")
    stats_seen, kb_seen = sem("stats_seen"), sem("kb_seen")
    stats, moments, var_eps, rstd_ok, xhat_ok = (sem(n) for n in ("stats", "moments", "var_eps", "rstd", "xhat"))
    xT_psum, xT_dve, xT_act = sem("xT_psum"), sem("xT_dve"), sem("xT_act")
    kb_psum, kb_dve, kb_act = sem("kb_psum"), sem("kb_dve"), sem("kb_act")
    kb_moved_a, kb_moved_b = sem("kb_moved_a"), sem("kb_moved_b")
    qk_psum, v_psum, qk_ok, v_ok = (sem(n) for n in ("qk_psum", "v_psum", "qk_ok", "v_ok"))
    logits, max_ok, exp_ok, recip_ok, prob_ok = (sem(n) for n in ("logits", "max_ok", "exp_ok", "recip_ok", "prob_ok"))
    pT_psum, pT_ok, o_psum, o_ok, a_ok = (sem(n) for n in ("pT_psum", "pT_ok", "o_psum", "o_ok", "a_ok"))
    a_moved_a, a_moved_b = sem("a_moved_a"), sem("a_moved_b")
    y_psum, y_ok, vb_psum, vb_ok, hT_psum, h2_ok = (sem(n) for n in ("y_psum", "y_ok", "vb_psum", "vb_ok", "hT_psum", "h2_ok"))

    off = [0]

    def take(cols):
        a = arena[:, off[0]:off[0] + cols]
        off[0] += cols
        return a
    xT_lo, xT_hi, hin = group_rows(arena)
    xT_lo, xT_hi = (a.rearrange("p (i n) -> p i n", i=GROUP) for a in (xT_lo, xT_hi))
    off[0] = 2 * GT + CHUNKS * D
    hres = take(CHUNKS * D).rearrange("p (c n) -> p c n", c=CHUNKS)
    st = take(CHUNKS * 6).rearrange("p (c n) -> p c n", c=CHUNKS)
    mv = take(CHUNKS * 2).rearrange("p (c n) -> p c n", c=CHUNKS)
    ve, rstd = take(CHUNKS), take(CHUNKS)
    kst = take(3 * GT).rearrange("p (t n) -> p t n", t=3)
    qx = take(H1 * NT).rearrange("p (h n) -> p h n", h=H1)
    prob = take(3 * 2 * NT).rearrange("p (b c n) -> p b c n", b=3, c=2)
    pT = take(2 * 2 * NT).rearrange("p (b c n) -> p b c n", b=2, c=2)
    nmax = take(3 * 2).rearrange("p (b c) -> p b c", b=3)
    psums = take(3 * 2).rearrange("p (b c) -> p b c", b=3)
    prec = take(3 * 2).rearrange("p (b c) -> p b c", b=3)
    oT = take(2 * 6 * NT).rearrange("p (b h n) -> p b h n", b=2, h=6)
    ast = take(H1 * NT).rearrange("p (h n) -> p h n", h=H1)
    ap = take(3 * GT).rearrange("p (t n) -> p t n", t=3)
    yT = take(2 * GT).rearrange("p (f n) -> p f n", f=2)
    assert off[0] <= arena.shape[1], off[0]
    kx, vx = w["kx"], w["vx"]
    QK, VB, L0, T0, O0 = 0, 1, 2, 4, 6

    def parts(side):
        n = ROWS if side == 0 else SIDE
        for q in range(0, n, PER_BANK):
            yield q + PER_BANK >= n, range(q, min(q + PER_BANK, n))

    def kb_jobs():
        for side in range(2):
            for hs, nh, p0 in (("a", 8, 0), ("b", 4, 64 * side)):
                for last, gs in parts(side):
                    yield side, hs, nh, p0, last, gs

    def tokens(a, side, gs):
        if side == 0:
            lo = 1 + SIDE * gs[0]
            return a[:, :, lo:lo + SIDE * len(gs)].rearrange("p i (g j) -> p g i j", g=len(gs))
        return a[:, :, 1:].rearrange("p i (j g) -> p g i j", g=SIDE)[:, gs[0]:gs[-1] + 1]

    def pair_use(u):
        return u + max(0, (u - 2) // 6)

    def y_use(i):
        return 7 * i + 8 if i < GROUP - 1 else 7 * i + 6

    def pair_bank(u):
        return O0 + pair_use(u) % 2

    def y_bank(i):
        return O0 + y_use(i) % 2
    USED = {pair_use(u): ("pair", u) for u in range(NH // 2)} | {y_use(i): ("y", i) for i in range(GROUP)}

    with nc.Block() as block:
        @block.sync
        def _(sp):
            def move(dst, src, s):
                sp.dma_start(dst, src).then_inc(s, 16)

            def bias_in(i, g):
                cols = slice(i * NT, (i + 1) * NT)
                if i == 0:
                    sp.wait_ge(kb_dve, JOBS // 2 * (g + 1))
                    sp.sem_inc(kb_seen, 1)
                    sp.wait_ge(kb_act, JOBS // 2 * (g + 1))
                    sp.sem_inc(kb_seen, 1)
                if counts(g * NH + (i * H1 - 4 if i else 0)):
                    sp.wait_ge(logits, g * NH + (i * H1 - 4 if i else 0))
                for side in range(2):
                    move(qx[DH1 + SLOT * side:DH1 + SLOT * (side + 1), 0:8, :], kst[:, side, cols], kb_moved_a)
                if counts(g * NH + i * H1):
                    sp.wait_ge(logits, g * NH + i * H1)
                move(qx[DH1:KQ, 8:H1, :], kst[:, 2, cols], kb_moved_b)

            def sums_out(i, g):
                cols = slice(i * NT, (i + 1) * NT)
                sp.wait_ge(a_ok, g * NH // 2 + (i * H1 + 8) // 2)
                for side in range(2):
                    move(ap[:, side, cols], ast[DH1 + SLOT * side:DH1 + SLOT * (side + 1), 0:8, :], a_moved_a)
                sp.wait_ge(a_ok, g * NH // 2 + (i + 1) * H1 // 2)
                move(ap[:, 2, cols], ast[DH1:KQ, 8:H1, :], a_moved_b)

            def table_loads(side):
                n = ROWS if side == 0 else SIDE
                row = H1 * D
                for dst, nh, h0 in ((w["pv_a"][:, side * (ROWS + 1):side * (ROWS + 1) + n + 1, :], 8, 0),
                                    (w["pv_b"][64 * side:64 * side + 64, 0:n + 1, :], 4, 8)):
                    base = side * TAB * row + h0 * D
                    for h in range(nh):
                        sp.dma_start(dst[h:h + nh * (SLOT - 1) + 1:nh, 0:n, :],
                                     bass.AP(tensor=pv_rows.tensor, offset=base + (IDX0 - n + 1) * row + h * D,
                                             ap=[[row, SLOT], [row, n], [1, D]])).then_inc(pv_loaded, 16)
                    sp.dma_start(dst[:, n, :], bass.AP(tensor=pv_rows.tensor, offset=base,
                                                       ap=[[0, SLOT], [D, nh], [1, D]])).then_inc(pv_loaded, 16)

            def group(g, first, last):
                bias_in(0, g)
                for i in range(GROUP):
                    if i + 1 < GROUP:
                        bias_in(i + 1, g)
                    sums_out(i, g)
                    if first and 1 <= i <= 2:
                        table_loads(i - 1)
                    if i == 0 and not last:
                        sp.wait_ge(xT_psum, GROUP * (g + 1))
                        for to, src in h_loads(hA, nimg, hin, g + 1):
                            sp.dma_start(to, src).then_inc(h_in, 16)
                    if i == 1:
                        if counts(16 * GROUP * g):
                            sp.wait_ge(h_out, 16 * GROUP * g)
                        for to, src in h_loads(hA, nimg, hres, g):
                            sp.dma_start(to, src).then_inc(h_again, 16)
                for i in range(GROUP):
                    sp.wait_ge(h2_ok, GROUP * g + i + 1)
                    sp.dma_start(h2[bass.ds(g * GT + i * NT, NT), :].rearrange("(c p) n -> p c n", p=TC),
                                 hres[0:TC, 2 * i:2 * i + 2, :]).then_inc(h_out, 16)
            group(0, True, False)
            with sp.Fori(1, NG - 1) as g:
                group(g, False, False)
            group(NG - 1, False, True)
            sp.wait_ge(h_out, 16 * GROUP * NG)

        @block.tensor
        def _(pe):
            mm = nc.tensor.matmul

            def transposes_in(g):
                for i in range(GROUP):
                    if counts(g):
                        pe.wait_ge(h2_ok, GROUP * g - (GROUP - 1) + i)
                    pe.wait_ge(xhat_ok, CHUNKS * g + 2 * (i + 1))
                    for c in range(2):
                        for f, (a, m) in enumerate(((0, LO), (LO, HI))):
                            t = nc.tensor.transpose(psum[0:m, i, (2 * f + c) * TC:(2 * f + c + 1) * TC],
                                                    hin[0:TC, 2 * i + c, a:a + m], w["ident"][0:TC, 0:TC])
                    t.then_inc(xT_psum, 1)

            def bias_rows(g):
                pe.wait_ge(xT_dve, GROUP // 2 * (g + 1))
                pe.wait_ge(xT_act, GROUP // 2 * (g + 1))
                for j, (side, hs, nh, p0, last, gs) in enumerate(kb_jobs()):
                    m = nh * SLOT
                    if j >= 8:
                        pe.wait_ge(kb_act if j % 2 else kb_dve, JOBS // 2 * g + (j - 8) // 2 + 1)
                    out = psum[p0:p0 + m, j % 8, :]
                    n = GROUP * (SIDE if side == 0 else ROWS)
                    for k, q in enumerate(gs):
                        for a, x in enumerate((xT_lo, xT_hi[0:HI])):
                            t = mm(out[:, k * n:(k + 1) * n], w[f"tw_{hs}{a}"][:, side, IDX0 - q:IDX0 - q + SLOT, :],
                                   tokens(x, side, [q])[:, 0], start=(a == 0), stop=(a == 1), skip_group_check=True)
                    if last:
                        k = len(gs)
                        for a, x in enumerate((xT_lo, xT_hi[0:HI])):
                            t = mm(out[:, k * n:k * n + GROUP], w[f"tz_{hs}{a}"][:, side], x[:, :, 0],
                                   start=(a == 0), stop=(a == 1), skip_group_check=True)
                    t.then_inc(kb_psum, 1)

            def project(g, i, p):
                u = 6 * (GROUP * g + i) + p
                if counts(u):
                    pe.wait_ge(qk_ok, u)
                for n in range(2):
                    cols = slice((n * H1 + 2 * p) * DH1, (n * H1 + 2 * p + 2) * DH1)
                    out = psum[:, QK, n * NT:(n + 1) * NT]
                    mm(out, w["qkv_lo"][:, cols], xT_lo[:, i, :], start=True, stop=False)
                    t = mm(out, w["qkv_hi"][:, cols], xT_hi[:, i, :], start=False, stop=True)
                t.then_inc(qk_psum, 1)
                if counts(u):
                    pe.wait_ge(v_ok, u)
                for c in range(2):
                    cols = slice((2 * H1 + 2 * p) * DH1, (2 * H1 + 2 * p + 2) * DH1)
                    out = psum[0:TC, VB, c * 2 * DH1:(c + 1) * 2 * DH1]
                    mm(out, xT_lo[:, i, c * TC:(c + 1) * TC], w["qkv_lo"][:, cols], start=True, stop=False)
                    t = mm(out, xT_hi[:, i, c * TC:(c + 1) * TC], w["qkv_hi"][:, cols], start=False, stop=True)
                t.then_inc(v_psum, 1)

            def make_logits(g, k):
                i, h = k // H1, k % H1
                pe.wait_ge(qk_ok, 6 * GROUP * g + k // 2 + 1)
                if h < 8:
                    pe.wait_ge(kb_moved_a, 16 * 2 * (GROUP * g + i + 1))
                else:
                    pe.wait_ge(kb_moved_b, 16 * (GROUP * g + i + 1))
                if counts(g * NH + max(k - 1, 0)):
                    pe.wait_ge(exp_ok, g * NH + max(k - 1, 0))
                for c in range(2):
                    t = mm(psum[0:TC, L0 + k % 2, c * NT:(c + 1) * NT], qx[0:KQ, h, c * TC:(c + 1) * TC], kx[0:KQ, h, :],
                           start=True, stop=True)
                t.then_inc(logits, 1)

            def turn(g, k):
                pe.wait_ge(prob_ok, g * NH + k + 1)
                if counts(g * NH + max(k - 1, 0)):
                    pe.wait_ge(pT_ok, g * NH + max(k - 1, 0))
                for c in range(2):
                    for kc in range(2):
                        t = nc.tensor.transpose(psum[0:TC, T0 + k % 2, kc * NT + c * TC:kc * NT + (c + 1) * TC],
                                                prob[0:TC, k % 3, c, kc * TC:(kc + 1) * TC], w["ident"][0:TC, 0:TC])
                t.then_inc(pT_psum, 1)

            def bank_taken(g, use):
                if use >= 2:
                    what, n = USED[use - 2]
                    if what == "pair":
                        pe.wait_ge(o_ok, g * NH // 2 + n + 1)
                        pe.wait_ge(a_ok, g * NH // 2 + n + 1)
                    else:
                        pe.wait_ge(y_ok, GROUP * g + n + 1)

            def weigh(g, k):
                pe.wait_ge(pT_ok, g * NH + k + 1)
                pe.wait_ge(v_ok, 6 * GROUP * g + k // 2 + 1)
                if k % 2 == 0:
                    bank_taken(g, pair_use(k // 2))
                for kc in range(2):
                    t = mm(psum[0:KQ, pair_bank(k // 2), (k % 2) * NT:(k % 2 + 1) * NT], vx[0:TC, kc, k % H1, :], pT[0:TC, k % 2, kc, :],
                           start=(kc == 0), stop=(kc == 1))
                t.then_inc(o_psum, 1)

            def output(g, i):
                pe.wait_ge(o_ok, g * NH // 2 + (i + 1) * 6)
                bank_taken(g, y_use(i))
                for f, (a, m) in enumerate(((0, LO), (LO, HI))):
                    for p in range(6):
                        t = mm(psum[0:m, y_bank(i), f * NT:(f + 1) * NT], w["proj"][:, p, a:a + m], oT[:, i % 2, p, :],
                               start=(p == 0), stop=(p == 5))
                t.then_inc(y_psum, 1)

            def value_tables(g):
                pe.wait_ge(a_moved_a, 16 * 2 * GROUP * (g + 1))
                pe.wait_ge(a_moved_b, 16 * GROUP * (g + 1))
                pe.wait_ge(y_ok, GROUP * (g + 1))
                pe.wait_ge(pv_loaded, 16 * 2 * (H1 + 2))
                j = 0
                for side in range(2):
                    n, each = (ROWS, SIDE) if side == 0 else (SIDE, ROWS)
                    at, bt = (ap[:, t, :].rearrange("p (i n) -> p i n", i=GROUP) for t in (side, 2))
                    bt = bt[64 * side:64 * side + 64]
                    for f, (a, m) in enumerate(((0, LO), (LO, HI))):
                        for last, gs in parts(side):
                            if j >= 8:
                                pe.wait_ge(vb_ok, JOBS * g + j - 7)
                            out = psum[0:m, j % 8, :]
                            for k, q in enumerate(gs):
                                o = out[:, k * GROUP * each:(k + 1) * GROUP * each]
                                mm(o, w["pv_a"][:, side * (ROWS + 1) + n - 1 - q, a:a + m], tokens(at, side, [q])[:, 0],
                                   start=True, stop=False, skip_group_check=True)
                                t = mm(o, w["pv_b"][64 * side:64 * side + 64, n - 1 - q, a:a + m], tokens(bt, side, [q])[:, 0],
                                       start=False, stop=True, skip_group_check=True)
                            if last:
                                k = len(gs) * GROUP * each
                                mm(out[:, k:k + GROUP], w["pv_a"][:, side * (ROWS + 1) + n, a:a + m], at[:, :, 0],
                                   start=True, stop=False, skip_group_check=True)
                                t = mm(out[:, k:k + GROUP], w["pv_b"][64 * side:64 * side + 64, n, a:a + m], bt[:, :, 0],
                                       start=False, stop=True, skip_group_check=True)
                            t.then_inc(vb_psum, 1)
                            j += 1

            def transposes_out(g):
                pe.wait_ge(vb_ok, JOBS * (g + 1))
                for i in range(GROUP):
                    for c in range(2):
                        for f, (a, m) in enumerate(((0, LO), (LO, HI))):
                            t = nc.tensor.transpose(psum[0:TC, i, c * D + a:c * D + a + m],
                                                    yT[0:m, f, i * NT + c * TC:i * NT + (c + 1) * TC],
                                                    w["ident"][0:m, 0:m])
                    t.then_inc(hT_psum, 1)

            def group(g):
                transposes_in(g)
                bias_rows(g)
                pe.wait_ge(kb_dve, JOBS // 2 * g + 5)
                pe.wait_ge(kb_act, JOBS // 2 * g + 5)
                for p in range(2):
                    project(g, 0, p)
                for s in range(NH + 7):
                    if s < NH:
                        make_logits(g, s)
                    if s < 4:
                        project(g, 0, s + 2)
                    if 0 <= s - 2 < NH:
                        turn(g, s - 2)
                    if 0 <= s - 3 < NH:
                        weigh(g, s - 3)
                    if s >= 5 and (s - 4) % 2 == 1:
                        i, p = (s - 4) // H1, (s - 4) % H1 // 2
                        if i + 1 < GROUP:
                            project(g, i + 1, p)
                    if s >= H1 + 6 and (s - 6) % H1 == 0:
                        output(g, (s - 6) // H1 - 1)
                value_tables(g)
                transposes_out(g)
            group(0)
            with pe.Fori(1, NG) as g:
                group(g)

        def take_xT(eng, copy, g, parity, done):
            for i in range(parity, GROUP, 2):
                eng.wait_ge(xT_psum, GROUP * g + i + 1)
                copy(xT_lo[:, i, :], psum[:, i, 0:NT])
                copy(xT_hi[0:HI, i, :], psum[0:HI, i, NT:2 * NT]).then_inc(done, 1)

        def kb_evacuate(eng, copy, g, parity, done):
            for j, (side, hs, nh, p0, last, gs) in enumerate(kb_jobs()):
                if j % 2 != parity:
                    continue
                eng.wait_ge(kb_psum, JOBS * g + j + 1)
                m, each = nh * SLOT, (SIDE if side == 0 else ROWS)
                tile = side if hs == "a" else 2
                dst = kst[p0:p0 + m, tile, :].rearrange("p (i n) -> p i n", i=GROUP)
                n = len(gs) * GROUP * each
                src = psum[p0:p0 + m, j % 8, 0:n].rearrange("p (g i j) -> p g i j", g=len(gs), i=GROUP)
                ins = copy(tokens(dst, side, gs), src)
                if last:
                    ins = copy(dst[:, :, 0], psum[p0:p0 + m, j % 8, n:n + GROUP])
                ins.then_inc(done, 1)

        @block.scalar
        def _(act):
            def take_v(g, i, p):
                u = 6 * (GROUP * g + i) + p
                act.wait_ge(v_psum, u + 1)
                nc.scalar.copy(vx[0:TC, :, 2 * p:2 * p + 2, 0:DH1],
                               psum[0:TC, VB, 0:4 * DH1].rearrange("p (c e d) -> p c e d", c=2, e=2)).then_inc(v_ok, 1)

            def exponent(g, k):
                act.wait_ge(max_ok, g * NH + k + 1)
                if counts(g * NH + max(k - 2, 0)):
                    act.wait_ge(pT_psum, g * NH + max(k - 2, 0))
                for c in range(2):
                    e = nc.scalar.activation(prob[0:TC, k % 3, c, :], psum[0:TC, L0 + k % 2, c * NT:(c + 1) * NT], ACT.Exp,
                                             bias=nmax[0:TC, k % 3, c:c + 1], accum_out=psums[0:TC, k % 3, c:c + 1])
                e.then_inc(exp_ok, 1)

            def take_out(g, u):
                i, p = u // 6, u % 6
                act.wait_ge(o_psum, g * NH + 2 * u + 2)
                if counts(GROUP * g + max(i - 1, 0)):
                    act.wait_ge(y_psum, GROUP * g + max(i - 1, 0))
                nc.scalar.copy(oT[0:DH1, i % 2, p, :], psum[0:DH1, pair_bank(u), 0:NT])
                nc.scalar.copy(oT[DH1:2 * DH1, i % 2, p, :], psum[0:DH1, pair_bank(u), NT:2 * NT]).then_inc(o_ok, 1)

            def group(g):
                take_xT(act, nc.scalar.copy, g, 1, xT_act)
                if counts(16 * 2 * GROUP * g):
                    act.wait_ge(kb_moved_a, 16 * 2 * GROUP * g)
                if counts(16 * GROUP * g):
                    act.wait_ge(kb_moved_b, 16 * GROUP * g)
                kb_evacuate(act, nc.scalar.copy, g, 1, kb_act)
                for p in range(2):
                    take_v(g, 0, p)
                for s in range(NH + 7):
                    if s < 4:
                        take_v(g, 0, s + 2)
                    if s < NH:
                        exponent(g, s)
                    if s >= 4 and (s - 4) % 2 == 0 and (s - 4) // 2 < NH // 2:
                        take_out(g, (s - 4) // 2)
                    if s >= 5 and (s - 4) % 2 == 1:
                        i, p = (s - 4) // H1, (s - 4) % H1 // 2
                        if i + 1 < GROUP:
                            take_v(g, i + 1, p)
            group(0)
            with act.Fori(1, NG) as g:
                group(g)

        @block.gpsimd
        def _(pool):
            def norm(g):
                pool.wait_ge(var_eps, g + 1)
                nc.gpsimd.tensor_tensor(rstd[0:TC], ve[0:TC], w["mhalf"][0:TC], ALU.pow).then_inc(rstd_ok, 1)
            norm(0)

            def group(g, last):
                for k in range(NH):
                    pool.wait_ge(recip_ok, g * NH + k + 1)
                    b = k % 3
                    pr = prob[0:TC, b]
                    nc.gpsimd.tensor_tensor(pr, pr, prec[0:TC, b].rearrange("p (c o) -> p c o", o=1)
                                            .broadcast_to([TC, 2, NT]), ALU.mult).then_inc(prob_ok, 1)
                    if k == LN_FROM + GROUP and not last:
                        norm(g + 1)
            group(0, False)
            with pool.Fori(1, NG - 1) as g:
                group(g, False)
            group(NG - 1, True)

        @block.vector
        def _(dve):
            v = nc.vector

            def ln_stats(g, i):
                if i == 0:
                    dve.wait_ge(h_in, 16 * NL * (g + 1))
                for c in (2 * i, 2 * i + 1):
                    v.bn_stats(st[0:TC, c], hin[0:TC, c]).then_inc(stats, 1)

            def ln_moments(g):
                dve.wait_ge(stats, CHUNKS * (g + 1))
                dve.sem_inc(stats_seen, 1)
                for c in range(CHUNKS):
                    v.bn_aggr(mv[0:TC, c], st[0:TC, c]).then_inc(moments, 1)
                dve.wait_ge(moments, CHUNKS * (g + 1))
                v.tensor_scalar(ve[0:TC], mv[0:TC, :, 1], EPS, None, ALU.add).then_inc(var_eps, 1)

            def ln_apply(g, i):
                if i == 0:
                    dve.wait_ge(rstd_ok, g + 1)
                for c in (2 * i, 2 * i + 1):
                    v.tensor_scalar(hin[0:TC, c], hin[0:TC, c], mv[0:TC, c, 0:1], rstd[0:TC, c:c + 1],
                                    ALU.subtract, ALU.mult).then_inc(xhat_ok, 1)

            def take_qk(g, i, p):
                dve.wait_ge(qk_psum, 6 * (GROUP * g + i) + p + 1)
                v.tensor_copy(qx[0:DH1, 2 * p, :], psum[0:DH1, QK, 0:NT])
                v.tensor_copy(qx[0:DH1, 2 * p + 1, :], psum[DH1:2 * DH1, QK, 0:NT])
                v.tensor_copy(kx[0:DH1, 2 * p, :], psum[0:DH1, QK, NT:2 * NT])
                v.tensor_copy(kx[0:DH1, 2 * p + 1, :], psum[DH1:2 * DH1, QK, NT:2 * NT]).then_inc(qk_ok, 1)

            def maximum(g, k):
                dve.wait_ge(logits, g * NH + k + 1)
                v.tensor_reduce(nmax[0:TC, k % 3], psum[0:TC, L0 + k % 2, 0:2 * NT].rearrange("p (c n) -> p c n", c=2),
                                AX.X, ALU.max, negate=True).then_inc(max_ok, 1)

            def reciprocals(g, k):
                dve.wait_ge(exp_ok, g * NH + k + 1)
                v.reciprocal(prec[0:TC, k % 3], psums[0:TC, k % 3]).then_inc(recip_ok, 1)

            def take_pT(g, k):
                dve.wait_ge(pT_psum, g * NH + k + 1)
                if counts(g * NH + max(k - 1, 0)):
                    dve.wait_ge(o_psum, g * NH + max(k - 1, 0))
                v.tensor_copy(pT[0:TC, k % 2], psum[0:TC, T0 + k % 2, 0:2 * NT].rearrange("p (c n) -> p c n", c=2)).then_inc(pT_ok, 1)

            def take_sums(g, u):
                i, p = u // 6, u % 6
                dve.wait_ge(o_psum, g * NH + 2 * u + 2)
                if p < 4:
                    if counts(16 * 2 * (GROUP * g + i)):
                        dve.wait_ge(a_moved_a, 16 * 2 * (GROUP * g + i))
                else:
                    if counts(16 * (GROUP * g + i)):
                        dve.wait_ge(a_moved_b, 16 * (GROUP * g + i))
                v.tensor_copy(ast[DH1:KQ, 2 * p:2 * p + 2, :],
                              psum[DH1:KQ, pair_bank(u), 0:2 * NT].rearrange("p (e n) -> p e n", e=2)).then_inc(a_ok, 1)

            def take_y(g, i):
                dve.wait_ge(y_psum, GROUP * g + i + 1)
                if counts(GROUP * g):
                    dve.wait_ge(hT_psum, GROUP * g)
                c = slice(i * NT, (i + 1) * NT)
                v.tensor_scalar(yT[:, 0, c], psum[:, y_bank(i), 0:NT], w["projb_lo"], None, ALU.add)
                v.tensor_scalar(yT[0:HI, 1, c], psum[0:HI, y_bank(i), NT:2 * NT], w["projb_hi"], None, ALU.add).then_inc(y_ok, 1)

            def add_tables(g):
                j = 0
                for side in range(2):
                    n, each = (ROWS, SIDE) if side == 0 else (SIDE, ROWS)
                    for f, m in enumerate((LO, HI)):
                        for last, gs in parts(side):
                            dve.wait_ge(vb_psum, JOBS * g + j + 1)
                            dve.wait_ge(y_ok, GROUP * (g + 1))
                            if side:
                                dve.wait_ge(vb_ok, JOBS * g + JOBS // 2)
                            y = yT[0:m, f, :].rearrange("p (i n) -> p i n", i=GROUP)
                            k = len(gs) * GROUP * each
                            src = psum[0:m, j % 8, 0:k].rearrange("p (g i j) -> p g i j", g=len(gs), i=GROUP)
                            ins = v.tensor_tensor(tokens(y, side, gs), src, tokens(y, side, gs), ALU.add)
                            if last:
                                ins = v.tensor_tensor(y[:, :, 0], psum[0:m, j % 8, k:k + GROUP], y[:, :, 0], ALU.add)
                            ins.then_inc(vb_ok, 1)
                            j += 1

            def residual(g):
                dve.wait_ge(h_again, 16 * NL * (g + 1))
                for i in range(GROUP):
                    dve.wait_ge(hT_psum, GROUP * g + i + 1)
                    r = hres[0:TC, 2 * i:2 * i + 2, :]
                    v.tensor_tensor(r, psum[0:TC, i, 0:2 * D].rearrange("p (c n) -> p c n", c=2), r, ALU.add).then_inc(h2_ok, 1)

            for i in range(GROUP):
                ln_stats(0, i)
            ln_moments(0)
            for i in range(GROUP):
                ln_apply(0, i)

            def group(g, last):
                take_xT(dve, v.tensor_copy, g, 0, xT_dve)
                if counts(16 * 2 * GROUP * g):
                    dve.wait_ge(kb_moved_a, 16 * 2 * GROUP * g)
                if counts(16 * GROUP * g):
                    dve.wait_ge(kb_moved_b, 16 * GROUP * g)
                kb_evacuate(dve, v.tensor_copy, g, 0, kb_dve)
                for p in range(2):
                    take_qk(g, 0, p)
                for s in range(NH + 7):
                    if 0 <= s - 1 < NH:
                        reciprocals(g, s - 1)
                    if s < NH:
                        maximum(g, s)
                    if s < 4:
                        take_qk(g, 0, s + 2)
                    if 0 <= s - 2 < NH:
                        take_pT(g, s - 2)
                    if s >= 4 and (s - 4) % 2 == 0 and (s - 4) // 2 < NH // 2:
                        take_sums(g, (s - 4) // 2)
                    if s >= 5 and (s - 4) % 2 == 1:
                        i, p = (s - 4) // H1, (s - 4) % H1 // 2
                        if i + 1 < GROUP:
                            take_qk(g, i + 1, p)
                    if s >= H1 + 6 and (s - 6) % H1 == 0:
                        take_y(g, (s - 6) // H1 - 1)
                    if not last and 0 <= s - LN_FROM < GROUP:
                        ln_stats(g + 1, s - LN_FROM)
                    if not last and s == LN_FROM + GROUP:
                        ln_moments(g + 1)
                    if not last and 0 <= s - LN_FROM - GROUP - 4 < GROUP:
                        ln_apply(g + 1, s - LN_FROM - GROUP - 4)
                add_tables(g)
                residual(g)
            group(0, False)
            with dve.Fori(1, NG - 1) as g:
                group(g, False)
            group(NG - 1, True)



TOPK = max(1, int(round(0.15 * NT)))
DH3 = D // H1
F = 4 * D
FT = F // 128
HQ = 4
QT = HQ * TOPK


def feed_forward(nc, ctx, io, arena, psum, h2, out, nimg):
    def sems(*names):
        return [ctx.enter_context(nc.semaphore(n)) for n in names]
    off = [0]

    def take(cols):
        a = arena[:, off[0]:off[0] + cols]
        off[0] += cols
        return a

    def two(cols):
        return [take(cols) for _ in range(2)]

    def tok(cols=D):
        return [take(2 * cols)[0:TC].rearrange("p (c n) -> p c n", c=2) for _ in range(2)]
    W = {}
    for n in ("Wq", "Wk", "Wv", "Wo", "Wm", "W1"):
        c = F if n == "W1" else D
        W[n] = (take(c), take(c)[0:HI])
    W2 = take(FT * D).rearrange("p (t n) -> p t n", t=FT)
    row = {n: take(D) for n in ("g1", "b1", "g2", "b2", "Wr", "bv", "bo", "bm", "bf2")}
    col = {n: (take(1), take(1)[0:HI]) for n in ("bq", "bk")}
    bf1, br = take(FT), take(1)
    nbr = take(1)
    ident, ones = take(128), take(128)
    slots = take(TOPK)[0:TC]
    before = take(2 * NT)[0:TC].rearrange("p (c n) -> p c n", c=2)
    own = take(8)
    mhalf = take(2)[0:TC]
    hc, n0, nn = tok(), tok(), tok()
    res, rb = tok(), tok()
    st = [take(12)[0:TC].rearrange("p (c n) -> p c n", c=2) for _ in range(2)]
    mv = [take(4)[0:TC].rearrange("p (c n) -> p c n", c=2) for _ in range(2)]
    ve, rs = [a[0:TC] for a in two(2)], [a[0:TC] for a in two(2)]
    st3 = take(12)[0:TC].rearrange("p (c n) -> p c n", c=2)
    mv3 = take(4)[0:TC].rearrange("p (c n) -> p c n", c=2)
    ve2, rs2 = take(2)[0:TC], take(2)[0:TC]
    cmp = [take(NT)[0:TC] for _ in range(4)]
    z = [a[0:TC] for a in two(2)]
    ez, ez1 = take(2)[0:TC], take(2)[0:TC]
    sel = [take(2 * (TOPK + 1))[0:TC].rearrange("p (c n) -> p c n", c=2) for _ in range(2)]
    zb = take(2 * TC)[0:TC].rearrange("p (c n) -> p c n", c=2)
    sb = take(2 * 128)[0:TC].rearrange("p (c n) -> p c n", c=2)
    junk = take(2 * D)[0:TC]
    lt, eq, rank = take(2)[0:TC], take(2)[0:TC], take(2)[0:TC]
    keep = [a[0:TC] for a in two(2)]
    nT = [(take(NT), take(NT)[0:HI]) for _ in range(2)]
    kT = [(take(NT), take(NT)[0:HI]) for _ in range(2)]
    vv = tok()
    nsel = (take(TOPK), take(TOPK)[0:HI])
    ssum, sinv = take(1), take(1)
    pooled = (take(1), take(1)[0:HI])
    selT = take(NT)[0:TOPK]
    qs = (take(TOPK), take(TOPK)[0:HI])
    qblk = (take(8 * TOPK).rearrange("p (h j) -> p h j", h=8), take(4 * TOPK)[0:HI].rearrange("p (h j) -> p h j", h=4))
    nmax, esum, einv = take(3)[0:QT], take(3)[0:QT], take(3)[0:QT]
    pr = take(3 * NT)[0:QT].rearrange("p (t n) -> p t n", t=3)
    pT = take(2 * 3 * QT)[0:TC].rearrange("p (c n) -> p c n", c=2)
    cm = (take(8 * TOPK).rearrange("p (h j) -> p h j", h=8), take(4 * TOPK)[0:HI].rearrange("p (h j) -> p h j", h=4))
    ctxT = (take(TOPK), take(TOPK)[0:HI])
    asel = take(D)[0:TOPK]
    mixT = (take(NT), take(NT)[0:HI])
    mixb, kept_mix = take(2 * D)[0:TC].rearrange("p (c n) -> p c n", c=2), take(2 * D)[0:TC].rearrange("p (c n) -> p c n", c=2)
    hh, n2 = tok(), tok()
    na, hg = tok()
    n2T = (take(NT), take(NT)[0:HI])
    gT = take(FT * NT).rearrange("p (t n) -> p t n", t=FT)
    oo = tok()
    assert off[0] <= arena.shape[1], off[0]
    NTB, RB, SB, KB, VB, L0, L1, UB = range(8)
    GA, GB, SS, ST, QA, QB = 0, 32, 64, 96, 300, 332
    feats = ((0, 0, LO), (1, LO, HI))

    stats3_seen, f_const = sems("stats3_seen", "f_const")
    vectors_loaded, weights_loaded = sems("f_vectors_loaded", "f_weights_loaded")
    f_in, f_out = sems("f_in0", "f_in1"), sems("f_out0", "f_out1")
    a_stats, a_mom, a_var, a_rstd, a_n0 = sems("a_stats", "a_mom", "a_var", "a_rstd", "a_n0")
    a_stats2, a_mom2, a_var2, a_rstd2 = sems("a_stats2", "a_mom2", "a_var2", "a_rstd2")
    a_ng, a_n, a_res = sems("a_ng", "a_n", "a_res")
    a_z, a_ez, a_ez1, a_score = sems("a_z", "a_ez", "a_ez1", "a_score")
    a_zb, a_sb, a_zrow, a_srow = sems("a_zb", "a_sb", "a_zrow", "a_srow")
    a_cnt, a_rank, a_sel = sems("a_cnt", "a_rank", "a_sel")
    a_nT_ps, a_nT, a_k_ps, a_k, a_v_ps, a_v = sems("a_nT_ps", "a_nT", "a_k_ps", "a_k", "a_v_ps", "a_v")
    b_gat_ps, b_gat, b_sinv, b_pool = sems("b_gat_ps", "b_gat", "b_sinv", "b_pool")
    b_q_ps, b_q, b_qblk, b_log = sems("b_q_ps", "b_q", "b_qblk", "b_log")
    b_max, b_exp, b_inv, b_prob = sems("b_max", "b_exp", "b_inv", "b_prob")
    b_pT_ps, b_pT, b_av_ps, b_av, b_ctx = sems("b_pT_ps", "b_pT", "b_av_ps", "b_av", "b_ctx")
    b_wo_ps, b_asel, b_sca_ps, b_h, b_res = sems("b_wo_ps", "b_asel", "b_sca_ps", "b_h", "b_res")
    b_mixT, b_mix_ps, b_mixb, b_kept = sems("b_mixT", "b_mix_ps", "b_mixb", "b_kept")
    b_stats, b_mom, b_var, b_rstd = sems("b_stats", "b_mom", "b_var", "b_rstd")
    b_hg, b_n2 = sems("b_hg", "b_n2")
    c_n2T_ps, c_n2T, c_down, c_out = sems("c_n2T_ps", "c_n2T", "c_down", "c_out")
    c_up, c_g = sems("c_up0", "c_up1", "c_up2"), sems("c_g0", "c_g1", "c_g2")
    mm, tr = nc.tensor.matmul, nc.tensor.transpose

    def images(n):
        return min(n, nimg) if isinstance(n, int) else n

    def pipeline(eng, step):
        def peeled(i):
            step(i, i % 2, [0 <= i - k < nimg for k in range(-1, 4)])
        for i in range(-1, 6):
            peeled(i)
        with eng.Fori(3, nimg // 2 - 1) as u:
            for r in range(2):
                step(u * 2 + r, r, [True] * 5)
        for i in range(nimg - 2, nimg + 3):
            peeled(i)

    with nc.Block() as block:
        VECTORS = len(row) + 4 + 7
        WEIGHTS = 12 + 1

        @block.sync
        def _(sp):
            def step(i, r, on):
                if on[0]:
                    if counts(i):
                        sp.wait_ge(a_res, i)
                        sp.wait_ge(a_n0, i)
                    src = h2[bass.ds((i + 1) * NT, NT), :].rearrange("(c p) n -> p c n", p=TC)
                    sp.dma_start(hc[1 - r], src).then_inc(f_in[1 - r], 16)
                if on[4]:
                    sp.wait_ge(c_out, i - 2)
                    dst = out[bass.ds((i - 3) * NT, NT), :].rearrange("(c p) n -> p c n", p=TC)
                    sp.dma_start(dst, oo[1 - r]).then_inc(f_out[1 - r], 16)
            pipeline(sp, step)
            for r in range(2):
                sp.wait_ge(f_out[r], 16 * (nimg // 2))

        @block.tensor
        def _(pe):
            def A_turn(i, r):
                pe.wait_ge(a_n, i + 1)
                if counts(i - 2):
                    pe.wait_ge(c_n2T, i - 2)
                for f, a, m in feats:
                    for c in range(2):
                        t = tr(psum[0:m, NTB, f * NT + c * TC:f * NT + (c + 1) * TC], nn[r][:, c, a:a + m], ident[0:TC, 0:TC])
                t.then_inc(a_nT_ps, 1)

            def A_zrow(i, r):
                pe.wait_ge(a_zb, i + 1)
                if counts(i):
                    pe.wait_ge(b_mixT, i)
                for c in range(2):
                    t = tr(psum[0:TC, RB, c * TC:(c + 1) * TC], zb[:, c, :], ident[0:TC, 0:TC])
                t.then_inc(a_zrow, 1)

            def A_srow(i, r):
                pe.wait_ge(a_sb, i + 1)
                pe.wait_ge(a_cnt, 4 * i + 4)
                for c in range(2):
                    t = tr(psum[:, RB, NT + c * TC:NT + (c + 1) * TC], sb[:, c, :], ident[0:TC, 0:TC])
                t.then_inc(a_srow, 1)

            def A_k(i, r):
                pe.wait_ge(a_nT, i + 1)
                if counts(i * 2 - 2):
                    pe.wait_ge(b_av, i * 2 - 2)
                if counts(i - 2):
                    pe.wait_ge(c_g[1], i - 2)
                for f, a, m in feats:
                    o = psum[0:m, KB, f * NT:(f + 1) * NT]
                    mm(o, W["Wk"][0][:, a:a + m], nT[r][0], start=True, stop=False)
                    t = mm(o, W["Wk"][1][:, a:a + m], nT[r][1], start=False, stop=True)
                t.then_inc(a_k_ps, 1)

            def A_v(i, r):
                if counts(i - 1):
                    pe.wait_ge(b_h, i - 1)
                for c in range(2):
                    o = psum[0:TC, VB, c * D:(c + 1) * D]
                    mm(o, nT[r][0][:, c * TC:(c + 1) * TC], W["Wv"][0], start=True, stop=False)
                    t = mm(o, nT[r][1][:, c * TC:(c + 1) * TC], W["Wv"][1], start=False, stop=True)
                t.then_inc(a_v_ps, 1)

            def B_gather(i, r):
                pe.wait_ge(a_sel, 4 * i + 4)
                pe.wait_ge(a_score, i + 1)
                if counts(i):
                    pe.wait_ge(b_asel, i)
                for (f, a, m), o in zip(feats, (GA, GB)):
                    for c in range(2):
                        mm(psum[0:m, SB, o:o + TOPK + 1], nn[r][:, c, a:a + m], sel[r][:, c, :],
                           start=(c == 0), stop=(c == 1))
                for c in range(2):
                    mm(psum[:, SB, SS:SS + 1], ones[0:TC, :], sel[r][:, c, TOPK:TOPK + 1], start=(c == 0), stop=(c == 1))
                for c in range(2):
                    t = tr(psum[0:TOPK, SB, ST + c * TC:ST + (c + 1) * TC], sel[r][:, c, 0:TOPK], ident[0:TC, 0:TC])
                t.then_inc(b_gat_ps, 1)

            def B_q(i, r):
                pe.wait_ge(b_gat, 4 * i + 4)
                pe.wait_ge(b_pool, 2 * i + 2)
                for (f, a, m), o in zip(feats, (QA, QB)):
                    for k in range(2):
                        t = mm(psum[0:m, SB, o:o + TOPK], W["Wq"][k][:, a:a + m], nsel[k], start=(k == 0), stop=(k == 1))
                t.then_inc(b_q_ps, 1)

            def B_logits(i, r):
                pe.wait_ge(b_qblk, 2 * i + 2)
                pe.wait_ge(a_k, i + 1)
                if counts(i):
                    pe.wait_ge(b_pT, i)
                for t3 in range(3):
                    k, h = (0, HQ * t3) if t3 < 2 else (1, 0)
                    o = psum[0:QT, L0 if t3 < 2 else L1, (t3 % 2) * NT:(t3 % 2 + 1) * NT]
                    t = mm(o, qblk[k][:, h:h + HQ, :], kT[r][k], start=True, stop=True)
                t.then_inc(b_log, 1)

            def B_turn(i, r):
                pe.wait_ge(b_prob, i + 1)
                for c in range(2):
                    for t3 in range(3):
                        t = tr(psum[0:TC, L0 + c, t3 * QT:(t3 + 1) * QT], pr[:, t3, c * TC:(c + 1) * TC], ident[0:QT, 0:QT])
                t.then_inc(b_pT_ps, 1)

            def B_av(i, r):
                pe.wait_ge(b_pT, i + 1)
                pe.wait_ge(a_v, i + 1)
                pe.wait_ge(a_k, images(i + 2))
                for k, (f, a, m) in enumerate(feats):
                    w_ = (8 if k == 0 else 4) * TOPK
                    for c in range(2):
                        t = mm(psum[0:m, KB, k * 8 * TOPK:k * 8 * TOPK + w_], vv[r][:, c, a:a + m],
                               pT[:, c, k * 8 * TOPK:k * 8 * TOPK + w_], start=(c == 0), stop=(c == 1))
                t.then_inc(b_av_ps, 1)

            def B_wo(i, r):
                pe.wait_ge(b_ctx, 2 * i + 2)
                for k in range(2):
                    t = mm(psum[0:TOPK, SB, 0:D], ctxT[k], W["Wo"][k], start=(k == 0), stop=(k == 1))
                t.then_inc(b_wo_ps, 1)

            def B_scatter(i, r):
                pe.wait_ge(b_asel, i + 1)
                pe.wait_ge(a_v, images(i + 2))
                for c in range(2):
                    t = mm(psum[0:TC, VB, c * D:(c + 1) * D], selT[:, c * TC:(c + 1) * TC], asel, start=True, stop=True)
                t.then_inc(b_sca_ps, 1)

            def B_mix(i, r):
                pe.wait_ge(b_mixT, i + 1)
                if counts(i - 1):
                    pe.wait_ge(c_g[2], i - 1)
                for c in range(2):
                    for k in range(2):
                        t = mm(psum[0:TC, UB, c * D:(c + 1) * D], mixT[k][:, c * TC:(c + 1) * TC], W["Wm"][k],
                               start=(k == 0), stop=(k == 1))
                t.then_inc(b_mix_ps, 1)

            def C_turn(i, r):
                pe.wait_ge(b_n2, i + 1)
                if counts(i):
                    pe.wait_ge(c_out, i)
                for f, a, m in feats:
                    for c in range(2):
                        t = tr(psum[0:m, NTB, f * NT + c * TC:f * NT + (c + 1) * TC], n2[r][:, c, a:a + m], ident[0:TC, 0:TC])
                t.then_inc(c_n2T_ps, 1)

            def C_up(i, r, n):
                pe.wait_ge(c_n2T, i + 1)
                if n == 0:
                    pe.wait_ge(b_mixb, images(i + 2))
                if n == 1:
                    pe.wait_ge(b_av, 2 * images(i + 2))
                if n == 2:
                    pe.wait_ge(c_g[0], i + 1)
                for e in range(2):
                    o = psum[:, (UB, KB, UB)[n], e * NT:(e + 1) * NT]
                    cols = slice((2 * n + e) * 128, (2 * n + e + 1) * 128)
                    mm(o, W["W1"][0][:, cols], n2T[0], start=True, stop=False)
                    t = mm(o, W["W1"][1][:, cols], n2T[1], start=False, stop=True)
                t.then_inc(c_up[n], 1)

            def C_down(i, r, c, ts):
                pe.wait_ge(c_g[2], i + 1)
                pe.wait_ge(c_g[1], i + 1)
                pe.wait_ge(a_nT, images(i + 4))
                for t3 in ts:
                    t = mm(psum[0:TC, NTB, c * D:(c + 1) * D], gT[:, t3, c * TC:(c + 1) * TC], W2[:, t3, :],
                           start=(t3 == 0), stop=(t3 == FT - 1))
                if c == 1 and ts[-1] == FT - 1:
                    t.then_inc(c_down, 1)

            def step(i, r, on):
                nxt, a, b, b2, c = on
                q = 1 - r
                if c: C_turn(i - 3, q)
                if b: B_gather(i - 1, q)
                if c: C_up(i - 3, q, 0)
                if b: B_q(i - 1, q)
                if c: C_up(i - 3, q, 1)
                if c: C_up(i - 3, q, 2)
                if b: B_logits(i - 1, q)
                if a: A_turn(i, r)
                if b: B_mix(i - 1, q)
                if a: A_k(i, r)
                if a: A_zrow(i, r)
                if a: A_v(i, r)
                if b: B_turn(i - 1, q)
                if c: C_down(i - 3, q, 0, range(0, 3))
                if b: B_av(i - 1, q)
                if c: C_down(i - 3, q, 0, range(3, 6))
                if c: C_down(i - 3, q, 1, range(0, 4))
                if b: B_wo(i - 1, q)
                if c: C_down(i - 3, q, 1, range(4, 6))
                if b: B_scatter(i - 1, q)
                if a: A_srow(i, r)
            pe.wait_ge(vectors_loaded, 16 * VECTORS)
            pe.wait_ge(weights_loaded, 16 * WEIGHTS)
            pe.wait_ge(f_const, 2)
            pipeline(pe, step)

        @block.scalar
        def _(act):
            sa, cp = nc.scalar.activation, nc.scalar.copy
            vectors = [(mhalf, io["mhalf"][0:TC, 0:2])]
            vectors += [(row[name], io[name].partition_broadcast(128)) for name in row]
            vectors += [(ident, io["ident"]), (br, io["br"].partition_broadcast(128)), (bf1, io["bf1"]),
                        (slots, io["slots"]), (before, io["before"]), (own, io["own"])]
            vectors += [(col[name][f], io[name].rearrange("(n o) -> n o", o=1)[a:a + m, :])
                        for name in col for f, a, m in feats]
            assert len(vectors) == VECTORS
            for dst, src in vectors:
                act.dma_start(dst, src).then_inc(vectors_loaded, 16)
            weights = [(W[name][f], io[name][a:a + m, :]) for name in ("Wk", "Wv", "Wq", "Wm", "Wo", "W1") for f, a, m in feats]
            weights += [(W2, io["W2"].rearrange("(t p) n -> p t n", t=FT))]
            assert len(weights) == WEIGHTS
            for dst, src in weights:
                act.dma_start(dst, src).then_inc(weights_loaded, 16)

            def C_n2T(i):
                act.wait_ge(c_n2T_ps, i + 1)
                cp(n2T[0], psum[:, NTB, 0:NT])
                cp(n2T[1], psum[0:HI, NTB, NT:2 * NT]).then_inc(c_n2T, 1)

            def C_gelu(i, n):
                act.wait_ge(c_up[n], i + 1)
                if counts(i):
                    act.wait_ge(c_down, i)
                for e in range(2):
                    t = 2 * n + e
                    g = sa(gT[:, t, :], psum[:, (UB, KB, UB)[n], e * NT:(e + 1) * NT], ACT.Gelu, bias=bf1[:, t:t + 1])
                g.then_inc(c_g[n], 1)

            def A_nT(i, r):
                act.wait_ge(a_nT_ps, i + 1)
                if counts(i - 1):
                    act.wait_ge(b_mixT, i - 1)
                cp(nT[r][0], psum[:, NTB, 0:NT])
                cp(nT[r][1], psum[0:HI, NTB, NT:2 * NT]).then_inc(a_nT, 1)

            def A_k(i, r):
                act.wait_ge(a_k_ps, i + 1)
                for f, a, m in feats:
                    t = sa(kT[r][f], psum[0:m, KB, f * NT:(f + 1) * NT], ACT.Identity, bias=col["bk"][f])
                t.then_inc(a_k, 1)

            def A_ez(i, r):
                act.wait_ge(a_z, i + 1)
                if counts(i):
                    act.wait_ge(a_ez1, i)
                sa(ez, z[r], ACT.Exp, bias=nbr[0:TC], scale=-1.0).then_inc(a_ez, 1)

            def B_exp(i):
                act.wait_ge(b_max, 2 * i + 2)
                if counts(i):
                    act.wait_ge(b_pT_ps, i)
                for t in range(3):
                    o = psum[0:QT, L0 if t < 2 else L1, (t % 2) * NT:(t % 2 + 1) * NT]
                    e = sa(pr[:, t, :], o, ACT.Exp, bias=nmax[:, t:t + 1], accum_out=esum[:, t:t + 1])
                e.then_inc(b_exp, 1)

            def B_pT(i):
                act.wait_ge(b_pT_ps, i + 1)
                cp(pT[:, 0, :], psum[0:TC, L0, 0:3 * QT])
                cp(pT[:, 1, :], psum[0:TC, L1, 0:3 * QT]).then_inc(b_pT, 1)

            def step(i, r, on):
                nxt, a, b, b2, c = on
                if c: C_n2T(i - 3)
                for n in range(3):
                    if c: C_gelu(i - 3, n)
                if a: A_nT(i, r)
                if b: B_exp(i - 1)
                if a: A_k(i, r)
                if a: A_ez(i, r)
                if b: B_pT(i - 1)
            act.wait_ge(vectors_loaded, 16 * VECTORS)
            act.wait_ge(f_const, 2)
            pipeline(act, step)

        def rowc(name):
            return row[name][0:TC].rearrange("p (o n) -> p o n", o=1).broadcast_to([TC, 2, D])

        @block.gpsimd
        def _(pool):
            g = nc.gpsimd

            def A_rstd(i):
                pool.wait_ge(a_var, i + 1)
                g.tensor_tensor(rs[0], ve[0], mhalf, ALU.pow).then_inc(a_rstd, 1)

            def A_res(i, r):
                pool.wait_ge(f_in[r], (i * 8 + (16 - 8 * r)))
                if counts(i - 1):
                    pool.wait_ge(b_res, i - 1)
                g.tensor_tensor(res[r], hc[r], rowc("bf2"), ALU.add).then_inc(a_res, 1)

            def A_rstd2(i):
                pool.wait_ge(a_var2, i + 1)
                g.tensor_tensor(rs[1], ve[1], mhalf, ALU.pow).then_inc(a_rstd2, 1)

            def A_zb(i, r):
                pool.wait_ge(f_const, 2)
                pool.wait_ge(a_z, i + 1)
                if counts(i):
                    pool.wait_ge(a_zrow, i)
                g.tensor_copy(zb, z[r].rearrange("p (c o) -> p c o", o=1).broadcast_to([TC, 2, TC])).then_inc(a_zb, 1)

            def A_sb(i, r):
                pool.wait_ge(f_const, 2)
                pool.wait_ge(a_score, i + 1)
                if counts(i):
                    pool.wait_ge(a_srow, i)
                g.tensor_copy(sb, sel[r][:, :, TOPK:TOPK + 1].broadcast_to([TC, 2, 128])).then_inc(a_sb, 1)

            def B_prob(i):
                pool.wait_ge(b_inv, i + 1)
                g.tensor_tensor(pr, pr, einv.rearrange("p (t o) -> p t o", o=1).broadcast_to([QT, 3, NT]),
                                ALU.mult).then_inc(b_prob, 1)

            def B_res(i, r):
                pool.wait_ge(b_h, i + 1)
                pool.wait_ge(a_res, i + 1)
                if counts(i - 1):
                    pool.wait_ge(c_out, i - 1)
                g.tensor_tensor(rb[r], res[r], hh[r], ALU.add).then_inc(b_res, 1)

            def B_rstd(i):
                pool.wait_ge(b_var, i + 1)
                g.tensor_tensor(rs2, ve2, mhalf, ALU.pow).then_inc(b_rstd, 1)

            def step(i, r, on):
                nxt, a, b, b2, c = on
                q = 1 - r
                if a: A_rstd2(i)
                if a: A_zb(i, r)
                if b2: B_rstd(i - 2)
                if b: B_prob(i - 1)
                if b2: B_res(i - 2, r)
                if a: A_res(i, r)
                if nxt: A_rstd(i + 1)
                if a: A_sb(i, r)
            pool.wait_ge(vectors_loaded, 16 * VECTORS)
            pipeline(pool, step)

        @block.vector
        def _(dve):
            v = nc.vector

            def statistics(src, st, mv, ve, stats, mom, var, i):
                for c in range(2):
                    v.bn_stats(st[:, c], src[:, c]).then_inc(stats, 1)
                dve.wait_ge(stats, 2 * i + 2)
                dve.sem_inc(stats3_seen, 1)
                for c in range(2):
                    v.bn_aggr(mv[:, c], st[:, c]).then_inc(mom, 1)
                dve.wait_ge(mom, 2 * i + 2)
                v.tensor_scalar(ve, mv[:, :, 1], EPS, None, ALU.add).then_inc(var, 1)

            def less_mean(src, to, mv, gain, done):
                for c in range(2):
                    v.scalar_tensor_tensor(out=to[:, c], in0=src[:, c], scalar=mv[:, c, 0:1], in1=row[gain][0:TC],
                                           op0=ALU.subtract, op1=ALU.mult).then_inc(done, 1)

            def scaled(src, to, rs, shift, done):
                for c in range(2):
                    t = v.scalar_tensor_tensor(out=to[:, c], in0=src[:, c], scalar=rs[:, c:c + 1], in1=row[shift][0:TC],
                                               op0=ALU.mult, op1=ALU.add)
                t.then_inc(done, 1)

            def A_stats(i, r):
                dve.wait_ge(f_in[r], i * 8 + (16 - 8 * r))
                statistics(hc[r], st[0], mv[0], ve[0], a_stats, a_mom, a_var, i)

            def A_n0(i, r):
                if counts(i - 1):
                    dve.wait_ge(b_kept, i - 1)
                dve.wait_ge(a_rstd, i + 1)
                for c in range(2):
                    t = v.tensor_scalar(n0[r][:, c], hc[r][:, c], mv[0][:, c, 0:1], rs[0][:, c:c + 1],
                                        ALU.subtract, ALU.mult)
                t.then_inc(a_n0, 1)

            def A_stats2(i, r):
                dve.wait_ge(a_n0, i + 1)
                statistics(n0[r], st[1], mv[1], ve[1], a_stats2, a_mom2, a_var2, i)
                less_mean(n0[r], na, mv[1], "g1", a_ng)

            def A_n(i, r):
                dve.wait_ge(a_ng, 2 * i + 2)
                dve.wait_ge(a_rstd2, i + 1)
                if counts(i - 1):
                    dve.wait_ge(b_gat_ps, i - 1)
                scaled(na, nn[r], rs[1], "b1", a_n)

            def B_stats(i, r):
                dve.wait_ge(b_h, i + 1)
                statistics(hh[r], st3, mv3, ve2, b_stats, b_mom, b_var, i)
                less_mean(hh[r], hg, mv3, "g2", b_hg)

            def B_n2(i, r):
                dve.wait_ge(b_hg, 2 * i + 2)
                dve.wait_ge(b_rstd, i + 1)
                if counts(i - 1):
                    dve.wait_ge(c_n2T_ps, i - 1)
                scaled(hg, n2[r], rs2, "b2", b_n2)

            def A_z(i, r):
                dve.wait_ge(a_n, i + 1)
                if counts(i - 1):
                    dve.wait_ge(a_ez, i - 1)
                if counts(i - 1):
                    dve.wait_ge(a_zb, i - 1)
                if counts(4 * i):
                    dve.wait_ge(a_cnt, 4 * i)
                for c in range(2):
                    t = v.tensor_tensor_reduce(out=junk[:, c * D:(c + 1) * D], in0=nn[r][:, c], in1=row["Wr"][0:TC], scale=1.0,
                                               scalar=0.0, op0=ALU.mult, op1=ALU.add, accum_out=z[r][:, c:c + 1])
                t.then_inc(a_z, 1)

            def A_rank(i, r):
                dve.wait_ge(a_zrow, i + 1)
                zr = psum[0:TC, RB, 0:NT]
                for c in range(2):
                    v.tensor_scalar(cmp[c], zr, z[r][:, c:c + 1], None, ALU.is_lt, ALU.add,
                                    accum_out=lt[:, c:c + 1]).then_inc(a_cnt, 1)
                    v.scalar_tensor_tensor(out=cmp[2 + c], in0=zr, scalar=z[r][:, c:c + 1], in1=before[:, c], op0=ALU.is_equal,
                                           op1=ALU.mult, accum_out=eq[:, c:c + 1]).then_inc(a_cnt, 1)
                dve.wait_ge(a_cnt, 4 * i + 4)
                v.tensor_tensor(rank, lt, eq, ALU.add).then_inc(a_rank, 1)
                dve.wait_ge(a_rank, i + 1)
                for c in range(2):
                    v.tensor_scalar(sel[r][:, c, 0:TOPK], slots, rank[:, c:c + 1], None, ALU.is_equal).then_inc(a_sel, 1)
                    v.tensor_scalar(keep[r][:, c:c + 1], rank[:, c:c + 1], float(TOPK), None, ALU.is_ge).then_inc(a_sel, 1)

            def A_score(i, r):
                dve.wait_ge(a_ez, i + 1)
                v.tensor_scalar(ez1, ez, 1.0, None, ALU.add).then_inc(a_ez1, 1)
                dve.wait_ge(a_ez1, i + 1)
                v.reciprocal(sel[r][:, :, TOPK], ez1).then_inc(a_score, 1)

            def A_v(i, r):
                dve.wait_ge(a_v_ps, i + 1)
                v.tensor_tensor(vv[r], psum[0:TC, VB, 0:2 * D].rearrange("p (c n) -> p c n", c=2), rowc("bv"),
                                ALU.add).then_inc(a_v, 1)

            def B_gat(i, r):
                dve.wait_ge(b_gat_ps, i + 1)
                v.tensor_scalar(ssum, psum[:, SB, SS:SS + 1], 1e-6, None, ALU.add).then_inc(b_gat, 1)
                v.tensor_copy(nsel[0], psum[:, SB, GA:GA + TOPK]).then_inc(b_gat, 1)
                v.tensor_copy(nsel[1], psum[0:HI, SB, GB:GB + TOPK]).then_inc(b_gat, 1)
                v.tensor_copy(selT, psum[0:TOPK, SB, ST:ST + NT]).then_inc(b_gat, 1)
                dve.wait_ge(b_gat, 4 * i + 4)
                v.reciprocal(sinv, ssum).then_inc(b_sinv, 1)
                dve.wait_ge(b_sinv, i + 1)
                for (f, a, m), o in zip(feats, (GA, GB)):
                    v.tensor_tensor(pooled[f], psum[0:m, SB, o + TOPK:o + TOPK + 1], sinv[0:m], ALU.mult).then_inc(b_pool, 1)

            def B_q(i):
                dve.wait_ge(b_q_ps, i + 1)
                for (f, a, m), o in zip(feats, (QA, QB)):
                    v.tensor_scalar(qs[f], psum[0:m, SB, o:o + TOPK], col["bq"][f], DH3 ** -0.5, ALU.add,
                                    ALU.mult).then_inc(b_q, 1)
                dve.wait_ge(b_q, 2 * i + 2)
                for k, nh in ((0, 8), (1, 4)):
                    m = qs[k].shape[0]
                    v.tensor_tensor(qblk[k], qs[k].rearrange("p (o j) -> p o j", o=1).broadcast_to([m, nh, TOPK]),
                                    own[0:m, 0:nh].rearrange("p (h o) -> p h o", o=1).broadcast_to([m, nh, TOPK]),
                                    ALU.mult).then_inc(b_qblk, 1)

            def B_max(i):
                dve.wait_ge(b_log, i + 1)
                v.tensor_reduce(nmax[:, 0:2], psum[0:QT, L0, 0:2 * NT].rearrange("p (t n) -> p t n", t=2), AX.X, ALU.max,
                                negate=True).then_inc(b_max, 1)
                v.tensor_reduce(nmax[:, 2:3], psum[0:QT, L1, 0:NT], AX.X, ALU.max, negate=True).then_inc(b_max, 1)

            def B_inv(i):
                dve.wait_ge(b_exp, i + 1)
                v.reciprocal(einv, esum).then_inc(b_inv, 1)

            def B_mixT(i, r):
                dve.wait_ge(a_srow, i + 1)
                dve.wait_ge(a_nT, i + 1)
                dve.wait_ge(b_pool, 2 * i + 2)
                if counts(i):
                    dve.wait_ge(b_mix_ps, i)
                for f, a, m in feats:
                    t = v.scalar_tensor_tensor(out=mixT[f], in0=psum[0:m, RB, NT:2 * NT], scalar=pooled[f], in1=nT[r][f],
                                               op0=ALU.mult, op1=ALU.add)
                t.then_inc(b_mixT, 1)

            def B_mixb(i):
                dve.wait_ge(b_mix_ps, i + 1)
                v.tensor_tensor(mixb, psum[0:TC, UB, 0:2 * D].rearrange("p (c n) -> p c n", c=2), rowc("bm"),
                                ALU.add).then_inc(b_mixb, 1)

            def B_kept(i, r):
                dve.wait_ge(b_mixb, i + 1)
                for c in range(2):
                    t = v.scalar_tensor_tensor(out=kept_mix[:, c], in0=mixb[:, c], scalar=keep[r][:, c:c + 1], in1=n0[r][:, c],
                                               op0=ALU.mult, op1=ALU.add)
                t.then_inc(b_kept, 1)

            def B_av(i):
                dve.wait_ge(b_av_ps, i + 1)
                for k, nh in ((0, 8), (1, 4)):
                    m = qs[k].shape[0]
                    o = psum[0:m, KB, k * 8 * TOPK:k * 8 * TOPK + nh * TOPK].rearrange("p (h j) -> p h j", h=nh)
                    v.tensor_tensor(cm[k], o, own[0:m, 0:nh].rearrange("p (h o) -> p h o", o=1).broadcast_to([m, nh, TOPK]),
                                    ALU.mult).then_inc(b_av, 1)
                dve.wait_ge(b_av, 2 * i + 2)
                for k in range(2):
                    v.tensor_reduce(ctxT[k], cm[k].rearrange("p h j -> p j h"), AX.X, ALU.add).then_inc(b_ctx, 1)

            def B_asel(i):
                dve.wait_ge(b_wo_ps, i + 1)
                v.tensor_tensor(asel, psum[0:TOPK, SB, 0:D], row["bo"][0:TOPK], ALU.add).then_inc(b_asel, 1)

            def B_h(i, r):
                dve.wait_ge(b_sca_ps, i + 1)
                dve.wait_ge(b_kept, i + 1)
                if counts(i - 1):
                    dve.wait_ge(b_res, i - 1)
                v.tensor_tensor(hh[r], psum[0:TC, VB, 0:2 * D].rearrange("p (c n) -> p c n", c=2), kept_mix,
                                ALU.add).then_inc(b_h, 1)

            def C_out(i, r):
                dve.wait_ge(c_down, i + 1)
                dve.wait_ge(b_res, i + 1)
                if counts(i * 8 - 8 * r):
                    dve.wait_ge(f_out[r], i * 8 - 8 * r)
                v.tensor_tensor(oo[r], psum[0:TC, NTB, 0:2 * D].rearrange("p (c n) -> p c n", c=2), rb[r],
                                ALU.add).then_inc(c_out, 1)

            def step(i, r, on):
                nxt, a, b, b2, c = on
                q = 1 - r
                if b2: B_h(i - 2, r)
                if b: B_gat(i - 1, q)
                if a: A_stats2(i, r)
                if b: B_q(i - 1)
                if a: A_n(i, r)
                if b: B_mixT(i - 1, q)
                if a: A_z(i, r)
                if b: B_max(i - 1)
                if b2: B_stats(i - 2, r)
                if b: B_mixb(i - 1)
                if b: B_inv(i - 1)
                if b: B_kept(i - 1, q)
                if b2: B_n2(i - 2, r)
                if nxt: A_stats(i + 1, q)
                if a: A_rank(i, r)
                if nxt: A_n0(i + 1, q)
                if a: A_v(i, r)
                if a: A_score(i, r)
                if b: B_av(i - 1)
                if b: B_asel(i - 1)
                if c: C_out(i - 3, q)
            dve.wait_ge(vectors_loaded, 16 * VECTORS)
            v.memset(ones, 1.0).then_inc(f_const, 1)
            v.tensor_scalar(nbr, br, -1.0, None, ALU.mult).then_inc(f_const, 1)
            pipeline(dve, step)


def kept(nc, ctx):
    sb = lambda n, cols: ctx.enter_context(nc.sbuf_tensor("sb_" + n, [128, cols], F32))
    w = {}
    w["qkv_lo"], w["qkv_hi"] = sb("qkv_lo", 3 * H1 * DH1)[:], sb("qkv_hi", 3 * H1 * DH1)[0:HI + 1]
    w["proj"] = sb("proj", 6 * D)[:].rearrange("p (h n) -> p h n", h=6)
    w["projb_lo"], w["projb_hi"] = sb("projb_lo", 1)[:], sb("projb_hi", 1)[0:HI]
    w["ident"] = sb("ident", 128)[:]
    w["mhalf"] = sb("mhalf", CHUNKS)[:]
    w["kx"] = sb("kx", H1 * NT)[:].rearrange("p (h n) -> p h n", h=H1)
    w["vx"] = sb("vx", 2 * H1 * KQ)[0:TC].rearrange("p (c h d) -> p c h d", c=2, h=H1)
    for hs, nh in (("a", 8), ("b", 4)):
        for f, m in enumerate((LO, HI)):
            n = f"tw_{hs}{f}"
            w[n] = sb(n, 2 * nh * TAB)[0:m].rearrange("p (s i h) -> p s i h", s=2, h=nh)
            n = f"tz_{hs}{f}"
            w[n] = sb(n, 2 * nh * SLOT)[0:m].rearrange("p (s i h) -> p s i h", s=2, h=nh)
    w["pv_a"] = sb("pv_a", (ROWS + SIDE + 2) * D)[:].rearrange("p (g n) -> p g n", n=D)
    w["pv_b"] = sb("pv_b", (ROWS + 1) * D)[:].rearrange("p (g n) -> p g n", n=D)
    return w


def vit_block(nc, io, out, nimg):
    hA = nc.dram_tensor("h_by_class", [nimg * NT, D], F32).ap()
    h2 = nc.dram_tensor("h_attended", [nimg * NT, D], F32).ap()
    pv_rows = nc.dram_tensor("table_rows", [2, TAB, H1 * D], F32).ap()
    with ExitStack() as ctx:
        w = kept(nc, ctx)
        arena = ctx.enter_context(nc.sbuf_tensor("arena", [128, 31040], F32))[:]
        psum = ctx.enter_context(nc.psum_tensor("banks", [128, 8, 512], F32))
        aw_loaded, h_in = ctx.enter_context(nc.semaphore("aw_loaded")), ctx.enter_context(nc.semaphore("h_in"))
        tokenizer(nc, ctx, io, w, arena, psum, hA, nimg, aw_loaded)
        attention_weights(nc, ctx, io, w, arena, psum, pv_rows, aw_loaded, hA, h_in, nimg)
        attention(nc, ctx, io, w, arena, psum, pv_rows, hA, h_in, h2, nimg)
        feed_forward(nc, ctx, io, arena, psum, h2, out, nimg)


def lay_out(x, tok_W, tok_b, qkv_w, proj_w, proj_b, tabs, ffn):
    import numpy as np
    n = x.shape[0]
    p = x.reshape(n, GP, P, GP, 2, P // 2, 3).transpose(0, 1, 3, 4, 2, 5, 6).reshape(n, GP, GP, PIX)

    def chunks(a, m):
        return a.reshape(-1, m, KT, 128).transpose(0, 3, 2, 1)
    e = GP - 1
    io = dict(
        xI=chunks(p[:, 1:e, 1:e].reshape(-1, PIX), 128).reshape(n // 8, 9, 128, KT, 128),
        xE=np.stack([chunks(a.reshape(-1, PIX), 96) for a in (p[:, 0, 1:e], p[:, e, 1:e], p[:, 1:e, 0], p[:, 1:e, e])]),
        xC=np.stack([chunks(a, n)[0] for a in (p[:, 0, 0], p[:, 0, e], p[:, e, 0], p[:, e, e])]),
        tokW=tok_W.reshape(P, 2, P // 2, 5, 3, D).transpose(3, 1, 0, 2, 4, 5).reshape(5, KT, 128, D).transpose(2, 0, 1, 3),
        tokb=tok_b)
    Q = H1 * DH1
    t = np.arange(NT)
    onehot = np.zeros((2 * SLOT, NT), np.float32)
    onehot[(t[1:] - 1) // SIDE, t[1:]] = 1
    onehot[SLOT + (t[1:] - 1) % SIDE, t[1:]] = 1
    first = np.zeros((1, GT), np.float32)
    first[0, ::NT] = 1
    side_by_side = lambda a, b: np.concatenate([np.pad(u.T, ((0, 0), (0, 1))) for u in (a, b)], 1)
    io.update(
        wq_d=qkv_w[:Q].reshape(H1, DH1, D).transpose(1, 0, 2).reshape(DH1, H1 * D),
        proj_d=proj_w.reshape(D, H1, DH1).transpose(2, 1, 0).reshape(DH1, H1 * D),
        tabk=side_by_side(*tabs[:2]), tabv=side_by_side(*tabs[2:]),
        t0=np.concatenate([u[0] for u in tabs]).reshape(1, 4 * DH1),
        qkvT=qkv_w.T, proj_p=proj_w.T.reshape(6, 128, D).transpose(1, 0, 2), projb=proj_b.reshape(D, 1),
        onehot=onehot, onehotT=onehot.T.reshape(2, TC, 2 * SLOT), first=first,
        ident=np.eye(128, dtype=np.float32), mhalf=np.full((128, CHUNKS), -0.5, np.float32),
        slots=np.tile(np.arange(TOPK, dtype=np.float32), (TC, 1)),
        before=(t[None] < t[:, None]).astype(np.float32).reshape(2, TC, NT).transpose(1, 0, 2),
        own=(np.arange(128)[:, None] // DH3 == np.arange(8)[None]).astype(np.float32))
    io.update(ffn)
    io["bf1"] = ffn["bf1"].reshape(FT, 128).T
    io["br"] = ffn["br"].reshape(1)
    return {k: np.ascontiguousarray(a) for k, a in io.items()}


def kernel(x, L0_tok_W, L0_tok_b, L0_attn_qkv_w, L0_attn_proj_w, L0_attn_proj_b, L0_attn_tab_kv, L0_attn_tab_kh,
           L0_attn_tab_vv, L0_attn_tab_vh, **ffn):
    import numpy as np
    import concourse.bacc as bacc
    from concourse.bass_utils import run_bass_kernel_spmd

    nimg = x.shape[0]
    ffn = {k.removeprefix("L0_ffn_"): np.asarray(a) for k, a in ffn.items()}
    arrays = lay_out(*(np.asarray(a) for a in (x, L0_tok_W, L0_tok_b, L0_attn_qkv_w, L0_attn_proj_w, L0_attn_proj_b)),
                     [np.asarray(a) for a in (L0_attn_tab_kv, L0_attn_tab_kh, L0_attn_tab_vv, L0_attn_tab_vh)], ffn)
    nc = bacc.Bacc("TRN2", target_bir_lowering=False, num_devices=1)
    io = {k: nc.dram_tensor("in_" + k, a.shape, F32, kind="ExternalInput").ap() for k, a in arrays.items()}
    out = nc.dram_tensor("out", [nimg * NT, D], F32, kind="ExternalOutput").ap()
    vit_block(nc, io, out, nimg)
    r = run_bass_kernel_spmd(nc, [{"in_" + k: a for k, a in arrays.items()}], core_ids=[0])
    return r.results[0]["out"].reshape(nimg, NT, D)
```
